# Optimizing a Trainium2 kernel written in Bass

```python
import numpy as np
import jax
import jax.numpy as jnp

def _softmax(x, axis=-1):
    return jax.nn.softmax(x, axis=axis)

def _gelu(x):
    return jax.nn.gelu(x, approximate=True)

def _silu(x):
    return jax.nn.silu(x)

def _sigmoid(x):
    return jax.nn.sigmoid(x)

def _layernorm(x, axis=-1, eps=1e-05):
    m = jnp.mean(x, axis=axis, keepdims=True)
    v = jnp.var(x, axis=axis, keepdims=True)
    return (x - m) / jnp.sqrt(v + eps)

def _scatter_add(tgt, idx, src, axis=0):
    return tgt.at[idx].add(src)

def _segment_sum(src, seg, n):
    return jax.ops.segment_sum(src, seg, n)
kernel_name = 'mk_xattn_seq_d2_seqx_r8_a320f0'

def setup_inputs(seed: int=0):
    np.random.seed(seed)
    _w = jnp.asarray

    def _rec_inputs():
        import jax
        import jax.numpy as jnp
        _rk = jax.random.key(seed)
        x = 7.22e-05 + 1 * jax.random.normal(jax.random.fold_in(_rk, 1), (4, 256, 256), jnp.float32)
        _lenS = 256 - jax.random.randint(jax.random.fold_in(_rk, 7), (4,), 0, max(1, 256 // 4) + 1, jnp.int32)
        _lenS2 = 256 - jax.random.randint(jax.random.fold_in(_rk, 8), (4,), 0, max(1, 256 // 4) + 1, jnp.int32)
        _ctx_2048P = jax.random.normal(jax.random.fold_in(_rk, 11), (4, 16, 256), jnp.float32)
        _ctx_2048c = jax.random.dirichlet(jax.random.fold_in(_rk, 511), 0.3 * jnp.ones((16,), jnp.float32), (4, 256))
        _ctx_2048t = jnp.einsum('bsk,bkd->bsd', _ctx_2048c, _ctx_2048P)
        _ctx_2048t = _ctx_2048t * jax.lax.rsqrt(jnp.mean(jnp.square(_ctx_2048t)) + 1e-12) * 0.953939
        ctx_2048 = 2.81802e-05 + 1.00001 * (_ctx_2048t + 0.3 * jax.random.normal(jax.random.fold_in(_rk, 611), (4, 256, 256), jnp.float32))
        _validS = jnp.arange(256)[None, :] < _lenS[:, None]
        _validS2 = jnp.arange(256)[None, :] < _lenS2[:, None]
        _causal = jnp.tril(jnp.ones((256, 256), dtype=bool))
        mask_BxS2_bf1 = jnp.ones((4, 256), dtype=bool)
        return (x, ctx_2048, mask_BxS2_bf1)
    x, ctx_2048, mask_BxS2_bf1 = _rec_inputs()

    def _L0_xattn_setup():
        import jax, jax.numpy as jnp
        import numpy as np
        D = 256
        H = 16
        HD = D // H
        INNER = 4 * D
        EPS = 1e-05

        def layer_norm(x, w, b):
            mu = jnp.mean(x, axis=-1, keepdims=True)
            var = jnp.mean(jnp.square(x - mu), axis=-1, keepdims=True)
            return (x - mu) * jax.lax.rsqrt(var + EPS) * w + b
        key = jax.random.key(seed)
        ks = jax.random.split(key, 12)
        B, LQ, LK = (4, 128, 256)
        std = 0.02
        inp = {'hidden_states': jax.random.normal(ks[0], (B, LQ, D), jnp.float32), 'encoder_hidden_states': jax.random.normal(ks[1], (B, LK, D), jnp.float32), 'encoder_attention_mask': jnp.ones((B, LK), dtype=bool), 'ln1_w': jnp.ones((D,), jnp.float32), 'ln1_b': jnp.zeros((D,), jnp.float32), 'q_w': jax.random.normal(ks[2], (D, D), jnp.float32) * std, 'q_b': jnp.zeros((D,), jnp.float32), 'k_w': jax.random.normal(ks[3], (D, D), jnp.float32) * std, 'k_b': jnp.zeros((D,), jnp.float32), 'v_w': jax.random.normal(ks[4], (D, D), jnp.float32) * std, 'v_b': jnp.zeros((D,), jnp.float32), 'cproj_w': jax.random.normal(ks[5], (D, D), jnp.float32) * std, 'cproj_b': jnp.zeros((D,), jnp.float32), 'ln2_w': jnp.ones((D,), jnp.float32), 'ln2_b': jnp.zeros((D,), jnp.float32), 'fc_w': jax.random.normal(ks[6], (D, INNER), jnp.float32) * std, 'fc_b': jnp.zeros((INNER,), jnp.float32), 'proj_w': jax.random.normal(ks[7], (INNER, D), jnp.float32) * std, 'proj_b': jnp.zeros((D,), jnp.float32)}
        return inp
    _L0_xattn_all = _L0_xattn_setup()
    _L0_xattn_in = {k: v for k, v in _L0_xattn_all.items() if k in ('ln1_w', 'ln1_b', 'q_w', 'q_b', 'k_w', 'k_b', 'v_w', 'v_b', 'cproj_w', 'cproj_b', 'ln2_w', 'ln2_b', 'fc_w', 'fc_b', 'proj_w', 'proj_b')}
    del _L0_xattn_all

    def _L1_xattn_setup():
        import jax, jax.numpy as jnp
        import numpy as np
        B, Q, S1, S2 = (4, 32, 256, 256)
        D, H, K, F = (256, 16, 128, 1024)
        LN_EPS = 1e-05

        def _layer_norm(x, scale, offset):
            mu = jnp.mean(x, axis=-1, keepdims=True)
            var = jnp.var(x, axis=-1, keepdims=True)
            return (x - mu) * jax.lax.rsqrt(var + LN_EPS) * scale + offset

        def _cross_attention(q_in, kv_in, wq, bq, wk, bk, wv, bv, wo, bo, bias_k, bias_v):
            b, q_len, _ = q_in.shape
            t = kv_in.shape[1]
            qh = (q_in @ wq + bq).reshape(b, q_len, H, K)
            kh = (kv_in @ wk + bk).reshape(b, t, H, K)
            vh = (kv_in @ wv + bv).reshape(b, t, H, K)
            kh = jnp.concatenate([kh, jnp.broadcast_to(bias_k, (b, 1, H, K))], axis=1)
            vh = jnp.concatenate([vh, jnp.broadcast_to(bias_v, (b, 1, H, K))], axis=1)
            scale = jnp.sqrt(jnp.asarray(K, q_in.dtype))
            logits = jnp.einsum('bqhk,bthk->bhqt', qh, kh) / scale
            weights = jax.nn.softmax(logits, axis=-1)
            ctx = jnp.einsum('bhqt,bthk->bqhk', weights, vh).reshape(b, q_len, H * K)
            return ctx @ wo + bo

        def _forward(x, xf_1, xf_2, ln1_scale, ln1_offset, wq1, bq1, wk1, bk1, wv1, bv1, wo1, bo1, bias_k1, bias_v1, ln2_scale, ln2_offset, wq2, bq2, wk2, bk2, wv2, bv2, wo2, bo2, bias_k2, bias_v2, ln_mlp_scale, ln_mlp_offset, w_fc1, b_fc1, w_fc2, b_fc2):
            res = x
            h = _layer_norm(x, ln1_scale, ln1_offset)
            x = res + _cross_attention(h, xf_1, wq1, bq1, wk1, bk1, wv1, bv1, wo1, bo1, bias_k1, bias_v1)
            res = x
            h = _layer_norm(x, ln2_scale, ln2_offset)
            x = res + _cross_attention(h, xf_2, wq2, bq2, wk2, bk2, wv2, bv2, wo2, bo2, bias_k2, bias_v2)
            h = _layer_norm(x, ln_mlp_scale, ln_mlp_offset)
            h = jax.nn.gelu(h @ w_fc1 + b_fc1, approximate=False) @ w_fc2 + b_fc2
            return x + h
        key = jax.random.key(seed)
        ks = iter(jax.random.split(key, 64))

        def rn(shape, s=0.02):
            return jax.random.normal(next(ks), shape, jnp.float32) * s
        inp = {'x': rn((B, Q, D), 1.0), 'xf_1': rn((B, S1, D), 1.0), 'xf_2': rn((B, S2, D), 1.0)}
        for i in (1, 2):
            inp[f'ln{i}_scale'] = jnp.ones((D,), jnp.float32)
            inp[f'ln{i}_offset'] = jnp.zeros((D,), jnp.float32)
            inp[f'wq{i}'] = rn((D, H * K))
            inp[f'bq{i}'] = jnp.zeros((H * K,), jnp.float32)
            inp[f'wk{i}'] = rn((D, H * K))
            inp[f'bk{i}'] = jnp.zeros((H * K,), jnp.float32)
            inp[f'wv{i}'] = rn((D, H * K))
            inp[f'bv{i}'] = jnp.zeros((H * K,), jnp.float32)
            inp[f'wo{i}'] = rn((H * K, D))
            inp[f'bo{i}'] = jnp.zeros((D,), jnp.float32)
            inp[f'bias_k{i}'] = rn((1, 1, H, K))
            inp[f'bias_v{i}'] = rn((1, 1, H, K))
        inp['ln_mlp_scale'] = jnp.ones((D,), jnp.float32)
        inp['ln_mlp_offset'] = jnp.zeros((D,), jnp.float32)
        inp['w_fc1'] = rn((D, F))
        inp['b_fc1'] = jnp.zeros((F,), jnp.float32)
        inp['w_fc2'] = rn((F, D))
        inp['b_fc2'] = jnp.zeros((D,), jnp.float32)
        return inp
    _L1_xattn_all = _L1_xattn_setup()
    _L1_xattn_in = {k: v for k, v in _L1_xattn_all.items() if k in ('ln1_scale', 'ln1_offset', 'wq1', 'bq1', 'wk1', 'bk1', 'wv1', 'bv1', 'wo1', 'bo1', 'bias_k1', 'bias_v1', 'ln2_scale', 'ln2_offset', 'wq2', 'bq2', 'wk2', 'bk2', 'wv2', 'bv2', 'wo2', 'bo2', 'bias_k2', 'bias_v2', 'ln_mlp_scale', 'ln_mlp_offset', 'w_fc1', 'b_fc1', 'w_fc2', 'b_fc2')}
    del _L1_xattn_all
    return {'x': x, 'ctx_2048': ctx_2048, 'mask_BxS2_bf1': mask_BxS2_bf1, 'L0_xattn_ln1_w': _L0_xattn_in['ln1_w'], 'L0_xattn_ln1_b': _L0_xattn_in['ln1_b'], 'L0_xattn_q_w': _L0_xattn_in['q_w'], 'L0_xattn_q_b': _L0_xattn_in['q_b'], 'L0_xattn_k_w': _L0_xattn_in['k_w'], 'L0_xattn_k_b': _L0_xattn_in['k_b'], 'L0_xattn_v_w': _L0_xattn_in['v_w'], 'L0_xattn_v_b': _L0_xattn_in['v_b'], 'L0_xattn_cproj_w': _L0_xattn_in['cproj_w'], 'L0_xattn_cproj_b': _L0_xattn_in['cproj_b'], 'L0_xattn_ln2_w': _L0_xattn_in['ln2_w'], 'L0_xattn_ln2_b': _L0_xattn_in['ln2_b'], 'L0_xattn_fc_w': _L0_xattn_in['fc_w'], 'L0_xattn_fc_b': _L0_xattn_in['fc_b'], 'L0_xattn_proj_w': _L0_xattn_in['proj_w'], 'L0_xattn_proj_b': _L0_xattn_in['proj_b'], 'L1_xattn_ln1_scale': _L1_xattn_in['ln1_scale'], 'L1_xattn_ln1_offset': _L1_xattn_in['ln1_offset'], 'L1_xattn_wq1': _L1_xattn_in['wq1'], 'L1_xattn_bq1': _L1_xattn_in['bq1'], 'L1_xattn_wk1': _L1_xattn_in['wk1'], 'L1_xattn_bk1': _L1_xattn_in['bk1'], 'L1_xattn_wv1': _L1_xattn_in['wv1'], 'L1_xattn_bv1': _L1_xattn_in['bv1'], 'L1_xattn_wo1': _L1_xattn_in['wo1'], 'L1_xattn_bo1': _L1_xattn_in['bo1'], 'L1_xattn_bias_k1': _L1_xattn_in['bias_k1'], 'L1_xattn_bias_v1': _L1_xattn_in['bias_v1'], 'L1_xattn_ln2_scale': _L1_xattn_in['ln2_scale'], 'L1_xattn_ln2_offset': _L1_xattn_in['ln2_offset'], 'L1_xattn_wq2': _L1_xattn_in['wq2'], 'L1_xattn_bq2': _L1_xattn_in['bq2'], 'L1_xattn_wk2': _L1_xattn_in['wk2'], 'L1_xattn_bk2': _L1_xattn_in['bk2'], 'L1_xattn_wv2': _L1_xattn_in['wv2'], 'L1_xattn_bv2': _L1_xattn_in['bv2'], 'L1_xattn_wo2': _L1_xattn_in['wo2'], 'L1_xattn_bo2': _L1_xattn_in['bo2'], 'L1_xattn_bias_k2': _L1_xattn_in['bias_k2'], 'L1_xattn_bias_v2': _L1_xattn_in['bias_v2'], 'L1_xattn_ln_mlp_scale': _L1_xattn_in['ln_mlp_scale'], 'L1_xattn_ln_mlp_offset': _L1_xattn_in['ln_mlp_offset'], 'L1_xattn_w_fc1': _L1_xattn_in['w_fc1'], 'L1_xattn_b_fc1': _L1_xattn_in['b_fc1'], 'L1_xattn_w_fc2': _L1_xattn_in['w_fc2'], 'L1_xattn_b_fc2': _L1_xattn_in['b_fc2']}

def reference(x, ctx_2048, mask_BxS2_bf1, L0_xattn_ln1_w, L0_xattn_ln1_b, L0_xattn_q_w, L0_xattn_q_b, L0_xattn_k_w, L0_xattn_k_b, L0_xattn_v_w, L0_xattn_v_b, L0_xattn_cproj_w, L0_xattn_cproj_b, L0_xattn_ln2_w, L0_xattn_ln2_b, L0_xattn_fc_w, L0_xattn_fc_b, L0_xattn_proj_w, L0_xattn_proj_b, L1_xattn_ln1_scale, L1_xattn_ln1_offset, L1_xattn_wq1, L1_xattn_bq1, L1_xattn_wk1, L1_xattn_bk1, L1_xattn_wv1, L1_xattn_bv1, L1_xattn_wo1, L1_xattn_bo1, L1_xattn_bias_k1, L1_xattn_bias_v1, L1_xattn_ln2_scale, L1_xattn_ln2_offset, L1_xattn_wq2, L1_xattn_bq2, L1_xattn_wk2, L1_xattn_bk2, L1_xattn_wv2, L1_xattn_bv2, L1_xattn_wo2, L1_xattn_bo2, L1_xattn_bias_k2, L1_xattn_bias_v2, L1_xattn_ln_mlp_scale, L1_xattn_ln_mlp_offset, L1_xattn_w_fc1, L1_xattn_b_fc1, L1_xattn_w_fc2, L1_xattn_b_fc2):
    import jax
    import jax.numpy as jnp

    def _L0_xattn_ref(hidden_states, encoder_hidden_states, encoder_attention_mask, ln1_w, ln1_b, q_w, q_b, k_w, k_b, v_w, v_b, cproj_w, cproj_b, ln2_w, ln2_b, fc_w, fc_b, proj_w, proj_b):
        import jax, jax.numpy as jnp
        import numpy as np
        D = 256
        H = 16
        HD = D // H
        INNER = 4 * D
        EPS = 1e-05

        def layer_norm(x, w, b):
            mu = jnp.mean(x, axis=-1, keepdims=True)
            var = jnp.mean(jnp.square(x - mu), axis=-1, keepdims=True)
            return (x - mu) * jax.lax.rsqrt(var + EPS) * w + b
        B, LQ, _ = hidden_states.shape
        LK = encoder_hidden_states.shape[1]
        residual = hidden_states
        x = layer_norm(hidden_states, ln1_w, ln1_b)
        q = (x @ q_w + q_b).reshape(B, LQ, H, HD).transpose(0, 2, 1, 3)
        k = (encoder_hidden_states @ k_w + k_b).reshape(B, LK, H, HD).transpose(0, 2, 1, 3)
        v = (encoder_hidden_states @ v_w + v_b).reshape(B, LK, H, HD).transpose(0, 2, 1, 3)
        scale = 1.0 / np.sqrt(HD).astype(np.float32)
        scores = jnp.einsum('bhqd,bhkd->bhqk', q, k) * scale
        mask = encoder_attention_mask[:, None, None, :]
        mask_value = jnp.finfo(scores.dtype).min
        scores = jnp.where(mask, scores, mask_value)
        attn = jax.nn.softmax(scores, axis=-1)
        out = jnp.einsum('bhqk,bhkd->bhqd', attn, v)
        out = out.transpose(0, 2, 1, 3).reshape(B, LQ, D)
        out = out @ cproj_w + cproj_b
        hidden = out + residual
        residual = hidden
        y = layer_norm(hidden, ln2_w, ln2_b)
        y = jax.nn.gelu(y @ fc_w + fc_b, approximate=True)
        y = y @ proj_w + proj_b
        return residual + y

    def _L1_xattn_ref(x, xf_1, xf_2, ln1_scale, ln1_offset, wq1, bq1, wk1, bk1, wv1, bv1, wo1, bo1, bias_k1, bias_v1, ln2_scale, ln2_offset, wq2, bq2, wk2, bk2, wv2, bv2, wo2, bo2, bias_k2, bias_v2, ln_mlp_scale, ln_mlp_offset, w_fc1, b_fc1, w_fc2, b_fc2):
        import jax, jax.numpy as jnp
        import numpy as np
        B, Q, S1, S2 = (4, 32, 256, 256)
        D, H, K, F = (256, 16, 128, 1024)
        LN_EPS = 1e-05

        def _layer_norm(x, scale, offset):
            mu = jnp.mean(x, axis=-1, keepdims=True)
            var = jnp.var(x, axis=-1, keepdims=True)
            return (x - mu) * jax.lax.rsqrt(var + LN_EPS) * scale + offset

        def _cross_attention(q_in, kv_in, wq, bq, wk, bk, wv, bv, wo, bo, bias_k, bias_v):
            b, q_len, _ = q_in.shape
            t = kv_in.shape[1]
            qh = (q_in @ wq + bq).reshape(b, q_len, H, K)
            kh = (kv_in @ wk + bk).reshape(b, t, H, K)
            vh = (kv_in @ wv + bv).reshape(b, t, H, K)
            kh = jnp.concatenate([kh, jnp.broadcast_to(bias_k, (b, 1, H, K))], axis=1)
            vh = jnp.concatenate([vh, jnp.broadcast_to(bias_v, (b, 1, H, K))], axis=1)
            scale = jnp.sqrt(jnp.asarray(K, q_in.dtype))
            logits = jnp.einsum('bqhk,bthk->bhqt', qh, kh) / scale
            weights = jax.nn.softmax(logits, axis=-1)
            ctx = jnp.einsum('bhqt,bthk->bqhk', weights, vh).reshape(b, q_len, H * K)
            return ctx @ wo + bo

        def _forward(x, xf_1, xf_2, ln1_scale, ln1_offset, wq1, bq1, wk1, bk1, wv1, bv1, wo1, bo1, bias_k1, bias_v1, ln2_scale, ln2_offset, wq2, bq2, wk2, bk2, wv2, bv2, wo2, bo2, bias_k2, bias_v2, ln_mlp_scale, ln_mlp_offset, w_fc1, b_fc1, w_fc2, b_fc2):
            res = x
            h = _layer_norm(x, ln1_scale, ln1_offset)
            x = res + _cross_attention(h, xf_1, wq1, bq1, wk1, bk1, wv1, bv1, wo1, bo1, bias_k1, bias_v1)
            res = x
            h = _layer_norm(x, ln2_scale, ln2_offset)
            x = res + _cross_attention(h, xf_2, wq2, bq2, wk2, bk2, wv2, bv2, wo2, bo2, bias_k2, bias_v2)
            h = _layer_norm(x, ln_mlp_scale, ln_mlp_offset)
            h = jax.nn.gelu(h @ w_fc1 + b_fc1, approximate=False) @ w_fc2 + b_fc2
            return x + h
        return _forward(x, xf_1, xf_2, ln1_scale, ln1_offset, wq1, bq1, wk1, bk1, wv1, bv1, wo1, bo1, bias_k1, bias_v1, ln2_scale, ln2_offset, wq2, bq2, wk2, bk2, wv2, bv2, wo2, bo2, bias_k2, bias_v2, ln_mlp_scale, ln_mlp_offset, w_fc1, b_fc1, w_fc2, b_fc2)
    x = _L0_xattn_ref(x, ctx_2048, mask_BxS2_bf1, L0_xattn_ln1_w, L0_xattn_ln1_b, L0_xattn_q_w, L0_xattn_q_b, L0_xattn_k_w, L0_xattn_k_b, L0_xattn_v_w, L0_xattn_v_b, L0_xattn_cproj_w, L0_xattn_cproj_b, L0_xattn_ln2_w, L0_xattn_ln2_b, L0_xattn_fc_w, L0_xattn_fc_b, L0_xattn_proj_w, L0_xattn_proj_b)
    x = _L1_xattn_ref(x, ctx_2048, ctx_2048, L1_xattn_ln1_scale, L1_xattn_ln1_offset, L1_xattn_wq1, L1_xattn_bq1, L1_xattn_wk1, L1_xattn_bk1, L1_xattn_wv1, L1_xattn_bv1, L1_xattn_wo1, L1_xattn_bo1, L1_xattn_bias_k1, L1_xattn_bias_v1, L1_xattn_ln2_scale, L1_xattn_ln2_offset, L1_xattn_wq2, L1_xattn_bq2, L1_xattn_wk2, L1_xattn_bk2, L1_xattn_wv2, L1_xattn_bv2, L1_xattn_wo2, L1_xattn_bo2, L1_xattn_bias_k2, L1_xattn_bias_v2, L1_xattn_ln_mlp_scale, L1_xattn_ln_mlp_offset, L1_xattn_w_fc1, L1_xattn_b_fc1, L1_xattn_w_fc2, L1_xattn_b_fc2)
    return x

_drawn_inputs = setup_inputs


def setup_inputs(seed=0):
    import zlib

    import numpy as np

    out = dict(_drawn_inputs(seed))
    spreads = {'L0_xattn_ln1_w': (1.0, 0.6),
     'L0_xattn_ln1_b': (0.0, 0.8),
     'L0_xattn_q_b': (0.0, 0.8),
     'L0_xattn_k_b': (0.0, 2.0),
     'L0_xattn_v_b': (0.0, 0.273),
     'L0_xattn_cproj_b': (0.0, 0.1),
     'L0_xattn_ln2_w': (1.0, 0.6),
     'L0_xattn_ln2_b': (0.0, 0.763),
     'L0_xattn_fc_b': (0.0, 0.1),
     'L0_xattn_proj_b': (0.0, 0.1),
     'L1_xattn_ln1_scale': (1.0, 0.6),
     'L1_xattn_ln1_offset': (0.0, 0.8),
     'L1_xattn_bq1': (0.0, 0.8),
     'L1_xattn_bk1': (0.0, 2.0),
     'L1_xattn_bv1': (0.0, 0.1),
     'L1_xattn_bo1': (0.0, 0.1),
     'L1_xattn_ln2_scale': (1.0, 0.6),
     'L1_xattn_ln2_offset': (0.0, 0.8),
     'L1_xattn_bq2': (0.0, 0.8),
     'L1_xattn_bk2': (0.0, 2.0),
     'L1_xattn_bv2': (0.0, 0.1),
     'L1_xattn_bo2': (0.0, 0.1),
     'L1_xattn_ln_mlp_scale': (1.0, 0.6),
     'L1_xattn_ln_mlp_offset': (0.0, 0.678),
     'L1_xattn_b_fc1': (0.0, 0.1),
     'L1_xattn_b_fc2': (0.0, 0.1)}
    factors = {'L0_xattn_q_w': 8.0,
     'L0_xattn_k_w': 8.0,
     'L1_xattn_wq1': 8.0,
     'L1_xattn_wk1': 8.0,
     'L1_xattn_bias_k1': 64.0,
     'L1_xattn_bias_v1': 64.0,
     'L1_xattn_wq2': 8.0,
     'L1_xattn_wk2': 8.0,
     'L1_xattn_bias_k2': 64.0,
     'L1_xattn_bias_v2': 64.0}
    for name, (base, spread) in spreads.items():
        noise = np.random.default_rng([zlib.crc32(name.encode()), seed]).standard_normal(out[name].shape)
        drawn = base * np.exp(spread * noise) if base else spread * noise
        out[name] = jnp.asarray(drawn.astype(out[name].dtype))
    for name, factor in factors.items():
        out[name] = (out[name] * factor).astype(out[name].dtype)
    return out
```

```python
import math
from contextlib import ExitStack

import concourse.bass as bass
from concourse import mybir

P = 128
B, S, D = 4, 256, 256
H = 16
HD0, HD1 = D // H, 128
F = 1024
NTOK = B * S
NT = NTOK // P
DC = D // P
HALF = NTOK // 2
QC = S // P
EPS = 1e-5
SLOT = 32
GROUP = 4
NGROUP = H // GROUP
KEYS1 = S + 1
KEYS1_EVEN = KEYS1 + 1
MASKED = -3.0e38

UNIT, UNITS = 512, 8
KQ_COL = [j * UNIT for j in range(GROUP)]
V_COL = GROUP * UNIT
O_COL = V_COL + 2 * UNIT
WCOLS = UNITS * UNIT
UNIT_COL = [KQ_COL[0], V_COL, V_COL + UNIT, KQ_COL[1], KQ_COL[2], O_COL, KQ_COL[3], O_COL + UNIT]
KQ_UNIT = [0, 3, 4, 6]
V_UNIT_LAST = 2
O_UNIT = [5, 7]
RING = 4
FFN1_COL = [UNIT_COL[f // 2] + f % 2 * (UNIT // 2) for f in range(F // P)]
FFN2_COL = [UNIT_COL[UNITS // 2 + f // 2] + f % 2 * (UNIT // 2) for f in range(F // P)]
ROUND_L0, ROUND_FFN0, ROUND_L1A, ROUND_L1B, ROUND_FFN1, ROUNDS = 0, 1, 2, 6, 10, 11

_COLS = {}
_n = 0
for _name, _w in [("q0", NGROUP), ("k0", NGROUP), ("v0", NGROUP), ("ln0a_w", DC), ("ln0a_b", DC),
                  ("ln0b_w", DC), ("ln0b_b", DC), ("ln1a_w", DC), ("ln1a_b", DC), ("ln1b_w", DC),
                  ("ln1b_b", DC), ("ln1c_w", DC), ("ln1c_b", DC), ("fc0", F // P), ("fc1", F // P),
                  ("q1a", H), ("k1a", H), ("bk1a", H), ("bv1a", H),
                  ("q1b", H), ("k1b", H), ("bk1b", H), ("bv1b", H)]:
    _COLS[_name] = (_n, _w)
    _n += _w
NCOLS = _n


def xattn_kernel(nc, x_d, ctxt_d, mask_d, ident_d, weights_d, cols_d, rows_d, vrows_d, out_d):
    f32, f32r, bf16, u8 = mybir.dt.float32, mybir.dt.float32r, mybir.dt.bfloat16, mybir.dt.uint8
    ALU, ACT, AX = mybir.AluOpType, mybir.ActivationFunctionType, mybir.AxisListType
    ds = bass.ds

    with ExitStack() as ctx:
        def sem(name):
            return ctx.enter_context(nc.semaphore(name))

        def pb(name, shape):
            return ctx.enter_context(nc.psum_tensor(name, shape, f32))

        def sb(name, shape, dt=f32):
            return ctx.enter_context(nc.sbuf_tensor(name, shape, dt))

        x_sb = sb("x_sb", [P, NT, D])
        ht_hi, ht_lo = sb("ht_hi", [P, DC, NTOK], f32r), sb("ht_lo", [P, DC, NTOK], f32r)
        ct_hi, ct_lo = sb("ct_hi", [P, DC, NTOK], f32r), sb("ct_lo", [P, DC, NTOK], f32r)
        w_hi, w_lo = sb("w_hi", [P, WCOLS], f32r), sb("w_lo", [P, WCOLS], f32r)
        w_raw = sb("w_raw", [P, RING, UNIT])
        cols = sb("cols", [P, NCOLS])
        rows = sb("rows", [P, 5, D])
        ident = sb("ident", [P, P])
        xn = sb("xn", [P, NT, D])
        tmp = sb("tmp", [P, 2, HALF])
        vrow = sb("vrow", [P, 2, H * HD1 // 2])
        probs = sb("probs", [P, 2, QC, KEYS1_EVEN])
        nmax, sums, rden = sb("nmax", [P, 2, QC]), sb("sums", [P, 2, QC]), sb("rden", [P, 2, QC])
        stats = sb("stats", [P, NT, 6])
        mv = sb("mv", [P, NT, 2])
        half_pow, rstd, vare = sb("half_pow", [P, NT]), sb("rstd", [P, NT]), sb("vare", [P, NT])

        base = nc.sbuf_base
        base = (base + 63) // 64 * 64
        KB = 1024

        def at(name, off, shape, dt=f32):
            return nc.alloc_sbuf_tensor_at(name, shape, dt, offset=base + off)

        kt_hi = at("kt_hi", 0, [P, 2, B, KEYS1_EVEN], f32r)
        kt_lo = at("kt_lo", 9 * KB, [P, 2, B, KEYS1_EVEN], f32r)
        v_hi, v_lo = at("v_hi", 18 * KB, [P, NT, UNIT], f32r), at("v_lo", 34 * KB, [P, NT, UNIT], f32r)
        qt_hi, qt_lo = at("qt_hi", 50 * KB, [P, 2, NTOK], f32r), at("qt_lo", 58 * KB, [P, 2, NTOK], f32r)
        cx_hi, cx_lo = at("cx_hi", 66 * KB, [P, 2, NTOK], f32r), at("cx_lo", 74 * KB, [P, 2, NTOK], f32r)
        pt_hi, pt_lo = at("pt_hi", 82 * KB, [P, 2, QC * S], f32r), at("pt_lo", 86 * KB, [P, 2, QC * S], f32r)
        v0_all = at("v0_all", 0, [P, NT, UNIT])
        q0t, k0t = at("q0t", 16 * KB, [P, NTOK]), at("k0t", 20 * KB, [P, NTOK])
        v0_now = at("v0_now", 24 * KB, [P, NT, P])
        c0_hi, c0_lo = at("c0_hi", 28 * KB, [P, NTOK], f32r), at("c0_lo", 32 * KB, [P, NTOK], f32r)
        kq_hi, kq_lo = at("kq_hi", 36 * KB, [P, UNIT], f32r), at("kq_lo", 38 * KB, [P, UNIT], f32r)
        pt0 = at("pt0", 40 * KB, [P, 2, QC * S])
        vtmp = at("vtmp", 82 * KB, [P, H * HD1])
        mask_raw = at("mask_raw", 44 * KB, [1, NTOK], u8)
        mask_row = at("mask_row", 46 * KB, [1, NTOK], bf16)
        mask_slot = at("mask_slot", 48 * KB, [1, P], bf16)
        g_hi, g_lo = at("g_hi", 50 * KB, [P, F // P, HALF], f32r), at("g_lo", 66 * KB, [P, F // P, HALF], f32r)
        ct_raw = at("ct_raw", 50 * KB, [P, DC, NTOK])

        ps_proj = pb("ps_proj", [P, 2, 512])
        ps_score = pb("ps_score", [P, QC, 512])
        ps_trans = pb("ps_trans", [P, 512])
        ps_ctx = pb("ps_ctx", [P, 512])
        ps_out = pb("ps_out", [P, 2, 512])

        def col(name, k=0):
            n, w = _COLS[name]
            return cols[:, n + k:n + k + 1]

        def col_at(name, k):
            return cols[:, ds(k + _COLS[name][0], 1)]

        x_loaded, ct_loaded, cols_loaded = sem("x_loaded"), sem("ct_loaded"), sem("cols_loaded")
        rows_loaded, ident_loaded, mask_loaded = sem("rows_loaded"), sem("ident_loaded"), sem("mask_loaded")
        vrow_loaded, vrow_ready, out_stored = sem("vrow_loaded"), sem("vrow_ready"), sem("out_stored")
        raw_loaded = [sem(f"raw_loaded{r}") for r in range(RING)]
        w_hi_ready, w_lo_ready = sem("w_hi_ready"), sem("w_lo_ready")
        consts_ready, cols_scaled, mask_ready = sem("consts_ready"), sem("cols_scaled"), sem("mask_ready")
        waited = sem("waited")
        ct_hi_ready, ct_lo_ready = sem("ct_hi_ready"), sem("ct_lo_ready")

        class NormSems:
            def __init__(self, stage):
                self.stats, self.pool, self.rstd = sem(f"ln{stage}_stats"), sem(f"ln{stage}_pool"), sem(f"ln{stage}_rstd")
                self.norm, self.turned, self.h32 = sem(f"ln{stage}_norm"), sem(f"ln{stage}_turned"), sem(f"ln{stage}_h32")
                self.hi, self.lo, self.biased = sem(f"ln{stage}_hi"), sem(f"ln{stage}_lo"), sem(f"ln{stage}_biased")

        class AttentionSems:
            def __init__(self, stage):
                self.proj, self.kq_hi, self.kq_lo = sem(f"att{stage}_proj"), sem(f"att{stage}_kq_hi"), sem(f"att{stage}_kq_lo")
                self.v32, self.v_hi, self.v_lo = sem(f"att{stage}_v32"), sem(f"att{stage}_v_hi"), sem(f"att{stage}_v_lo")
                self.learned, self.score, self.nmax = sem(f"att{stage}_learned"), sem(f"att{stage}_score"), sem(f"att{stage}_nmax")
                self.exp, self.rden, self.prob = sem(f"att{stage}_exp"), sem(f"att{stage}_rden"), sem(f"att{stage}_prob")
                self.turned, self.pt_hi, self.pt_lo = sem(f"att{stage}_turned"), sem(f"att{stage}_pt_hi"), sem(f"att{stage}_pt_lo")
                self.pv, self.cx_hi, self.cx_lo = sem(f"att{stage}_pv"), sem(f"att{stage}_cx_hi"), sem(f"att{stage}_cx_lo")
                self.out, self.acc, self.w_now = sem(f"att{stage}_out"), sem(f"att{stage}_acc"), sem(f"att{stage}_w_now")

        class MlpSems:
            def __init__(self, stage):
                self.fc1, self.gelu, self.hi = sem(f"ffn{stage}_fc1"), sem(f"ffn{stage}_gelu"), sem(f"ffn{stage}_hi")
                self.lo, self.fc2, self.acc = sem(f"ffn{stage}_lo"), sem(f"ffn{stage}_fc2"), sem(f"ffn{stage}_acc")

        LN = {s: NormSems(s) for s in range(5)}
        ATT = {s: AttentionSems(s) for s in ("0", "1a", "1b")}
        SEED = 1
        FFN = {s: MlpSems(s) for s in (0, 1)}

        TILES = ([("k", 0, 0), ("q", 0, 0)] + [("v", t, 0) for t in range(4)] + [("k", 0, 1), ("q", 0, 1)]
                 + [("v", t, 0) for t in range(4, NT)]
                 + [(w, j, h) for j in range(1, GROUP) for h in range(2) for w in "kq"])
        NTILE, NKQ, ITEMS, OUTS = len(TILES), 4 * GROUP, GROUP * B, 2 * B
        KQ_TILES = [t for t in TILES if t[0] != "v"]
        OUT_AT = {6: [0], 7: [1], 8: [2], 9: [3], 14: [4], 15: [5], 16: [6, 7]}
        SPLIT_AT = {0: [1], 1: [2], 4: [3], 8: [4], 10: [5], 12: [6], 16: [7]}
        UNIT_READ = {0: 8, 1: 12, 2: 12, 3: 16, 4: 20, 6: 24}
        SCORES_AT = {3: 0, 6: 1}
        AHEAD = TILES.index(("k", 1, 0))

        def alone(engine):
            engine.sem_inc(waited, 1)

        block = ctx.enter_context(nc.Block())

        @block.sync
        def _(sp):
            for A in ATT.values():
                for started in (A.proj, A.kq_hi, A.kq_lo, A.v32, A.v_hi, A.v_lo, A.learned, A.score, A.nmax, A.exp,
                                A.rden, A.prob, A.turned, A.pt_hi, A.pt_lo, A.pv, A.cx_hi, A.cx_lo, A.out, A.acc,
                                A.w_now):
                    sp.sem_inc(started, SEED)
            sp.dma_start(x_sb[:, :, :], x_d).then_inc(x_loaded, 16)
            sp.dma_start(ident[:, :], ident_d).then_inc(ident_loaded, 16)
            sp.dma_start(cols[:, :], cols_d).then_inc(cols_loaded, 16)
            sp.dma_start(mask_raw[:, :], mask_d).then_inc(mask_loaded, 16)
            sp.dma_start(ct_raw[:, :, :], ctxt_d).then_inc(ct_loaded, 16)

            for u in range(RING):
                sp.dma_start(w_raw[:, u, :], weights_d[0, :, u * UNIT:(u + 1) * UNIT]).then_inc(raw_loaded[u], 16)
            sp.dma_start(rows[:, :, :], rows_d.partition_broadcast(P)).then_inc(rows_loaded, 16)
            for u in range(RING, UNITS):
                sp.wait_ge(w_lo_ready, u - RING + 1)
                sp.dma_start(w_raw[:, u - RING, :],
                             weights_d[0, :, u * UNIT:(u + 1) * UNIT]).then_inc(raw_loaded[u - RING], 16)
            with sp.Fori(1, ROUNDS) as g:
                for u in range(UNITS):
                    sp.wait_ge(w_lo_ready, g * UNITS + (u - RING + 1))
                    sp.dma_start(w_raw[:, u % RING, :],
                                 weights_d[ds(g, 1), :, u * UNIT:(u + 1) * UNIT]
                                 .rearrange("a p c -> (a p) c")).then_inc(raw_loaded[u % RING], 16)
            for t in range(2):
                sp.wait_ge(FFN[1].acc, 2 * (t + 1))
                sp.dma_start(out_d[:, 4 * t:4 * t + 4, :], x_sb[:, 4 * t:4 * t + 4, :]).then_inc(out_stored, 16)
            sp.wait_ge(out_stored, 32)

        @block.gpsimd
        def _(pool):
            def split_lo(g, u):
                c = UNIT_COL[u]
                pool.wait_ge(w_hi_ready, g * UNITS + u + 1)
                nc.gpsimd.tensor_tensor(w_lo[:, c:c + UNIT], w_raw[:, u % RING, :],
                                        w_hi[:, c:c + UNIT].bitcast(f32), ALU.subtract).then_inc(w_lo_ready, 1)

            def layer_norm(s, splits=()):
                L = LN[s]
                for half in range(2):
                    t0 = 4 * half
                    pool.wait_ge(L.stats, 8 * (half + 1))
                    nc.gpsimd.tensor_scalar(vare[:, t0:t0 + 4], mv[:, t0:t0 + 4, 1], EPS, 1.0,
                                            ALU.add, ALU.mult).then_inc(L.pool, 1)
                    pool.wait_ge(L.pool, half + 1)
                    nc.gpsimd.tensor_tensor(rstd[:, t0:t0 + 4], vare[:, t0:t0 + 4], half_pow[:, t0:t0 + 4],
                                            ALU.pow).then_inc(L.rstd, 1)
                for g, u in splits:
                    split_lo(g, u)
                pool.wait_ge(rows_loaded, 16)
                for t in range(NT):
                    pool.wait_ge(L.norm, t + 1)
                    nc.gpsimd.tensor_tensor(x_sb[:, t, :], x_sb[:, t, :], rows[:, s, :],
                                            ALU.add).then_inc(L.biased, 1)

            def normalise(A, n, first, width):
                pool.wait_ge(A.rden, first + n + 1 + SEED)
                alone(pool)
                for c in range(QC):
                    last = nc.gpsimd.tensor_scalar(probs[:, n % 2, c, 0:width], probs[:, n % 2, c, 0:width],
                                                   rden[:, n % 2, c:c + 1], 1.0, ALU.mult, ALU.mult)
                last.then_inc(A.prob, 1)

            def value_rows(s):
                pool.wait_ge(vrow_loaded, 32 * (s + 1))
                for k in range(2):
                    w = H * HD1 // 2
                    nc.gpsimd.tensor_tensor(vrow[:, k, :], vrow[:, k, :], vtmp[:, k * w:(k + 1) * w],
                                            ALU.subtract).then_inc(vrow_ready, 1)

            def attention1(A, name, g0):
                def learned_key(g, it, j):
                    par = j % 2
                    bk = cols[:, ds((g - g0) * GROUP + (_COLS["bk" + name][0] + j), 1)].to_broadcast([P, B])
                    pool.wait_ge(A.score, it * ITEMS + max(0, 4 * (j - 1)) + SEED)
                    alone(pool)
                    nc.gpsimd.tensor_copy(kt_hi[:, par, :, S], bk).then_inc(A.learned, 1)
                    pool.wait_ge(A.learned, it * 2 * GROUP + 2 * j + 1 + SEED)
                    alone(pool)
                    nc.gpsimd.tensor_tensor(kt_lo[:, par, :, S], bk, kt_hi[:, par, :, S].bitcast(f32),
                                            ALU.subtract).then_inc(A.learned, 1)

                def v_lo_tile(it, t):
                    pool.wait_ge(A.v_hi, it * NT + t + 1 + SEED)
                    nc.gpsimd.tensor_tensor(v_lo[:, t, :], tmp[:, t % 2, :], v_hi[:, t, :].bitcast(f32),
                                            ALU.subtract).then_inc(A.v_lo, 1)

                with pool.Fori(g0, g0 + NGROUP) as g:
                    it = g - g0
                    learned_key(g, it, 0)
                    for t in range(NT):
                        if t == 3:
                            normalise(A, 0, it * ITEMS, S)
                        if t == 4:
                            normalise(A, 1, it * ITEMS, S)
                            split_lo(g + 1, 0)
                        v_lo_tile(it, t)
                    for n in range(ITEMS + 1):
                        j, b = divmod(n, B)
                        if b == 0 and j < GROUP - 1:
                            learned_key(g, it, j + 1)
                        if n + 2 < ITEMS:
                            normalise(A, n + 2, it * ITEMS, S)
                        for u in SPLIT_AT.get(n, ()):
                            split_lo(g + 1, u)

            nc.gpsimd.memset(half_pow[:, :], -0.5).then_inc(consts_ready, 1)
            pool.wait_ge(consts_ready, 1)
            layer_norm(0, [(ROUND_L0, u) for u in range(UNITS)])
            value_rows(0)
            A = ATT["0"]
            with pool.Fori(0, NGROUP) as i:
                for n in range(ITEMS):
                    normalise(A, n, i * ITEMS, S)
            layer_norm(1, [(ROUND_FFN0, u) for u in range(UNITS)])
            for u in range(UNITS // 2):
                split_lo(ROUND_L1A, u)
            layer_norm(2, [(ROUND_L1A, u) for u in range(UNITS // 2, UNITS)])
            attention1(ATT["1a"], "1a", ROUND_L1A)
            layer_norm(3)
            value_rows(1)
            attention1(ATT["1b"], "1b", ROUND_L1B)
            layer_norm(4)


        @block.scalar
        def _(act):
            def split_hi(g, u):
                c = UNIT_COL[u]
                act.wait_ge(raw_loaded[u % RING], g * (16 * UNITS // RING) + 16 * (u // RING + 1))
                nc.scalar.activation(w_hi[:, c:c + UNIT], w_raw[:, u % RING, :], ACT.Copy).then_inc(w_hi_ready, 1)

            def layer_norm(s):
                L = LN[s]
                for e in range(4):
                    half, c = divmod(e, DC)
                    act.wait_ge(L.h32, e + 1)
                    nc.scalar.activation(ht_hi[:, c, half * HALF:(half + 1) * HALF], tmp[:, e % 2, :],
                                         ACT.Copy).then_inc(L.hi, 1)

            def exps(A, n, first, width):
                act.wait_ge(A.nmax, first + n + 1 + SEED)
                act.wait_ge(A.turned, first + max(0, n - 1) + SEED)
                for c in range(QC):
                    last = nc.scalar.activation(probs[:, n % 2, c, 0:width], ps_score[:, c, 0:width], ACT.Exp,
                                                bias=nmax[:, n % 2, c:c + 1], accum_out=sums[:, n % 2, c:c + 1])
                last.then_inc(A.exp, 1)

            def load_value_rows(s):
                act.dma_start(vrow[:, :, :].rearrange("p k w -> p (k w)"),
                              vrows_d[2 * s, :].partition_broadcast(P)).then_inc(vrow_loaded, 16)
                act.dma_start(vtmp[:, :], vrows_d[2 * s + 1, :].partition_broadcast(P)).then_inc(vrow_loaded, 16)

            for u in range(3):
                split_hi(0, u)
            act.wait_ge(ct_loaded, 16)
            for c in range(DC):
                nc.scalar.activation(ct_hi[:, c, :], ct_raw[:, c, :], ACT.Copy).then_inc(ct_hi_ready, 1)
            load_value_rows(0)
            for u in range(3, UNITS):
                split_hi(0, u)
            layer_norm(0)

            A = ATT["0"]
            for t in range(NT):
                act.wait_ge(A.proj, t + 1 + SEED)
                nc.scalar.activation(v0_all[:, t, :], ps_proj[:, t % 2, :], ACT.Copy).then_inc(A.v32, 1)
            act.wait_ge(cols_scaled, 5)
            act.wait_ge(w_hi_ready, UNITS)
            with act.Fori(0, NGROUP) as i:
                first = i * ITEMS

                def proj(k, name, dst, half):
                    act.wait_ge(A.score, first + SEED)
                    act.wait_ge(A.proj, i * 4 + (NT + k + 1) + SEED)
                    alone(act)
                    nc.scalar.activation(dst[:, half * HALF:(half + 1) * HALF], ps_proj[:, k % 2, :], ACT.Identity,
                                         bias=col_at(name, i)).then_inc(A.kq_hi, 1)

                act.wait_ge(A.proj, i * 4 + NT + SEED)
                alone(act)
                nc.scalar.activation(kq_hi[:, :], w_hi[:, ds(i * UNIT, UNIT)], ACT.Copy).then_inc(A.w_now, 1)
                proj(0, "k0", k0t, 0)
                proj(1, "q0", q0t, 0)
                exps(A, 0, first, S)
                proj(2, "k0", k0t, 1)
                proj(3, "q0", q0t, 1)
                for n in range(ITEMS):
                    b, j = divmod(n, GROUP)
                    if n < ITEMS - 1:
                        exps(A, n + 1, first, S)
                    if j == GROUP - 1:
                        act.wait_ge(A.out, i * B + b + SEED)
                        act.wait_ge(A.pv, first + n + 1 + SEED)
                        alone(act)
                        nc.scalar.activation(c0_hi[:, b * S:(b + 1) * S], ps_ctx[:, 0:S], ACT.Identity,
                                             bias=col_at("v0", i)).then_inc(A.cx_hi, 1)
            act.wait_ge(A.w_now, 2 * NGROUP + SEED)
            for u in range(UNITS):
                if u == UNITS // 2:
                    act.wait_ge(A.out, NGROUP * B + SEED)
                split_hi(ROUND_FFN0, u)
            layer_norm(1)

            def ffn(s, func, name, next_round):
                N = FFN[s]
                act.wait_ge(LN[1 if s == 0 else 4].lo, 4)
                for half in range(2):
                    for f in range(F // P):
                        k = half * (F // P) + f
                        act.wait_ge(N.fc1, k + 1)
                        if k >= 2:
                            act.wait_ge(N.lo, k - 1)
                        nc.scalar.activation(tmp[:, k % 2, :], ps_proj[:, k % 2, :], func,
                                             bias=col(name, f)).then_inc(N.gelu, 1)
                if next_round is not None:
                    act.wait_ge(N.fc1, 2 * F // P)
                    for u in range(UNITS):
                        if u == UNITS // 2:
                            act.wait_ge(N.fc2, 4)
                        split_hi(next_round, u)

            ffn(0, ACT.Gelu_apprx_tanh, "fc0", ROUND_L1A)
            layer_norm(2)

            def attention1(A, name, g0):
                with act.Fori(g0, g0 + NGROUP) as g:
                    it = g - g0
                    first = it * ITEMS

                    def kq_tile(t):
                        w, j, half = TILES[t]
                        act.wait_ge(A.score, first + max(0, 4 * (j - 1)) + SEED)
                        act.wait_ge(A.proj, it * NTILE + (t + 1) + SEED)
                        alone(act)
                        bias = cols[:, ds(it * GROUP + (_COLS[w + name][0] + j), 1)]
                        if w == "k":
                            out = kt_hi[:, j % 2, 2 * half:2 * half + 2, 0:S]
                            src = ps_proj[:, t % 2, :].rearrange("p (b k) -> p b k", b=2)
                        else:
                            out = qt_hi[:, j % 2, half * HALF:(half + 1) * HALF]
                            src = ps_proj[:, t % 2, :]
                        nc.scalar.activation(out, src, ACT.Identity, bias=bias).then_inc(A.kq_hi, 1)

                    def v_tile(t):
                        act.wait_ge(A.v32, it * NT + t + 1 + SEED)
                        nc.scalar.activation(v_hi[:, t, :], tmp[:, t % 2, :], ACT.Copy).then_inc(A.v_hi, 1)

                    def context(m):
                        j, b = divmod(m, B)
                        if j < 2:
                            act.wait_ge(A.out, it * OUTS + SEED)
                        else:
                            act.wait_ge(A.out, it * OUTS + b + 1 + SEED)
                        act.wait_ge(A.pv, first + m + 1 + SEED)
                        alone(act)
                        nc.scalar.activation(cx_hi[:, j % 2, b * S:(b + 1) * S], ps_ctx[:, 0:S], ACT.Identity,
                                             bias=cols[:, ds(it * GROUP + (_COLS["bv" + name][0] + j), 1)])\
                            .then_inc(A.cx_hi, 1)

                    for t in range(AHEAD):
                        if t in SCORES_AT:
                            exps(A, SCORES_AT[t], first, KEYS1)
                        if TILES[t][0] == "v":
                            v_tile(TILES[t][1])
                        else:
                            kq_tile(t)
                        if t == UNIT_READ[0] - 1:
                            act.wait_ge(A.proj, it * NTILE + UNIT_READ[0] + SEED)
                            split_hi(g + 1, 0)
                    for n in range(ITEMS + 1):
                        if n < ITEMS:
                            act.wait_ge(A.pv, first + max(0, n - 1) + SEED)
                            act.wait_ge(A.turned, first + n + 1 + SEED)
                            nc.scalar.activation(pt_hi[:, n % 2, :], ps_trans[:, :], ACT.Copy).then_inc(A.pt_hi, 1)
                        if AHEAD + n < NTILE:
                            kq_tile(AHEAD + n)
                        if n + 2 < ITEMS:
                            exps(A, n + 2, first, KEYS1)
                        if n > 0:
                            context(n - 1)
                        for u in SPLIT_AT.get(n, ()):
                            if u in O_UNIT:
                                act.wait_ge(A.out, it * OUTS + 4 * (O_UNIT.index(u) + 1) + SEED)
                            else:
                                act.wait_ge(A.proj, it * NTILE + UNIT_READ[u] + SEED)
                            split_hi(g + 1, u)

            attention1(ATT["1a"], "1a", ROUND_L1A)
            act.wait_ge(ATT["1a"].pv, NGROUP * ITEMS + SEED)
            act.wait_ge(ATT["1a"].v32, NGROUP * NT + SEED)
            load_value_rows(1)
            layer_norm(3)
            attention1(ATT["1b"], "1b", ROUND_L1B)
            layer_norm(4)
            ffn(1, ACT.Gelu, "fc1", None)

        @block.vector
        def _(dve):
            def layer_norm(s, w, b, ready):
                L = LN[s]
                for half in range(2):
                    for t in range(4 * half, 4 * half + 4):
                        ready(t)
                        nc.vector.bn_stats(stats[:, t, :], x_sb[:, t, :]).then_inc(L.stats, 1)
                    for t in range(4 * half, 4 * half + 4):
                        dve.wait_ge(L.stats, 8 * half + t - 4 * half + 1)
                        nc.vector.bn_aggr(mv[:, t, :], stats[:, t, :]).then_inc(L.stats, 1)
                for half in range(2):
                    dve.wait_ge(L.stats, 8 * (half + 1))
                    dve.wait_ge(L.rstd, half + 1)
                    for t in range(4 * half, 4 * half + 4):
                        nc.vector.tensor_scalar(xn[:, t, :], x_sb[:, t, :], mv[:, t, 0:1], rstd[:, t:t + 1],
                                                ALU.subtract, ALU.mult).then_inc(L.norm, 1)
                dve.wait_ge(cols_scaled, 5)

                def scaled(e):
                    half, c = divmod(e, DC)
                    if e >= 2:
                        dve.wait_ge(L.lo, e - 1)
                    dve.wait_ge(L.turned, e + 1)
                    nc.vector.tensor_scalar(tmp[:, e % 2, :], ps_proj[:, e % 2, :], col(w, c), col(b, c),
                                            ALU.mult, ALU.add).then_inc(L.h32, 1)

                def low(e):
                    half, c = divmod(e, DC)
                    tok = slice(half * HALF, (half + 1) * HALF)
                    dve.wait_ge(L.hi, e + 1)
                    nc.vector.tensor_tensor(ht_lo[:, c, tok], tmp[:, e % 2, :], ht_hi[:, c, tok].bitcast(f32),
                                            ALU.subtract).then_inc(L.lo, 1)

                scaled(0)
                scaled(1)
                low(0)
                scaled(2)
                low(1)
                scaled(3)
                low(2)
                low(3)

            def negmax(A, n, first, width):
                dve.wait_ge(A.score, first + n + 1 + SEED)
                nc.vector.tensor_reduce(nmax[:, n % 2, :], ps_score[:, :, 0:width], AX.X, ALU.max, negate=True)\
                    .then_inc(A.nmax, 1)

            def reciprocals(A, n, first):
                dve.wait_ge(A.exp, first + n + 1 + SEED)
                nc.vector.reciprocal(rden[:, n % 2, :], sums[:, n % 2, :]).then_inc(A.rden, 1)

            def accumulate(A, k, bank, t):
                dve.wait_ge(A.out, k + 1 + SEED)
                nc.vector.tensor_tensor(x_sb[:, t:t + 2, :], x_sb[:, t:t + 2, :],
                                        ps_out[:, bank, :].rearrange("p (t d) -> p t d", t=2), ALU.add)\
                    .then_inc(A.acc, 1)

            nc.vector.memset(mask_slot[:, :], 0.0).then_inc(consts_ready, 1)
            dve.wait_ge(consts_ready, 2)
            nc.vector.memset(mask_slot[:, :].rearrange("p (j w) -> p j w", w=SLOT)[:, :, HD0:HD0 + 1], 1.0)\
                .then_inc(consts_ready, 1)
            dve.wait_ge(mask_loaded, 16)
            nc.vector.tensor_scalar(mask_row[:, :], mask_raw[:, :], 1.0, -MASKED, ALU.subtract, ALU.mult)\
                .then_inc(mask_ready, 1)
            dve.wait_ge(cols_loaded, 16)
            s0, s1 = 1.0 / math.sqrt(HD0), 1.0 / math.sqrt(HD1)
            for names, f in ((("q0",), s0), (("ln0a_w", "ln0a_b"), s0),
                             (("ln1a_w", "ln1a_b", "ln1b_w", "ln1b_b"), s1), (("q1a",), s1), (("q1b",), s1)):
                lo = _COLS[names[0]][0]
                hi = sum(_COLS[names[-1]])
                last = nc.vector.tensor_scalar(cols[:, lo:hi], cols[:, lo:hi], f, None, ALU.mult)
                last.then_inc(cols_scaled, 1)
            for c in range(DC):
                dve.wait_ge(ct_hi_ready, c + 1)
                nc.vector.tensor_tensor(ct_lo[:, c, :], ct_raw[:, c, :], ct_hi[:, c, :].bitcast(f32),
                                        ALU.subtract).then_inc(ct_lo_ready, 1)

            layer_norm(0, "ln0a_w", "ln0a_b", lambda t: dve.wait_ge(x_loaded, 16))

            A = ATT["0"]
            dve.wait_ge(A.v32, NT + SEED)
            dve.wait_ge(w_lo_ready, UNITS)
            with dve.Fori(0, NGROUP) as i:
                first = i * ITEMS
                dve.wait_ge(A.proj, i * 4 + NT + SEED)
                nc.vector.tensor_copy(kq_lo[:, :], w_lo[:, ds(i * UNIT, UNIT)].bitcast(f32)).then_inc(A.w_now, 1)
                dve.wait_ge(A.pv, first + SEED)
                nc.vector.tensor_copy(v0_now[:, :, :], v0_all[:, :, ds(i * P, P)]).then_inc(A.v_lo, 1)
                negmax(A, 0, first, S)
                reciprocals(A, 0, first)
                for n in range(ITEMS):
                    b, j = divmod(n, GROUP)
                    dve.wait_ge(A.pv, first + max(0, n - 1) + SEED)
                    dve.wait_ge(A.turned, first + n + 1 + SEED)
                    nc.vector.tensor_copy(pt0[:, n % 2, :], ps_trans[:, :]).then_inc(A.pt_lo, 1)
                    if n < ITEMS - 1:
                        negmax(A, n + 1, first, S)
                    if j == GROUP - 1:
                        dve.wait_ge(A.cx_hi, i * B + b + 1 + SEED)
                        nc.vector.scalar_tensor_tensor(out=c0_lo[:, b * S:(b + 1) * S], in0=ps_ctx[:, 0:S],
                                                       scalar=col_at("v0", i),
                                                       in1=c0_hi[:, b * S:(b + 1) * S].bitcast(f32),
                                                       op0=ALU.add, op1=ALU.subtract).then_inc(A.cx_lo, 1)
                    if n < ITEMS - 1:
                        reciprocals(A, n + 1, first)
                    if j == 0 and b > 0:
                        if b == 1:
                            dve.wait_ge(LN[0].biased, NT)
                        dve.wait_ge(A.acc, i * B + 0 + SEED)
                        accumulate(A, i * B + b - 1, (b - 1) % 2, 2 * (b - 1))
                accumulate(A, i * B + B - 1, (B - 1) % 2, 2 * (B - 1))

            layer_norm(1, "ln0b_w", "ln0b_b", lambda t: dve.wait_ge(ATT["0"].acc, NGROUP * B - 3 + t // 2 + SEED))

            def ffn(s):
                N = FFN[s]
                nf = F // P
                dve.wait_ge(LN[1 if s == 0 else 4].biased, NT)
                for half in range(2):
                    for f in range(nf):
                        k = half * nf + f
                        if half:
                            dve.wait_ge(N.fc2, 2)
                        dve.wait_ge(N.gelu, k + 1)
                        nc.vector.tensor_copy(g_hi[:, f, :], tmp[:, k % 2, :]).then_inc(N.hi, 1)
                        dve.wait_ge(N.hi, k + 1)
                        nc.vector.tensor_tensor(g_lo[:, f, :], tmp[:, k % 2, :], g_hi[:, f, :].bitcast(f32),
                                                ALU.subtract).then_inc(N.lo, 1)
                    for r in range(2):
                        k, t = 2 * half + r, 4 * half + 2 * r
                        dve.wait_ge(N.fc2, k + 1)
                        nc.vector.tensor_tensor(x_sb[:, t:t + 2, :], x_sb[:, t:t + 2, :],
                                                ps_out[:, r, :].rearrange("p (t d) -> p t d", t=2), ALU.add)\
                            .then_inc(N.acc, 1)

            ffn(0)
            for part in (kt_hi, kt_lo):
                nc.vector.memset(part[:, :, :, KEYS1:KEYS1_EVEN].bitcast(f32), 0.0).then_inc(consts_ready, 1)
            layer_norm(2, "ln1a_w", "ln1a_b", lambda t: dve.wait_ge(FFN[0].acc, t // 2 + 1))

            def attention1(A, name, g0, s):
                dve.wait_ge(vrow_ready, 2 * (s + 1))
                dve.wait_ge(LN[2 + s].biased, NT)
                with dve.Fori(g0, g0 + NGROUP) as g:
                    it = g - g0
                    first = it * ITEMS
                    vr = vrow[:, :, :].rearrange("p k w -> p (k w)")

                    def kq_tile(t):
                        w, j, half = TILES[t]
                        dve.wait_ge(A.kq_hi, it * NKQ + KQ_TILES.index(TILES[t]) + 1 + SEED)
                        bias = cols[:, ds(it * GROUP + (_COLS[w + name][0] + j), 1)]
                        if w == "k":
                            out = kt_lo[:, j % 2, 2 * half:2 * half + 2, 0:S]
                            hi = kt_hi[:, j % 2, 2 * half:2 * half + 2, 0:S]
                            src = ps_proj[:, t % 2, :].rearrange("p (b k) -> p b k", b=2)
                        else:
                            out = qt_lo[:, j % 2, half * HALF:(half + 1) * HALF]
                            hi = qt_hi[:, j % 2, half * HALF:(half + 1) * HALF]
                            src = ps_proj[:, t % 2, :]
                        nc.vector.scalar_tensor_tensor(out=out, in0=src, scalar=bias, in1=hi.bitcast(f32),
                                                       op0=ALU.add, op1=ALU.subtract).then_inc(A.kq_lo, 1)

                    def v_tile(t):
                        dve.wait_ge(A.v_lo, it * NT + max(0, t - 1) + SEED)
                        dve.wait_ge(A.proj, it * NTILE + TILES.index(("v", t, 0)) + 1 + SEED)
                        nc.vector.tensor_tensor(tmp[:, t % 2, :], ps_proj[:, t % 2, :],
                                                vr[:, ds(it * UNIT, UNIT)], ALU.add).then_inc(A.v32, 1)

                    def context(m):
                        j, b = divmod(m, B)
                        dve.wait_ge(A.cx_hi, first + m + 1 + SEED)
                        nc.vector.scalar_tensor_tensor(out=cx_lo[:, j % 2, b * S:(b + 1) * S], in0=ps_ctx[:, 0:S],
                                                       scalar=cols[:, ds(it * GROUP + (_COLS["bv" + name][0] + j), 1)],
                                                       in1=cx_hi[:, j % 2, b * S:(b + 1) * S].bitcast(f32),
                                                       op0=ALU.add, op1=ALU.subtract).then_inc(A.cx_lo, 1)

                    for t in range(AHEAD):
                        if t in SCORES_AT:
                            negmax(A, SCORES_AT[t], first, KEYS1)
                        if TILES[t][0] == "v":
                            v_tile(TILES[t][1])
                        else:
                            kq_tile(t)
                        if t - 1 in SCORES_AT:
                            reciprocals(A, SCORES_AT[t - 1], first)
                    for n in range(ITEMS + 1):
                        if n < ITEMS:
                            dve.wait_ge(A.pt_hi, first + n + 1 + SEED)
                            nc.vector.tensor_tensor(pt_lo[:, n % 2, :], ps_trans[:, :],
                                                    pt_hi[:, n % 2, :].bitcast(f32), ALU.subtract).then_inc(A.pt_lo, 1)
                        if AHEAD + n < NTILE:
                            kq_tile(AHEAD + n)
                        if n + 2 < ITEMS:
                            negmax(A, n + 2, first, KEYS1)
                        if n > 0:
                            context(n - 1)
                        if n + 2 < ITEMS:
                            reciprocals(A, n + 2, first)
                        for o in OUT_AT.get(n, ()):
                            dve.wait_ge(A.acc, it * OUTS + o // B * B + SEED)
                            accumulate(A, it * OUTS + o, o % 2, 2 * (o % B))

            attention1(ATT["1a"], "1a", ROUND_L1A, 0)
            layer_norm(3, "ln1b_w", "ln1b_b", lambda t: dve.wait_ge(ATT["1a"].acc, NGROUP * OUTS - 3 + t // 2 + SEED))
            attention1(ATT["1b"], "1b", ROUND_L1B, 1)
            layer_norm(4, "ln1c_w", "ln1c_b", lambda t: dve.wait_ge(ATT["1b"].acc, NGROUP * OUTS - 3 + t // 2 + SEED))
            ffn(1)

        @block.tensor
        def _(pe):
            def mm3(out, w, x, start, stop):
                (wh, wl), (xh, xl) = w, x
                pe.matmul(out, wl, xh, start=start, stop=False)
                pe.matmul(out, wh, xl, start=False, stop=False)
                return pe.matmul(out, wh, xh, start=False, stop=stop)

            def both(pair, *index):
                return pair[0][index], pair[1][index]

            W, HT, CT = (w_hi, w_lo), (ht_hi, ht_lo), (ct_hi, ct_lo)
            ALLP = slice(None)

            def layer_norm(s):
                L = LN[s]
                for e in range(4):
                    half, c = divmod(e, DC)
                    pe.wait_ge(L.norm, 4 * (half + 1))
                    if e >= 2:
                        pe.wait_ge(L.h32, e - 1)
                    for k in range(4):
                        last = pe.transpose(ps_proj[:, e % 2, k * P:(k + 1) * P],
                                            xn[:, 4 * half + k, c * P:(c + 1) * P], ident[:, :])
                    last.then_inc(L.turned, 1)

            def transposes(A, n, first):
                pe.wait_ge(A.prob, first + n + 1 + SEED)
                pe.wait_ge(A.pt_lo, first + n + SEED)
                for kc in range(QC):
                    for c in range(QC):
                        last = pe.transpose(ps_trans[:, kc * S + c * P:kc * S + (c + 1) * P],
                                            probs[:, n % 2, c, kc * P:(kc + 1) * P], ident[:, :])
                last.then_inc(A.turned, 1)

            pe.wait_ge(ident_loaded, 16)
            layer_norm(0)

            A = ATT["0"]
            pe.wait_ge(ct_lo_ready, DC)
            pe.wait_ge(w_lo_ready, V_UNIT_LAST + 1)
            pe.wait_ge(LN[0].h32, 4)
            for t in range(NT):
                if t >= 2:
                    pe.wait_ge(A.v32, t - 1 + SEED)
                for c in range(DC):
                    last = mm3(ps_proj[:, t % 2, :], both(CT, ALLP, c, slice(t * P, (t + 1) * P)),
                               both(W, ALLP, slice(V_COL + c * UNIT, V_COL + (c + 1) * UNIT)),
                               c == 0, c == DC - 1)
                last.then_inc(A.proj, 1)
            pe.wait_ge(LN[0].lo, 4)
            pe.wait_ge(A.v32, NT + SEED)
            pe.wait_ge(w_lo_ready, UNITS)
            pe.wait_ge(mask_ready, 1)
            pe.wait_ge(consts_ready, 3)
            with pe.Fori(0, NGROUP) as i:
                first = i * ITEMS

                def proj0(k, keys, half):
                    if k >= 2:
                        pe.wait_ge(A.kq_hi, i * 4 + k - 1 + SEED)
                    tok = slice(half * HALF, (half + 1) * HALF)
                    for c in range(DC):
                        o = (0 if keys else D) + c * P
                        last = mm3(ps_proj[:, k % 2, :], (kq_hi[:, o:o + P], kq_lo[:, o:o + P]),
                                   both(CT if keys else HT, ALLP, c, tok), c == 0, not keys and c == DC - 1)
                    if keys:
                        last = pe.matmul(ps_proj[:, k % 2, :], mask_slot[:, :], mask_row[:, tok],
                                         start=False, stop=True)
                    last.then_inc(A.proj, 1)

                def scores(n):
                    b, j = divmod(n, GROUP)
                    rows_j = slice(j * SLOT, (j + 1) * SLOT)
                    pe.wait_ge(A.kq_hi, i * 4 + (2 if b < 2 else 4) + SEED)
                    pe.wait_ge(A.exp, first + n + SEED)
                    for c in range(QC):
                        last = pe.matmul(ps_score[:, c, 0:S], q0t[rows_j, b * S + c * P:b * S + (c + 1) * P],
                                         k0t[rows_j, b * S:(b + 1) * S], start=True, stop=True)
                    last.then_inc(A.score, 1)

                def out0(b):
                    k = i * B + b
                    pe.wait_ge(A.acc, k + (0 if b == 0 else -1) + SEED)
                    pe.wait_ge(A.cx_lo, k + 1 + SEED)
                    for q in range(QC):
                        t = QC * b + q
                        last = mm3(ps_out[:, b % 2, q * D:(q + 1) * D],
                                   (c0_hi[:, t * P:(t + 1) * P], c0_lo[:, t * P:(t + 1) * P]),
                                   both(W, ALLP, ds(i * D + O_COL, D)), True, True)
                    last.then_inc(A.out, 1)

                pe.wait_ge(A.w_now, i * 2 + 2 + SEED)
                pe.wait_ge(A.kq_hi, i * 4 + SEED)
                proj0(0, True, 0)
                proj0(1, False, 0)
                scores(0)
                proj0(2, True, 1)
                proj0(3, False, 1)
                pe.wait_ge(A.v_lo, i + 1 + SEED)
                for n in range(ITEMS):
                    b, j = divmod(n, GROUP)
                    transposes(A, n, first)
                    if n < ITEMS - 1:
                        scores(n + 1)
                    if j == 0 and b > 0:
                        out0(b - 1)
                    pe.wait_ge(A.pt_lo, first + n + 1 + SEED)
                    pe.wait_ge(A.cx_lo, i * B + b + SEED)
                    for kc in range(QC):
                        last = pe.matmul(ps_ctx[j * SLOT:(j + 1) * SLOT, 0:S],
                                         v0_now[:, QC * b + kc, j * SLOT:(j + 1) * SLOT],
                                         pt0[:, n % 2, kc * S:(kc + 1) * S], start=kc == 0, stop=kc == QC - 1)
                    last.then_inc(A.pv, 1)
                out0(B - 1)
            pe.wait_ge(A.kq_hi, NGROUP * 4 + SEED)

            layer_norm(1)

            def ffn(s, g, turned):
                N = FFN[s]
                nf = F // P
                pe.wait_ge(turned.lo, 4)
                for half in range(2):
                    tok = slice(half * HALF, (half + 1) * HALF)
                    for f in range(nf):
                        k = half * nf + f
                        if k >= 2:
                            pe.wait_ge(N.gelu, k - 1)
                        pe.wait_ge(w_lo_ready, g * UNITS + f // 2 + 1)
                        for c in range(DC):
                            o = FFN1_COL[f] + c * P
                            last = mm3(ps_proj[:, k % 2, :], both(W, ALLP, slice(o, o + P)),
                                       both(HT, ALLP, c, tok), c == 0, c == DC - 1)
                        last.then_inc(N.fc1, 1)
                    for r in range(2):
                        if half:
                            pe.wait_ge(N.acc, r + 1)
                        for q in range(2):
                            t = 2 * r + q
                            for f in range(nf):
                                if t == 0:
                                    pe.wait_ge(w_lo_ready, g * UNITS + (UNITS // 2 + f // 2 + 1))
                                    pe.wait_ge(N.lo, half * nf + f + 1)
                                o = FFN2_COL[f]
                                last = mm3(ps_out[:, r, q * D:(q + 1) * D],
                                           both((g_hi, g_lo), ALLP, f, slice(t * P, (t + 1) * P)),
                                           both(W, ALLP, slice(o, o + D)), f == 0, f == nf - 1)
                        last.then_inc(N.fc2, 1)

            ffn(0, ROUND_FFN0, LN[1])
            pe.wait_ge(FFN[0].gelu, 2 * F // P)
            layer_norm(2)

            def attention1(A, g0, turned):
                pe.wait_ge(turned.h32, 4)
                pe.wait_ge(consts_ready, 5)
                with pe.Fori(g0, g0 + NGROUP) as g:
                    it = g - g0
                    first = it * ITEMS

                    def tile(t):
                        w, j, half = TILES[t]
                        if t >= 2:
                            if TILES[t - 2][0] == "v":
                                pe.wait_ge(A.v32, it * NT + TILES[t - 2][1] + 1 + SEED)
                            else:
                                pe.wait_ge(A.kq_lo, it * NKQ + KQ_TILES.index(TILES[t - 2]) + 1 + SEED)
                        elif t == 0:
                            pe.wait_ge(A.kq_lo, it * NKQ + SEED)
                        if w == "v":
                            if j == 0:
                                pe.wait_ge(w_lo_ready, g * UNITS + (V_UNIT_LAST + 1))
                            for c in range(DC):
                                last = mm3(ps_proj[:, t % 2, :], both(CT, ALLP, c, slice(j * P, (j + 1) * P)),
                                           both(W, ALLP, slice(V_COL + c * UNIT, V_COL + (c + 1) * UNIT)),
                                           c == 0, c == DC - 1)
                        else:
                            if w == "k" and half == 0:
                                pe.wait_ge(w_lo_ready, g * UNITS + (KQ_UNIT[j] + 1))
                            if w == "q" and j == 0:
                                pe.wait_ge(turned.lo, 2 * (half + 1))
                            tok = slice(half * HALF, (half + 1) * HALF)
                            for c in range(DC):
                                o = KQ_COL[j] + (0 if w == "k" else D) + c * P
                                last = mm3(ps_proj[:, t % 2, :], both(W, ALLP, slice(o, o + P)),
                                           both(CT if w == "k" else HT, ALLP, c, tok), c == 0, c == DC - 1)
                        last.then_inc(A.proj, 1)

                    def scores(n):
                        j, b = divmod(n, B)
                        need = max(KQ_TILES.index((w, j, b // 2)) for w in "kq") + 1
                        pe.wait_ge(A.kq_lo, it * NKQ + need + SEED)
                        if b == 0:
                            pe.wait_ge(A.learned, it * 2 * GROUP + 2 * j + 2 + SEED)
                        pe.wait_ge(A.exp, first + n + SEED)
                        for c in range(QC):
                            q = b * S + c * P
                            last = mm3(ps_score[:, c, 0:KEYS1_EVEN], both((qt_hi, qt_lo), ALLP, j % 2, slice(q, q + P)),
                                       both((kt_hi, kt_lo), ALLP, j % 2, b, ALLP), True, True)
                        last.then_inc(A.score, 1)

                    def out(o):
                        pair, b = divmod(o, B)
                        pe.wait_ge(A.acc, it * OUTS + max(0, o - 1) + SEED)
                        pe.wait_ge(A.cx_lo, first + (2 * pair + 1) * B + b + 1 + SEED)
                        if b == 0:
                            pe.wait_ge(w_lo_ready, g * UNITS + (O_UNIT[pair] + 1))
                        for q in range(QC):
                            t = QC * b + q
                            for k in range(2):
                                o_col = O_COL + (2 * pair + k) * D
                                last = mm3(ps_out[:, o % 2, q * D:(q + 1) * D],
                                           both((cx_hi, cx_lo), ALLP, k, slice(t * P, (t + 1) * P)),
                                           both(W, ALLP, slice(o_col, o_col + D)), k == 0, k == 1)
                        last.then_inc(A.out, 1)

                    def context(m):
                        j, b = divmod(m, B)
                        if j == 0:
                            pe.wait_ge(A.v_lo, it * NT + QC * b + QC + SEED)
                        pe.wait_ge(A.pt_lo, first + m + 1 + SEED)
                        pe.wait_ge(A.cx_lo, first + m + SEED)
                        for kc in range(QC):
                            last = mm3(ps_ctx[:, 0:S],
                                       both((v_hi, v_lo), ALLP, QC * b + kc, slice(j * HD1, (j + 1) * HD1)),
                                       both((pt_hi, pt_lo), ALLP, m % 2, slice(kc * S, (kc + 1) * S)),
                                       kc == 0, kc == QC - 1)
                        last.then_inc(A.pv, 1)

                    for t in range(AHEAD):
                        if t in SCORES_AT:
                            scores(SCORES_AT[t])
                        tile(t)
                    for n in range(ITEMS + 1):
                        if n < ITEMS:
                            transposes(A, n, first)
                        if AHEAD + n < NTILE:
                            tile(AHEAD + n)
                        if n + 2 < ITEMS:
                            scores(n + 2)
                        if n > 0:
                            context(n - 1)
                        for o in OUT_AT.get(n, ()):
                            out(o)

            attention1(ATT["1a"], ROUND_L1A, LN[2])
            pe.wait_ge(ATT["1a"].kq_lo, NGROUP * NKQ + SEED)
            layer_norm(3)
            attention1(ATT["1b"], ROUND_L1B, LN[3])
            pe.wait_ge(ATT["1b"].kq_lo, NGROUP * NKQ + SEED)
            layer_norm(4)
            ffn(1, ROUND_FFN1, LN[4])


def _pack_attention(np, wq, wk, wv, wo):
    rounds = []
    for g in range(wq.shape[1] // UNIT):
        cut = slice(g * UNIT, (g + 1) * UNIT)
        k, q, v = (w[:, cut].reshape(DC, P, UNIT).transpose(1, 0, 2) for w in (wk, wq, wv))
        o = wo[cut].reshape(GROUP, P, D).transpose(1, 0, 2)
        kq = [np.concatenate([w[:, :, j * P:(j + 1) * P].reshape(P, DC * P) for w in (k, q)], axis=1)
              for j in range(GROUP)]
        out = [o[:, 2 * r:2 * r + 2].reshape(P, UNIT) for r in range(2)]
        rounds.append(np.concatenate([kq[0], v[:, 0], v[:, 1], kq[1], kq[2], out[0], kq[3], out[1]], axis=1))
    return rounds


def _pack_mlp(np, w1, w2):
    first = w1.reshape(DC, P, F // P, P).transpose(1, 2, 0, 3).reshape(P, -1)
    second = w2.reshape(F // P, P, D).transpose(1, 0, 2).reshape(P, -1)
    return [np.concatenate([first, second], axis=1)]


def _slots(np, w, axis):
    shape = list(w.shape)
    shape[axis:axis + 1] = [H, HD0]
    padded = list(shape)
    padded[axis + 1] = SLOT
    out = np.zeros(padded, w.dtype)
    out[tuple([slice(None)] * (axis + 1) + [slice(0, HD0)])] = w.reshape(shape)
    final = list(w.shape)
    final[axis] = H * SLOT
    return out.reshape(final)


def kernel(**inputs):
    import numpy as np
    import concourse.bacc as bacc
    from concourse.bass_utils import run_bass_kernel_spmd

    a = {k: np.asarray(v) for k, v in inputs.items()}
    l0 = {k[len("L0_xattn_"):]: v for k, v in a.items() if k.startswith("L0_xattn_")}
    l1 = {k[len("L1_xattn_"):]: v for k, v in a.items() if k.startswith("L1_xattn_")}

    rounds = _pack_attention(np, _slots(np, l0["q_w"], 1), _slots(np, l0["k_w"], 1),
                             _slots(np, l0["v_w"], 1), _slots(np, l0["cproj_w"], 0))
    rounds += _pack_mlp(np, l0["fc_w"], l0["proj_w"])
    for n in "12":
        rounds += _pack_attention(np, l1["wq" + n], l1["wk" + n], l1["wv" + n], l1["wo" + n])
    rounds += _pack_mlp(np, l1["w_fc1"], l1["w_fc2"])
    weights = np.stack(rounds)

    q0 = _slots(np, l0["q_b"], 0).reshape(NGROUP, GROUP, SLOT)
    q0[:, :, HD0] = math.sqrt(HD0)
    vectors = [q0, _slots(np, l0["k_b"], 0), _slots(np, l0["v_b"], 0), l0["ln1_w"], l0["ln1_b"],
               l0["ln2_w"], l0["ln2_b"], l1["ln1_scale"], l1["ln1_offset"], l1["ln2_scale"], l1["ln2_offset"],
               l1["ln_mlp_scale"], l1["ln_mlp_offset"], l0["fc_b"], l1["b_fc1"]]
    for n in "12":
        vectors += [l1["bq" + n], l1["bk" + n], l1["bias_k" + n], l1["bias_v" + n]]
    cols = np.concatenate([v.reshape(-1, P) for v in vectors]).T
    rows = np.stack([l0["cproj_b"], l0["proj_b"], l1["bo1"], l1["bo2"], l1["b_fc2"]])
    vrows = np.stack([v.reshape(-1) for n in "12" for v in (l1["bv" + n], l1["bias_v" + n])])

    arrays = {"x": a["x"].reshape(NTOK, D), "ctxt": a["ctx_2048"].reshape(NTOK, D).T,
              "mask": a["mask_BxS2_bf1"].reshape(1, NTOK).view(np.uint8), "ident": np.eye(P, dtype=np.float32),
              "weights": weights, "cols": cols, "rows": rows, "vrows": vrows}
    arrays = {"in_" + k: np.ascontiguousarray(v) for k, v in arrays.items()}
    nc = bacc.Bacc("TRN2", target_bir_lowering=False, num_devices=1)
    d = {k[3:]: nc.dram_tensor(k, v.shape, mybir.dt.from_np(v.dtype), kind="ExternalInput").ap()
         for k, v in arrays.items()}
    out = nc.dram_tensor("out", (NTOK, D), mybir.dt.float32, kind="ExternalOutput").ap()
    xattn_kernel(nc, d["x"].rearrange("(t p) d -> p t d", p=P), d["ctxt"].rearrange("(c p) t -> p c t", p=P),
                 d["mask"], d["ident"], d["weights"], d["cols"], d["rows"], d["vrows"],
                 out.rearrange("(t p) d -> p t d", p=P))
    r = run_bass_kernel_spmd(nc, [arrays], core_ids=[0])
    return r.results[0]["out"].reshape(B, S, D)
```

```python
import math
from contextlib import ExitStack

import concourse.bass as bass
from concourse import mybir

P = 128
B, S, D = 4, 256, 256
H = 16
HD0, HD1 = D // H, 128
F = 1024
NTOK = B * S
NT = NTOK // P
DC = D // P
HALF = NTOK // 2
QC = S // P
EPS = 1e-5
SLOT = 32
GROUP = 4
NGROUP = H // GROUP
KEYS1 = S + 1
KEYS1_EVEN = KEYS1 + 1
LIVE = 3
MASKED = -3.0e38

UNIT, UNITS = 512, 8
KQ_COL = [j * UNIT for j in range(GROUP)]
V_COL = GROUP * UNIT
O_COL = V_COL + 2 * UNIT
WCOLS = UNITS * UNIT
UNIT_COL = [KQ_COL[0], V_COL, V_COL + UNIT, KQ_COL[1], KQ_COL[2], O_COL, KQ_COL[3], O_COL + UNIT]
KQ_UNIT = [0, 3, 4, 6]
V_UNIT_LAST = 2
O_UNIT = [5, 7]
RING = 4
FFN1_COL = [UNIT_COL[f // 2] + f % 2 * (UNIT // 2) for f in range(F // P)]
FFN2_COL = [UNIT_COL[UNITS // 2 + f // 2] + f % 2 * (UNIT // 2) for f in range(F // P)]
ROUND_L0, ROUND_FFN0, ROUND_L1A, ROUND_L1B, ROUND_FFN1, ROUNDS = 0, 1, 2, 6, 10, 11

_COLS = {}
_n = 0
for _name, _w in [("q0", NGROUP), ("k0", NGROUP), ("v0", NGROUP), ("ln0a_w", DC), ("ln0a_b", DC),
                  ("ln0b_w", DC), ("ln0b_b", DC), ("ln1a_w", DC), ("ln1a_b", DC), ("ln1b_w", DC),
                  ("ln1b_b", DC), ("ln1c_w", DC), ("ln1c_b", DC), ("fc0", F // P), ("fc1", F // P),
                  ("q1a", H), ("k1a", H), ("bk1a", H), ("bv1a", H),
                  ("q1b", H), ("k1b", H), ("bk1b", H), ("bv1b", H)]:
    _COLS[_name] = (_n, _w)
    _n += _w
NCOLS = _n


def xattn_kernel(nc, x_d, ctxt_d, mask_d, ident_d, weights_d, cols_d, rows_d, vrows_d, out_d):
    f32, f32r, bf16, u8 = mybir.dt.float32, mybir.dt.float32r, mybir.dt.bfloat16, mybir.dt.uint8
    ALU, ACT, AX = mybir.AluOpType, mybir.ActivationFunctionType, mybir.AxisListType
    ds = bass.ds

    with ExitStack() as ctx:
        def sem(name):
            return ctx.enter_context(nc.semaphore(name))

        def pb(name, shape):
            return ctx.enter_context(nc.psum_tensor(name, shape, f32))

        def sb(name, shape, dt=f32):
            return ctx.enter_context(nc.sbuf_tensor(name, shape, dt))

        x_sb = sb("x_sb", [P, NT, D])
        ht_hi, ht_lo = sb("ht_hi", [P, DC, NTOK], f32r), sb("ht_lo", [P, DC, NTOK], f32r)
        ct_hi, ct_lo = sb("ct_hi", [P, DC, NTOK], f32r), sb("ct_lo", [P, DC, NTOK], f32r)
        w_hi, w_lo = sb("w_hi", [P, WCOLS], f32r), sb("w_lo", [P, WCOLS], f32r)
        w_raw = sb("w_raw", [P, RING, UNIT])
        cols = sb("cols", [P, NCOLS])
        rows = sb("rows", [P, 5, D])
        ident = sb("ident", [P, P])
        xn = sb("xn", [P, NT, D])
        tmp = sb("tmp", [P, 2, HALF])
        vrow = sb("vrow", [P, 2, H * HD1 // 2])
        probs = sb("probs", [P, LIVE, QC, KEYS1_EVEN])
        nmax, sums, rden = sb("nmax", [P, LIVE, QC]), sb("sums", [P, LIVE, QC]), sb("rden", [P, LIVE, QC])
        stats = sb("stats", [P, NT, 6])
        mv = sb("mv", [P, NT, 2])
        half_pow, rstd, vare = sb("half_pow", [P, NT]), sb("rstd", [P, NT]), sb("vare", [P, NT])

        base = nc.sbuf_base
        base = (base + 63) // 64 * 64
        KB = 1024

        def at(name, off, shape, dt=f32):
            return nc.alloc_sbuf_tensor_at(name, shape, dt, offset=base + off)

        kt_hi = at("kt_hi", 0, [P, 2, B, KEYS1_EVEN], f32r)
        kt_lo = at("kt_lo", 9 * KB, [P, 2, B, KEYS1_EVEN], f32r)
        v_hi, v_lo = at("v_hi", 18 * KB, [P, NT, UNIT], f32r), at("v_lo", 34 * KB, [P, NT, UNIT], f32r)
        qt_hi, qt_lo = at("qt_hi", 50 * KB, [P, 2, NTOK], f32r), at("qt_lo", 58 * KB, [P, 2, NTOK], f32r)
        cx_hi, cx_lo = at("cx_hi", 66 * KB, [P, 2, NTOK], f32r), at("cx_lo", 74 * KB, [P, 2, NTOK], f32r)
        pt_hi, pt_lo = at("pt_hi", 82 * KB, [P, 2, QC * S], f32r), at("pt_lo", 86 * KB, [P, 2, QC * S], f32r)
        v0_all = at("v0_all", 0, [P, NT, UNIT], f32r)
        v0_now = at("v0_now", 16 * KB, [P, NT, GROUP, P], f32r)
        q0_hi, q0_lo = at("q0_hi", 32 * KB, [P, NTOK], f32r), at("q0_lo", 36 * KB, [P, NTOK], f32r)
        k0_hi, k0_lo = at("k0_hi", 40 * KB, [P, NTOK], f32r), at("k0_lo", 44 * KB, [P, NTOK], f32r)
        c0_hi, c0_lo = at("c0_hi", 60 * KB, [P, NTOK], f32r), at("c0_lo", 64 * KB, [P, NTOK], f32r)
        kq_hi, kq_lo = at("kq_hi", 68 * KB, [P, UNIT], f32r), at("kq_lo", 70 * KB, [P, UNIT], f32r)
        p0_hi, p0_lo = at("p0_hi", 72 * KB, [P, 2, QC * S], f32r), at("p0_lo", 76 * KB, [P, 2, QC * S], f32r)
        vtmp = at("vtmp", 82 * KB, [P, H * HD1])
        mask_raw = at("mask_raw", 48 * KB, [1, NTOK], u8)
        mask_slot = at("mask_slot", 49 * KB, [1, P], bf16)
        mask_row = at("mask_row", 58 * KB, [1, NTOK], bf16)
        g_hi, g_lo = at("g_hi", 50 * KB, [P, F // P, HALF], f32r), at("g_lo", 66 * KB, [P, F // P, HALF], f32r)
        ct_raw = at("ct_raw", 50 * KB, [P, DC, NTOK])

        ps_proj = pb("ps_proj", [P, 2, 512])
        ps_score = pb("ps_score", [P, 2, QC, 512])
        ps_trans = pb("ps_trans", [P, 512])
        ps_ctx = pb("ps_ctx", [P, 512])

        def col(name, k=0):
            n, w = _COLS[name]
            return cols[:, n + k:n + k + 1]

        def col_at(name, k):
            return cols[:, ds(k + _COLS[name][0], 1)]

        x_loaded, ct_loaded, cols_loaded = sem("x_loaded"), sem("ct_loaded"), sem("cols_loaded")
        rows_loaded, ident_loaded, mask_loaded = sem("rows_loaded"), sem("ident_loaded"), sem("mask_loaded")
        vrow_loaded, vrow_ready, out_stored = sem("vrow_loaded"), sem("vrow_ready"), sem("out_stored")
        raw_loaded = [sem(f"raw_loaded{r}") for r in range(RING)]
        w_hi_ready, w_lo_ready = sem("w_hi_ready"), sem("w_lo_ready")
        consts_ready, cols_scaled, mask_ready = sem("consts_ready"), sem("cols_scaled"), sem("mask_ready")
        waited, slots_cleared = sem("waited"), sem("slots_cleared")
        ct_hi_ready, ct_lo_ready = sem("ct_hi_ready"), sem("ct_lo_ready")

        class NormSems:
            def __init__(self, stage):
                self.stats, self.pool, self.rstd = sem(f"ln{stage}_stats"), sem(f"ln{stage}_pool"), sem(f"ln{stage}_rstd")
                self.norm, self.turned, self.h32 = sem(f"ln{stage}_norm"), sem(f"ln{stage}_turned"), sem(f"ln{stage}_h32")
                self.hi, self.lo, self.biased = sem(f"ln{stage}_hi"), sem(f"ln{stage}_lo"), sem(f"ln{stage}_biased")

        class AttentionSems:
            def __init__(self, stage):
                self.proj, self.kq_hi, self.kq_lo = sem(f"att{stage}_proj"), sem(f"att{stage}_kq_hi"), sem(f"att{stage}_kq_lo")
                self.v32, self.v_hi, self.v_lo = sem(f"att{stage}_v32"), sem(f"att{stage}_v_hi"), sem(f"att{stage}_v_lo")
                self.learned, self.score, self.nmax = sem(f"att{stage}_learned"), sem(f"att{stage}_score"), sem(f"att{stage}_nmax")
                self.exp, self.rden, self.prob = sem(f"att{stage}_exp"), sem(f"att{stage}_rden"), sem(f"att{stage}_prob")
                self.turned, self.pt_hi, self.pt_lo = sem(f"att{stage}_turned"), sem(f"att{stage}_pt_hi"), sem(f"att{stage}_pt_lo")
                self.pv, self.cx_hi, self.cx_lo = sem(f"att{stage}_pv"), sem(f"att{stage}_cx_hi"), sem(f"att{stage}_cx_lo")
                self.out, self.acc, self.w_now = sem(f"att{stage}_out"), sem(f"att{stage}_acc"), sem(f"att{stage}_w_now")
                self.v_now = sem(f"att{stage}_v_now")

        class MlpSems:
            def __init__(self, stage):
                self.fc1, self.gelu, self.hi = sem(f"ffn{stage}_fc1"), sem(f"ffn{stage}_gelu"), sem(f"ffn{stage}_hi")
                self.lo, self.fc2, self.acc = sem(f"ffn{stage}_lo"), sem(f"ffn{stage}_fc2"), sem(f"ffn{stage}_acc")

        LN = {s: NormSems(s) for s in range(5)}
        ATT = {s: AttentionSems(s) for s in ("0", "1a", "1b")}
        SEED = 1
        FFN = {s: MlpSems(s) for s in (0, 1)}

        KQ_TILES = [(w, j, h) for j in range(GROUP) for h in range(2) for w in "kq"]
        TILES = (KQ_TILES[0:2] + [("v", t, 0) for t in range(4)] + KQ_TILES[2:4]
                 + [("v", t, 0) for t in range(4, NT)] + KQ_TILES[4:5])
        AHEAD = len(TILES)
        SCORES_AT = {3: 0, 4: 1}
        OUT_AT = {7: [0], 8: [1], 10: [2], 11: [3], 14: [4], 15: [5], 16: [6, 7]}
        NKQ, ITEMS, OUTS = len(KQ_TILES), GROUP * B, 2 * B
        SLOT_TILES = {}
        for n in range(ITEMS + 1):
            more = KQ_TILES[5 + n:6 + n] + [("o", o, 0) for o in OUT_AT.get(n, ())]
            SLOT_TILES[n] = list(range(len(TILES), len(TILES) + len(more)))
            TILES += more
        NTILE = len(TILES)
        DONE = {tile: k + 1 for k, tile in enumerate(TILES)}
        SPLIT_AT = {0: [1], 1: [2], 3: [3], 7: [4], 12: [5], 13: [6], 16: [7]}
        UNIT_READ = [("q", 0, 1), ("v", NT - 1, 0), ("v", NT - 1, 0), ("q", 1, 1), ("q", 2, 1), ("o", B - 1, 0),
                     ("q", 3, 1), ("o", OUTS - 1, 0)]

        def alone(engine):
            engine.sem_inc(waited, 1)

        block = ctx.enter_context(nc.Block())

        @block.sync
        def _(sp):
            for A in ATT.values():
                for started in (A.proj, A.kq_hi, A.kq_lo, A.v32, A.v_hi, A.v_lo, A.learned, A.score, A.nmax, A.exp,
                                A.rden, A.prob, A.turned, A.pt_hi, A.pt_lo, A.pv, A.cx_hi, A.cx_lo, A.out, A.acc,
                                A.w_now, A.v_now):
                    sp.sem_inc(started, SEED)
            sp.dma_start(x_sb[:, :, :], x_d).then_inc(x_loaded, 16)
            sp.dma_start(ident[:, :], ident_d).then_inc(ident_loaded, 16)
            sp.dma_start(cols[:, :], cols_d).then_inc(cols_loaded, 16)
            sp.dma_start(mask_raw[:, :], mask_d).then_inc(mask_loaded, 16)
            sp.dma_start(ct_raw[:, :, :], ctxt_d).then_inc(ct_loaded, 16)

            for u in range(RING):
                sp.dma_start(w_raw[:, u, :], weights_d[0, :, u * UNIT:(u + 1) * UNIT]).then_inc(raw_loaded[u], 16)
            sp.dma_start(rows[:, :, :], rows_d.partition_broadcast(P)).then_inc(rows_loaded, 16)
            for u in range(RING, UNITS):
                sp.wait_ge(w_lo_ready, u - RING + 1)
                sp.dma_start(w_raw[:, u - RING, :],
                             weights_d[0, :, u * UNIT:(u + 1) * UNIT]).then_inc(raw_loaded[u - RING], 16)
            with sp.Fori(1, ROUNDS) as g:
                for u in range(UNITS):
                    sp.wait_ge(w_lo_ready, g * UNITS + (u - RING + 1))
                    sp.dma_start(w_raw[:, u % RING, :],
                                 weights_d[ds(g, 1), :, u * UNIT:(u + 1) * UNIT]
                                 .rearrange("a p c -> (a p) c")).then_inc(raw_loaded[u % RING], 16)
            for t in range(2):
                sp.wait_ge(FFN[1].acc, 2 * (t + 1))
                sp.dma_start(out_d[:, 4 * t:4 * t + 4, :], x_sb[:, 4 * t:4 * t + 4, :]).then_inc(out_stored, 16)
            sp.wait_ge(out_stored, 32)

        @block.gpsimd
        def _(pool):
            def split_lo(g, u):
                c = UNIT_COL[u]
                pool.wait_ge(w_hi_ready, g * UNITS + u + 1)
                nc.gpsimd.tensor_tensor(w_lo[:, c:c + UNIT], w_raw[:, u % RING, :],
                                        w_hi[:, c:c + UNIT].bitcast(f32), ALU.subtract).then_inc(w_lo_ready, 1)

            def layer_norm(s, splits=()):
                L = LN[s]
                for half in range(2):
                    t0 = 4 * half
                    pool.wait_ge(L.stats, 8 * (half + 1))
                    nc.gpsimd.tensor_scalar(vare[:, t0:t0 + 4], mv[:, t0:t0 + 4, 1], EPS, 1.0,
                                            ALU.add, ALU.mult).then_inc(L.pool, 1)
                    pool.wait_ge(L.pool, half + 1)
                    nc.gpsimd.tensor_tensor(rstd[:, t0:t0 + 4], vare[:, t0:t0 + 4], half_pow[:, t0:t0 + 4],
                                            ALU.pow).then_inc(L.rstd, 1)
                for g, u in splits:
                    split_lo(g, u)
                pool.wait_ge(rows_loaded, 16)
                for t in range(NT):
                    pool.wait_ge(L.norm, t + 1)
                    nc.gpsimd.tensor_tensor(x_sb[:, t, :], x_sb[:, t, :], rows[:, s, :],
                                            ALU.add).then_inc(L.biased, 1)

            def normalise(A, n, first, width):
                pool.wait_ge(A.rden, first + n + 1 + SEED)
                alone(pool)
                for c in range(QC):
                    e = probs[:, n % LIVE, c, 0:width]
                    last = nc.gpsimd.tensor_scalar(e, e, rden[:, n % LIVE, c:c + 1], 1.0, ALU.mult, ALU.mult)
                last.then_inc(A.prob, 1)

            def value_rows(s):
                pool.wait_ge(vrow_loaded, 32 * (s + 1))
                for k in range(2):
                    w = H * HD1 // 2
                    nc.gpsimd.tensor_tensor(vrow[:, k, :], vrow[:, k, :], vtmp[:, k * w:(k + 1) * w],
                                            ALU.subtract).then_inc(vrow_ready, 1)

            def attention1(A, name, g0):
                def learned_key(g, it, j):
                    par = j % 2
                    bk = cols[:, ds((g - g0) * GROUP + (_COLS["bk" + name][0] + j), 1)].to_broadcast([P, B])
                    pool.wait_ge(A.score, it * ITEMS + max(0, 4 * (j - 1)) + SEED)
                    alone(pool)
                    nc.gpsimd.tensor_copy(kt_hi[:, par, :, S], bk).then_inc(A.learned, 1)
                    pool.wait_ge(A.learned, it * 2 * GROUP + 2 * j + 1 + SEED)
                    alone(pool)
                    nc.gpsimd.tensor_tensor(kt_lo[:, par, :, S], bk, kt_hi[:, par, :, S].bitcast(f32),
                                            ALU.subtract).then_inc(A.learned, 1)

                def v_lo_tile(it, t):
                    pool.wait_ge(A.v_hi, it * NT + t + 1 + SEED)
                    nc.gpsimd.tensor_tensor(v_lo[:, t, :], tmp[:, t % 2, :], v_hi[:, t, :].bitcast(f32),
                                            ALU.subtract).then_inc(A.v_lo, 1)

                with pool.Fori(g0, g0 + NGROUP) as g:
                    it = g - g0
                    learned_key(g, it, 0)
                    for t in range(NT):
                        if t == 3:
                            normalise(A, 0, it * ITEMS, S)
                        if t == 4:
                            split_lo(g + 1, 0)
                        v_lo_tile(it, t)
                    for n in range(ITEMS + 1):
                        j, b = divmod(n, B)
                        if n + 1 < ITEMS:
                            normalise(A, n + 1, it * ITEMS, S)
                        if b == 0 and j < GROUP - 1:
                            learned_key(g, it, j + 1)
                        for u in SPLIT_AT.get(n, ()):
                            split_lo(g + 1, u)

            nc.gpsimd.memset(half_pow[:, :], -0.5).then_inc(consts_ready, 1)
            nc.gpsimd.memset(v0_now[:, :, :, :].bitcast(f32), 0.0).then_inc(slots_cleared, 1)
            pool.wait_ge(consts_ready, 1)
            layer_norm(0, [(ROUND_L0, u) for u in range(UNITS)])
            value_rows(0)
            A = ATT["0"]
            with pool.Fori(0, NGROUP) as i:
                for n in range(ITEMS):
                    normalise(A, n, i * ITEMS, S)
            layer_norm(1, [(ROUND_FFN0, u) for u in range(UNITS)])
            for u in range(UNITS // 2):
                split_lo(ROUND_L1A, u)
            layer_norm(2, [(ROUND_L1A, u) for u in range(UNITS // 2, UNITS)])
            attention1(ATT["1a"], "1a", ROUND_L1A)
            layer_norm(3)
            value_rows(1)
            attention1(ATT["1b"], "1b", ROUND_L1B)
            layer_norm(4)


        @block.scalar
        def _(act):
            def split_hi(g, u):
                c = UNIT_COL[u]
                act.wait_ge(raw_loaded[u % RING], g * (16 * UNITS // RING) + 16 * (u // RING + 1))
                nc.scalar.activation(w_hi[:, c:c + UNIT], w_raw[:, u % RING, :], ACT.Copy).then_inc(w_hi_ready, 1)

            def layer_norm(s):
                L = LN[s]
                for e in range(4):
                    half, c = divmod(e, DC)
                    act.wait_ge(L.h32, e + 1)
                    nc.scalar.activation(ht_hi[:, c, half * HALF:(half + 1) * HALF], tmp[:, e % 2, :],
                                         ACT.Copy).then_inc(L.hi, 1)

            def exps(A, n, first, width):
                act.wait_ge(A.nmax, first + n + 1 + SEED)
                act.wait_ge(A.turned, first + max(0, n - LIVE + 1) + SEED)
                for c in range(QC):
                    last = nc.scalar.activation(probs[:, n % LIVE, c, 0:width], ps_score[:, n % 2, c, 0:width], ACT.Exp,
                                                bias=nmax[:, n % LIVE, c:c + 1],
                                                accum_out=sums[:, n % LIVE, c:c + 1])
                last.then_inc(A.exp, 1)

            def load_value_rows(s):
                act.dma_start(vrow[:, :, :].rearrange("p k w -> p (k w)"),
                              vrows_d[2 * s, :].partition_broadcast(P)).then_inc(vrow_loaded, 16)
                act.dma_start(vtmp[:, :], vrows_d[2 * s + 1, :].partition_broadcast(P)).then_inc(vrow_loaded, 16)

            for u in range(RING):
                split_hi(0, u)
            act.wait_ge(ct_loaded, 16)
            for c in range(DC):
                nc.scalar.activation(ct_hi[:, c, :], ct_raw[:, c, :], ACT.Copy).then_inc(ct_hi_ready, 1)
            load_value_rows(0)
            layer_norm(0)

            A = ATT["0"]
            for t in range(NT):
                act.wait_ge(A.proj, t + 1 + SEED)
                nc.scalar.activation(v0_all[:, t, :].rearrange("p (h e) -> p h e", h=H)[:, :, 0:HD0],
                                     ps_proj[:, t % 2, :].rearrange("p (h e) -> p h e", h=H)[:, :, 0:HD0],
                                     ACT.Copy).then_inc(A.v_hi, 1)
                if RING + t < UNITS:
                    split_hi(0, RING + t)
            act.wait_ge(cols_scaled, 5)
            act.wait_ge(w_hi_ready, UNITS)
            nc.scalar.activation(kq_hi[:, :], w_hi[:, 0:UNIT], ACT.Copy).then_inc(A.w_now, 1)
            with act.Fori(0, NGROUP) as i:
                first = i * ITEMS

                def proj(k, name, dst, half):
                    act.wait_ge(A.score, first + SEED)
                    act.wait_ge(A.proj, i * 4 + (NT + k + 1) + SEED)
                    alone(act)
                    nc.scalar.activation(dst[:, half * HALF:(half + 1) * HALF], ps_proj[:, k % 2, :], ACT.Identity,
                                         bias=col_at(name, i)).then_inc(A.kq_hi, 1)

                proj(0, "k0", k0_hi, 0)
                proj(1, "q0", q0_hi, 0)
                proj(2, "k0", k0_hi, 1)
                exps(A, 0, first, S)
                proj(3, "q0", q0_hi, 1)
                exps(A, 1, first, S)
                for n in range(ITEMS + 1):
                    b, j = divmod(n, GROUP)
                    if n + 2 < ITEMS:
                        exps(A, n + 2, first, S)
                    if n < ITEMS:
                        act.wait_ge(A.pv, first + max(0, n - 1) + SEED)
                        act.wait_ge(A.turned, first + n + 1 + SEED)
                        nc.scalar.activation(p0_hi[:, n % 2, :], ps_trans[:, :], ACT.Copy).then_inc(A.pt_hi, 1)
                    if j == 0 and b > 0:
                        act.wait_ge(A.out, i * B + (b - 1) + SEED)
                        act.wait_ge(A.pv, first + n + SEED)
                        alone(act)
                        nc.scalar.activation(c0_hi[:, (b - 1) * S:b * S], ps_ctx[:, 0:S], ACT.Identity,
                                             bias=col_at("v0", i)).then_inc(A.cx_hi, 1)
                    if n == ITEMS // 2:
                        act.wait_ge(A.proj, i * 4 + (NT + 4) + SEED)
                        alone(act)
                        nc.scalar.activation(kq_hi[:, :], w_hi[:, ds(i * UNIT + UNIT, UNIT)], ACT.Copy)\
                            .then_inc(A.w_now, 1)
            act.wait_ge(A.w_now, 2 * (NGROUP + 1) + SEED)
            for u in range(UNITS):
                if u == UNITS // 2:
                    act.wait_ge(A.out, NGROUP * B + SEED)
                split_hi(ROUND_FFN0, u)
            layer_norm(1)

            def ffn(s, func, name, next_round):
                N = FFN[s]
                act.wait_ge(LN[1 if s == 0 else 4].lo, 4)
                for half in range(2):
                    for f in range(F // P):
                        k = half * (F // P) + f
                        act.wait_ge(N.fc1, k + 1)
                        if k >= 2:
                            act.wait_ge(N.lo, k - 1)
                        nc.scalar.activation(tmp[:, k % 2, :], ps_proj[:, k % 2, :], func,
                                             bias=col(name, f)).then_inc(N.gelu, 1)
                if next_round is not None:
                    act.wait_ge(N.fc1, 2 * F // P)
                    for u in range(UNITS):
                        if u == UNITS // 2:
                            act.wait_ge(N.fc2, 4)
                        split_hi(next_round, u)

            ffn(0, ACT.Gelu_apprx_tanh, "fc0", ROUND_L1A)
            layer_norm(2)

            def attention1(A, name, g0):
                with act.Fori(g0, g0 + NGROUP) as g:
                    it = g - g0
                    first = it * ITEMS

                    def kq_tile(t):
                        w, j, half = TILES[t]
                        act.wait_ge(A.score, first + max(0, 4 * (j - 1)) + SEED)
                        act.wait_ge(A.proj, it * NTILE + (t + 1) + SEED)
                        alone(act)
                        bias = cols[:, ds(it * GROUP + (_COLS[w + name][0] + j), 1)]
                        if w == "k":
                            out = kt_hi[:, j % 2, 2 * half:2 * half + 2, 0:S]
                            src = ps_proj[:, t % 2, :].rearrange("p (b k) -> p b k", b=2)
                        else:
                            out = qt_hi[:, j % 2, half * HALF:(half + 1) * HALF]
                            src = ps_proj[:, t % 2, :]
                        nc.scalar.activation(out, src, ACT.Identity, bias=bias).then_inc(A.kq_hi, 1)

                    def v_tile(t):
                        act.wait_ge(A.v32, it * NT + t + 1 + SEED)
                        nc.scalar.activation(v_hi[:, t, :], tmp[:, t % 2, :], ACT.Copy).then_inc(A.v_hi, 1)

                    def context(m):
                        j, b = divmod(m, B)
                        if j < 2:
                            act.wait_ge(A.proj, it * NTILE + SEED)
                        else:
                            act.wait_ge(A.proj, it * NTILE + DONE[("o", b, 0)] + SEED)
                        act.wait_ge(A.pv, first + m + 1 + SEED)
                        alone(act)
                        nc.scalar.activation(cx_hi[:, j % 2, b * S:(b + 1) * S], ps_ctx[:, 0:S], ACT.Identity,
                                             bias=cols[:, ds(it * GROUP + (_COLS["bv" + name][0] + j), 1)])\
                            .then_inc(A.cx_hi, 1)

                    for t in range(AHEAD):
                        if t - 1 in SCORES_AT and SCORES_AT[t - 1] == 0:
                            exps(A, 0, first, KEYS1)
                        if TILES[t][0] == "v":
                            v_tile(TILES[t][1])
                        else:
                            kq_tile(t)
                        if TILES[t] == UNIT_READ[0]:
                            act.wait_ge(A.proj, it * NTILE + (t + 1) + SEED)
                            split_hi(g + 1, 0)
                    for n in range(ITEMS + 1):
                        if n + 1 < ITEMS:
                            exps(A, n + 1, first, KEYS1)
                        if n < ITEMS:
                            act.wait_ge(A.pv, first + max(0, n - 1) + SEED)
                            act.wait_ge(A.turned, first + n + 1 + SEED)
                            nc.scalar.activation(pt_hi[:, n % 2, :], ps_trans[:, :], ACT.Copy).then_inc(A.pt_hi, 1)
                        for t in SLOT_TILES[n]:
                            if TILES[t][0] != "o":
                                kq_tile(t)
                        if n > 0:
                            context(n - 1)
                        for u in SPLIT_AT.get(n, ()):
                            act.wait_ge(A.proj, it * NTILE + DONE[UNIT_READ[u]] + SEED)
                            split_hi(g + 1, u)

            attention1(ATT["1a"], "1a", ROUND_L1A)
            act.wait_ge(ATT["1a"].pv, NGROUP * ITEMS + SEED)
            act.wait_ge(ATT["1a"].v32, NGROUP * NT + SEED)
            load_value_rows(1)
            layer_norm(3)
            attention1(ATT["1b"], "1b", ROUND_L1B)
            layer_norm(4)
            ffn(1, ACT.Gelu, "fc1", None)

        @block.vector
        def _(dve):
            def split_context():
                for c in range(DC):
                    dve.wait_ge(ct_hi_ready, c + 1)
                    nc.vector.tensor_tensor(ct_lo[:, c, :], ct_raw[:, c, :], ct_hi[:, c, :].bitcast(f32),
                                            ALU.subtract).then_inc(ct_lo_ready, 1)

            def layer_norm(s, w, b, ready):
                L = LN[s]
                for half in range(2):
                    for t in range(4 * half, 4 * half + 4):
                        ready(t)
                        nc.vector.bn_stats(stats[:, t, :], x_sb[:, t, :]).then_inc(L.stats, 1)
                    for t in range(4 * half, 4 * half + 4):
                        dve.wait_ge(L.stats, 8 * half + t - 4 * half + 1)
                        nc.vector.bn_aggr(mv[:, t, :], stats[:, t, :]).then_inc(L.stats, 1)
                if s == 0:
                    split_context()
                for half in range(2):
                    dve.wait_ge(L.stats, 8 * (half + 1))
                    dve.wait_ge(L.rstd, half + 1)
                    for t in range(4 * half, 4 * half + 4):
                        nc.vector.tensor_scalar(xn[:, t, :], x_sb[:, t, :], mv[:, t, 0:1], rstd[:, t:t + 1],
                                                ALU.subtract, ALU.mult).then_inc(L.norm, 1)
                dve.wait_ge(cols_scaled, 5)

                def scaled(e):
                    half, c = divmod(e, DC)
                    if e >= 2:
                        dve.wait_ge(L.lo, e - 1)
                    dve.wait_ge(L.turned, e + 1)
                    nc.vector.tensor_scalar(tmp[:, e % 2, :], ps_proj[:, e % 2, :], col(w, c), col(b, c),
                                            ALU.mult, ALU.add).then_inc(L.h32, 1)

                def low(e):
                    half, c = divmod(e, DC)
                    tok = slice(half * HALF, (half + 1) * HALF)
                    dve.wait_ge(L.hi, e + 1)
                    nc.vector.tensor_tensor(ht_lo[:, c, tok], tmp[:, e % 2, :], ht_hi[:, c, tok].bitcast(f32),
                                            ALU.subtract).then_inc(L.lo, 1)

                scaled(0)
                scaled(1)
                low(0)
                scaled(2)
                low(1)
                scaled(3)
                low(2)
                low(3)

            def negmax(A, n, first, width):
                dve.wait_ge(A.score, first + n + 1 + SEED)
                nc.vector.tensor_reduce(nmax[:, n % LIVE, :], ps_score[:, n % 2, :, 0:width], AX.X, ALU.max,
                                        negate=True)\
                    .then_inc(A.nmax, 1)

            def reciprocals(A, n, first):
                dve.wait_ge(A.exp, first + n + 1 + SEED)
                nc.vector.reciprocal(rden[:, n % LIVE, :], sums[:, n % LIVE, :]).then_inc(A.rden, 1)

            def accumulate(A, bank, t):
                nc.vector.tensor_tensor(x_sb[:, t:t + 2, :], x_sb[:, t:t + 2, :],
                                        ps_proj[:, bank, :].rearrange("p (t d) -> p t d", t=2), ALU.add)\
                    .then_inc(A.acc, 1)

            nc.vector.memset(mask_slot[:, :], 0.0).then_inc(consts_ready, 1)
            dve.wait_ge(consts_ready, 2)
            nc.vector.memset(mask_slot[:, :].rearrange("p (j w) -> p j w", w=SLOT)[:, :, HD0:HD0 + 1], 1.0)\
                .then_inc(consts_ready, 1)
            dve.wait_ge(mask_loaded, 16)
            nc.vector.tensor_scalar(mask_row[:, :], mask_raw[:, :], 1.0, -MASKED, ALU.subtract, ALU.mult)\
                .then_inc(mask_ready, 1)
            dve.wait_ge(cols_loaded, 16)
            s0, s1 = 1.0 / math.sqrt(HD0), 1.0 / math.sqrt(HD1)
            for names, f in ((("q0",), s0), (("ln0a_w", "ln0a_b"), s0),
                             (("ln1a_w", "ln1a_b", "ln1b_w", "ln1b_b"), s1), (("q1a",), s1), (("q1b",), s1)):
                lo = _COLS[names[0]][0]
                hi = sum(_COLS[names[-1]])
                last = nc.vector.tensor_scalar(cols[:, lo:hi], cols[:, lo:hi], f, None, ALU.mult)
                last.then_inc(cols_scaled, 1)
            layer_norm(0, "ln0a_w", "ln0a_b", lambda t: dve.wait_ge(x_loaded, 16))

            A = ATT["0"]
            for t in range(NT):
                dve.wait_ge(A.v_hi, t + 1 + SEED)
                slots = v0_all[:, t, :].rearrange("p (h e) -> p h e", h=H)
                nc.vector.tensor_tensor(slots[:, :, HD0:SLOT],
                                        ps_proj[:, t % 2, :].rearrange("p (h e) -> p h e", h=H)[:, :, HD0:SLOT],
                                        slots[:, :, 0:HD0].bitcast(f32), ALU.subtract).then_inc(A.v_lo, 1)
            dve.wait_ge(A.v_lo, NT + SEED)
            dve.wait_ge(slots_cleared, 1)
            dve.wait_ge(w_lo_ready, UNITS)
            nc.vector.tensor_copy(kq_lo[:, :], w_lo[:, 0:UNIT].bitcast(f32)).then_inc(A.w_now, 1)
            with dve.Fori(0, NGROUP) as i:
                first = i * ITEMS

                def proj(k, name, hi, lo, half):
                    dve.wait_ge(A.kq_hi, i * 4 + (k + 1) + SEED)
                    tok = slice(half * HALF, (half + 1) * HALF)
                    nc.vector.scalar_tensor_tensor(out=lo[:, tok], in0=ps_proj[:, k % 2, :], scalar=col_at(name, i),
                                                   in1=hi[:, tok].bitcast(f32), op0=ALU.add, op1=ALU.subtract)\
                        .then_inc(A.kq_lo, 1)

                dve.wait_ge(A.pv, first + SEED)
                for j in range(GROUP):
                    last = nc.vector.tensor_copy(v0_now[:, :, j, j * SLOT:(j + 1) * SLOT],
                                                 v0_all[:, :, ds(i * P + j * SLOT, SLOT)].bitcast(f32))
                last.then_inc(A.v_now, 1)
                proj(0, "k0", k0_hi, k0_lo, 0)
                proj(1, "q0", q0_hi, q0_lo, 0)
                proj(2, "k0", k0_hi, k0_lo, 1)
                negmax(A, 0, first, S)
                negmax(A, 1, first, S)
                proj(3, "q0", q0_hi, q0_lo, 1)
                reciprocals(A, 0, first)
                negmax(A, 2, first, S)
                reciprocals(A, 1, first)
                for n in range(ITEMS + 2):
                    b, j = divmod(n, GROUP)
                    if n + 2 < ITEMS:
                        reciprocals(A, n + 2, first)
                    if n + 3 < ITEMS:
                        negmax(A, n + 3, first, S)
                    if n < ITEMS:
                        dve.wait_ge(A.pt_hi, first + n + 1 + SEED)
                        nc.vector.tensor_tensor(p0_lo[:, n % 2, :], ps_trans[:, :], p0_hi[:, n % 2, :].bitcast(f32),
                                                ALU.subtract).then_inc(A.pt_lo, 1)
                    if j == 0 and b > 0:
                        tok = slice((b - 1) * S, b * S)
                        dve.wait_ge(A.cx_hi, i * B + b + SEED)
                        nc.vector.scalar_tensor_tensor(out=c0_lo[:, tok], in0=ps_ctx[:, 0:S], scalar=col_at("v0", i),
                                                       in1=c0_hi[:, tok].bitcast(f32),
                                                       op0=ALU.add, op1=ALU.subtract).then_inc(A.cx_lo, 1)
                    if n == ITEMS // 2:
                        dve.wait_ge(A.proj, i * 4 + (NT + 4) + SEED)
                        nc.vector.tensor_copy(kq_lo[:, :], w_lo[:, ds(i * UNIT + UNIT, UNIT)].bitcast(f32))\
                            .then_inc(A.w_now, 1)
                    if j == 1 and b > 0:
                        if b == 1:
                            dve.wait_ge(LN[0].biased, NT)
                        dve.wait_ge(A.acc, i * B + SEED)
                        dve.wait_ge(A.out, i * B + b + SEED)
                        accumulate(A, (b - 1) % 2, 2 * (b - 1))

            layer_norm(1, "ln0b_w", "ln0b_b", lambda t: dve.wait_ge(ATT["0"].acc, NGROUP * B - 3 + t // 2 + SEED))

            def ffn(s):
                N = FFN[s]
                nf = F // P
                dve.wait_ge(LN[1 if s == 0 else 4].biased, NT)
                for half in range(2):
                    for f in range(nf):
                        k = half * nf + f
                        if half:
                            dve.wait_ge(N.fc2, 2)
                        dve.wait_ge(N.gelu, k + 1)
                        nc.vector.tensor_copy(g_hi[:, f, :], tmp[:, k % 2, :]).then_inc(N.hi, 1)
                        dve.wait_ge(N.hi, k + 1)
                        nc.vector.tensor_tensor(g_lo[:, f, :], tmp[:, k % 2, :], g_hi[:, f, :].bitcast(f32),
                                                ALU.subtract).then_inc(N.lo, 1)
                    for r in range(2):
                        k, t = 2 * half + r, 4 * half + 2 * r
                        dve.wait_ge(N.fc2, k + 1)
                        nc.vector.tensor_tensor(x_sb[:, t:t + 2, :], x_sb[:, t:t + 2, :],
                                                ps_score[:, half, r, :].rearrange("p (t d) -> p t d", t=2), ALU.add)\
                            .then_inc(N.acc, 1)

            ffn(0)
            for part in (kt_hi, kt_lo):
                nc.vector.memset(part[:, :, :, KEYS1:KEYS1_EVEN].bitcast(f32), 0.0).then_inc(consts_ready, 1)
            layer_norm(2, "ln1a_w", "ln1a_b", lambda t: dve.wait_ge(FFN[0].acc, t // 2 + 1))

            def attention1(A, name, g0, s):
                dve.wait_ge(vrow_ready, 2 * (s + 1))
                dve.wait_ge(LN[2 + s].biased, NT)
                with dve.Fori(g0, g0 + NGROUP) as g:
                    it = g - g0
                    first = it * ITEMS
                    vr = vrow[:, :, :].rearrange("p k w -> p (k w)")

                    def kq_tile(t):
                        w, j, half = TILES[t]
                        dve.wait_ge(A.kq_hi, it * NKQ + KQ_TILES.index(TILES[t]) + 1 + SEED)
                        bias = cols[:, ds(it * GROUP + (_COLS[w + name][0] + j), 1)]
                        if w == "k":
                            out = kt_lo[:, j % 2, 2 * half:2 * half + 2, 0:S]
                            hi = kt_hi[:, j % 2, 2 * half:2 * half + 2, 0:S]
                            src = ps_proj[:, t % 2, :].rearrange("p (b k) -> p b k", b=2)
                        else:
                            out = qt_lo[:, j % 2, half * HALF:(half + 1) * HALF]
                            hi = qt_hi[:, j % 2, half * HALF:(half + 1) * HALF]
                            src = ps_proj[:, t % 2, :]
                        nc.vector.scalar_tensor_tensor(out=out, in0=src, scalar=bias, in1=hi.bitcast(f32),
                                                       op0=ALU.add, op1=ALU.subtract).then_inc(A.kq_lo, 1)

                    def v_tile(t):
                        dve.wait_ge(A.v_lo, it * NT + max(0, t - 1) + SEED)
                        dve.wait_ge(A.proj, it * NTILE + TILES.index(("v", t, 0)) + 1 + SEED)
                        nc.vector.tensor_tensor(tmp[:, t % 2, :], ps_proj[:, t % 2, :],
                                                vr[:, ds(it * UNIT, UNIT)], ALU.add).then_inc(A.v32, 1)

                    def context(m):
                        j, b = divmod(m, B)
                        dve.wait_ge(A.cx_hi, first + m + 1 + SEED)
                        nc.vector.scalar_tensor_tensor(out=cx_lo[:, j % 2, b * S:(b + 1) * S], in0=ps_ctx[:, 0:S],
                                                       scalar=cols[:, ds(it * GROUP + (_COLS["bv" + name][0] + j), 1)],
                                                       in1=cx_hi[:, j % 2, b * S:(b + 1) * S].bitcast(f32),
                                                       op0=ALU.add, op1=ALU.subtract).then_inc(A.cx_lo, 1)

                    for t in range(AHEAD):
                        if t - 1 in SCORES_AT:
                            negmax(A, SCORES_AT[t - 1], first, KEYS1)
                        if TILES[t][0] == "v":
                            v_tile(TILES[t][1])
                        else:
                            kq_tile(t)
                        if t - 1 in SCORES_AT and SCORES_AT[t - 1] == 1:
                            reciprocals(A, 0, first)
                    for n in range(ITEMS + 1):
                        if n + 1 < ITEMS:
                            reciprocals(A, n + 1, first)
                        if n + 2 < ITEMS:
                            negmax(A, n + 2, first, KEYS1)
                        if n < ITEMS:
                            dve.wait_ge(A.pt_hi, first + n + 1 + SEED)
                            nc.vector.tensor_tensor(pt_lo[:, n % 2, :], ps_trans[:, :],
                                                    pt_hi[:, n % 2, :].bitcast(f32), ALU.subtract).then_inc(A.pt_lo, 1)
                        for t in SLOT_TILES[n]:
                            if TILES[t][0] != "o":
                                kq_tile(t)
                        if n > 0:
                            context(n - 1)
                        for t in SLOT_TILES[n]:
                            if TILES[t][0] == "o":
                                o = TILES[t][1]
                                dve.wait_ge(A.acc, it * OUTS + o // B * B + SEED)
                                dve.wait_ge(A.proj, it * NTILE + (t + 1) + SEED)
                                accumulate(A, t % 2, 2 * (o % B))

            attention1(ATT["1a"], "1a", ROUND_L1A, 0)
            layer_norm(3, "ln1b_w", "ln1b_b", lambda t: dve.wait_ge(ATT["1a"].acc, NGROUP * OUTS - 3 + t // 2 + SEED))
            attention1(ATT["1b"], "1b", ROUND_L1B, 1)
            layer_norm(4, "ln1c_w", "ln1c_b", lambda t: dve.wait_ge(ATT["1b"].acc, NGROUP * OUTS - 3 + t // 2 + SEED))
            ffn(1)

        @block.tensor
        def _(pe):
            def mm3(out, w, x, start, stop):
                (wh, wl), (xh, xl) = w, x
                pe.matmul(out, wl, xh, start=start, stop=False)
                pe.matmul(out, wh, xl, start=False, stop=False)
                return pe.matmul(out, wh, xh, start=False, stop=stop)

            def both(pair, *index):
                return pair[0][index], pair[1][index]

            W, HT, CT = (w_hi, w_lo), (ht_hi, ht_lo), (ct_hi, ct_lo)
            ALLP = slice(None)

            def layer_norm(s):
                L = LN[s]
                for e in range(4):
                    half, c = divmod(e, DC)
                    pe.wait_ge(L.norm, 4 * (half + 1))
                    if e >= 2:
                        pe.wait_ge(L.h32, e - 1)
                    for k in range(4):
                        last = pe.transpose(ps_proj[:, e % 2, k * P:(k + 1) * P],
                                            xn[:, 4 * half + k, c * P:(c + 1) * P], ident[:, :])
                    last.then_inc(L.turned, 1)

            def transposes(A, n, first):
                pe.wait_ge(A.prob, first + n + 1 + SEED)
                pe.wait_ge(A.pt_lo, first + n + SEED)
                for kc in range(QC):
                    for c in range(QC):
                        last = pe.transpose(ps_trans[:, kc * S + c * P:kc * S + (c + 1) * P],
                                            probs[:, n % LIVE, c, kc * P:(kc + 1) * P], ident[:, :])
                last.then_inc(A.turned, 1)

            pe.wait_ge(ident_loaded, 16)
            layer_norm(0)

            A = ATT["0"]
            pe.wait_ge(ct_lo_ready, DC)
            pe.wait_ge(w_lo_ready, V_UNIT_LAST + 1)
            pe.wait_ge(LN[0].h32, 4)
            for t in range(NT):
                if t >= 2:
                    pe.wait_ge(A.v_lo, t - 1 + SEED)
                for c in range(DC):
                    last = mm3(ps_proj[:, t % 2, :], both(CT, ALLP, c, slice(t * P, (t + 1) * P)),
                               both(W, ALLP, slice(V_COL + c * UNIT, V_COL + (c + 1) * UNIT)),
                               c == 0, c == DC - 1)
                last.then_inc(A.proj, 1)
            pe.wait_ge(LN[0].lo, 4)
            pe.wait_ge(A.v_lo, NT + SEED)
            pe.wait_ge(w_lo_ready, UNITS)
            pe.wait_ge(mask_ready, 1)
            pe.wait_ge(consts_ready, 3)
            with pe.Fori(0, NGROUP) as i:
                first = i * ITEMS

                def proj0(k, keys, half):
                    if k >= 2:
                        pe.wait_ge(A.kq_lo, i * 4 + (k - 1) + SEED)
                    else:
                        pe.wait_ge(A.acc, i * B + SEED)
                    tok = slice(half * HALF, (half + 1) * HALF)
                    for c in range(DC):
                        o = (0 if keys else D) + c * P
                        last = mm3(ps_proj[:, k % 2, :], (kq_hi[:, o:o + P], kq_lo[:, o:o + P]),
                                   both(CT if keys else HT, ALLP, c, tok), c == 0, not keys and c == DC - 1)
                    if keys:
                        last = pe.matmul(ps_proj[:, k % 2, :], mask_slot[:, :], mask_row[:, tok],
                                         start=False, stop=True)
                    last.then_inc(A.proj, 1)

                def scores(n):
                    b, j = divmod(n, GROUP)
                    rows_j = slice(j * SLOT, (j + 1) * SLOT)
                    pe.wait_ge(A.kq_lo, i * 4 + (2 if b < 2 else 4) + SEED)
                    pe.wait_ge(A.exp, first + max(0, n - 1) + SEED)
                    for c in range(QC):
                        q = b * S + c * P
                        last = mm3(ps_score[:, n % 2, c, 0:S], both((q0_hi, q0_lo), rows_j, slice(q, q + P)),
                                   both((k0_hi, k0_lo), rows_j, slice(b * S, (b + 1) * S)), True, True)
                    last.then_inc(A.score, 1)

                def out0(b):
                    k = i * B + b
                    if b < 2:
                        pe.wait_ge(A.kq_lo, i * 4 + 4 + SEED)
                    else:
                        pe.wait_ge(A.acc, i * B + (b - 1) + SEED)
                    pe.wait_ge(A.cx_lo, k + 1 + SEED)
                    for q in range(QC):
                        t = QC * b + q
                        last = mm3(ps_proj[:, b % 2, q * D:(q + 1) * D],
                                   (c0_hi[:, t * P:(t + 1) * P], c0_lo[:, t * P:(t + 1) * P]),
                                   both(W, ALLP, ds(i * D + O_COL, D)), True, True)
                    last.then_inc(A.out, 1)

                def context(m):
                    b, j = divmod(m, GROUP)
                    pe.wait_ge(A.pt_lo, first + m + 1 + SEED)
                    if j == 0:
                        pe.wait_ge(A.cx_lo, i * B + b + SEED)
                    for kc in range(QC):
                        for part in (p0_lo, p0_hi):
                            last = pe.matmul(ps_ctx[:, 0:S], v0_now[:, QC * b + kc, j, :],
                                             part[:, m % 2, kc * S:(kc + 1) * S],
                                             start=(j, kc) == (0, 0) and part is p0_lo,
                                             stop=(j, kc) == (GROUP - 1, QC - 1) and part is p0_hi)
                    last.then_inc(A.pv, 1)

                pe.wait_ge(A.w_now, i * 2 + 2 + SEED)
                proj0(0, True, 0)
                proj0(1, False, 0)
                proj0(2, True, 1)
                scores(0)
                scores(1)
                proj0(3, False, 1)
                scores(2)
                pe.wait_ge(A.v_now, i + 1 + SEED)
                for n in range(ITEMS + 2):
                    b, j = divmod(n, GROUP)
                    if n < ITEMS:
                        transposes(A, n, first)
                    if n + 3 < ITEMS:
                        scores(n + 3)
                    if 0 < n <= ITEMS:
                        context(n - 1)
                    if j == 1 and b > 0:
                        out0(b - 1)
            pe.wait_ge(A.kq_lo, NGROUP * 4 + SEED)

            layer_norm(1)

            def ffn(s, g, turned):
                N = FFN[s]
                nf = F // P
                pe.wait_ge(turned.lo, 4)
                for half in range(2):
                    tok = slice(half * HALF, (half + 1) * HALF)
                    for f in range(nf):
                        k = half * nf + f
                        if k >= 2:
                            pe.wait_ge(N.gelu, k - 1)
                        pe.wait_ge(w_lo_ready, g * UNITS + f // 2 + 1)
                        for c in range(DC):
                            o = FFN1_COL[f] + c * P
                            last = mm3(ps_proj[:, k % 2, :], both(W, ALLP, slice(o, o + P)),
                                       both(HT, ALLP, c, tok), c == 0, c == DC - 1)
                        last.then_inc(N.fc1, 1)
                    for r in range(2):
                        for q in range(2):
                            t = 2 * r + q
                            for f in range(nf):
                                if t == 0:
                                    pe.wait_ge(w_lo_ready, g * UNITS + (UNITS // 2 + f // 2 + 1))
                                    pe.wait_ge(N.lo, half * nf + f + 1)
                                o = FFN2_COL[f]
                                last = mm3(ps_score[:, half, r, q * D:(q + 1) * D],
                                           both((g_hi, g_lo), ALLP, f, slice(t * P, (t + 1) * P)),
                                           both(W, ALLP, slice(o, o + D)), f == 0, f == nf - 1)
                        last.then_inc(N.fc2, 1)

            ffn(0, ROUND_FFN0, LN[1])
            pe.wait_ge(FFN[0].gelu, 2 * F // P)
            layer_norm(2)

            def attention1(A, g0, turned):
                pe.wait_ge(turned.h32, 4)
                pe.wait_ge(consts_ready, 5)
                with pe.Fori(g0, g0 + NGROUP) as g:
                    it = g - g0
                    first = it * ITEMS

                    def tile(t):
                        w, j, half = TILES[t]
                        bank = ps_proj[:, t % 2, :]
                        if t < 2:
                            pe.wait_ge(A.acc, it * OUTS + SEED)
                        else:
                            before = TILES[t - 2]
                            if before[0] == "v":
                                pe.wait_ge(A.v32, it * NT + (before[1] + 1) + SEED)
                            elif before[0] == "o":
                                pe.wait_ge(A.acc, it * OUTS + (before[1] + 1) + SEED)
                            else:
                                pe.wait_ge(A.kq_lo, it * NKQ + (KQ_TILES.index(before) + 1) + SEED)
                        if w == "o":
                            pair, b = divmod(j, B)
                            pe.wait_ge(A.cx_lo, first + (2 * pair + 1) * B + b + 1 + SEED)
                            if b == 0:
                                pe.wait_ge(w_lo_ready, g * UNITS + (O_UNIT[pair] + 1))
                            for q in range(QC):
                                t0 = QC * b + q
                                for k in range(2):
                                    o_col = O_COL + (2 * pair + k) * D
                                    last = mm3(bank[:, q * D:(q + 1) * D],
                                               both((cx_hi, cx_lo), ALLP, k, slice(t0 * P, (t0 + 1) * P)),
                                               both(W, ALLP, slice(o_col, o_col + D)), k == 0, k == 1)
                            last.then_inc(A.proj, 1)
                            return
                        if w == "v":
                            if j == 0:
                                pe.wait_ge(w_lo_ready, g * UNITS + (V_UNIT_LAST + 1))
                            for c in range(DC):
                                last = mm3(ps_proj[:, t % 2, :], both(CT, ALLP, c, slice(j * P, (j + 1) * P)),
                                           both(W, ALLP, slice(V_COL + c * UNIT, V_COL + (c + 1) * UNIT)),
                                           c == 0, c == DC - 1)
                        else:
                            if w == "k" and half == 0:
                                pe.wait_ge(w_lo_ready, g * UNITS + (KQ_UNIT[j] + 1))
                            if w == "q" and j == 0:
                                pe.wait_ge(turned.lo, 2 * (half + 1))
                            tok = slice(half * HALF, (half + 1) * HALF)
                            for c in range(DC):
                                o = KQ_COL[j] + (0 if w == "k" else D) + c * P
                                last = mm3(ps_proj[:, t % 2, :], both(W, ALLP, slice(o, o + P)),
                                           both(CT if w == "k" else HT, ALLP, c, tok), c == 0, c == DC - 1)
                        last.then_inc(A.proj, 1)

                    def scores(n):
                        j, b = divmod(n, B)
                        need = max(KQ_TILES.index((w, j, b // 2)) for w in "kq") + 1
                        pe.wait_ge(A.kq_lo, it * NKQ + need + SEED)
                        if b == 0:
                            pe.wait_ge(A.learned, it * 2 * GROUP + 2 * j + 2 + SEED)
                        pe.wait_ge(A.exp, first + max(0, n - 1) + SEED)
                        for c in range(QC):
                            q = b * S + c * P
                            last = mm3(ps_score[:, n % 2, c, 0:KEYS1_EVEN], both((qt_hi, qt_lo), ALLP, j % 2, slice(q, q + P)),
                                       both((kt_hi, kt_lo), ALLP, j % 2, b, ALLP), True, True)
                        last.then_inc(A.score, 1)

                    def context(m):
                        j, b = divmod(m, B)
                        if j == 0:
                            pe.wait_ge(A.v_lo, it * NT + QC * b + QC + SEED)
                        pe.wait_ge(A.pt_lo, first + m + 1 + SEED)
                        pe.wait_ge(A.cx_lo, first + m + SEED)
                        for kc in range(QC):
                            last = mm3(ps_ctx[:, 0:S],
                                       both((v_hi, v_lo), ALLP, QC * b + kc, slice(j * HD1, (j + 1) * HD1)),
                                       both((pt_hi, pt_lo), ALLP, m % 2, slice(kc * S, (kc + 1) * S)),
                                       kc == 0, kc == QC - 1)
                        last.then_inc(A.pv, 1)

                    for t in range(AHEAD):
                        if t in SCORES_AT:
                            scores(SCORES_AT[t])
                        tile(t)
                    for n in range(ITEMS + 1):
                        if n < ITEMS:
                            transposes(A, n, first)
                        if n + 2 < ITEMS:
                            scores(n + 2)
                        for t in SLOT_TILES[n]:
                            if TILES[t][0] != "o":
                                tile(t)
                        if n > 0:
                            context(n - 1)
                        for t in SLOT_TILES[n]:
                            if TILES[t][0] == "o":
                                tile(t)

            attention1(ATT["1a"], ROUND_L1A, LN[2])
            pe.wait_ge(ATT["1a"].kq_lo, NGROUP * NKQ + SEED)
            layer_norm(3)
            attention1(ATT["1b"], ROUND_L1B, LN[3])
            pe.wait_ge(ATT["1b"].kq_lo, NGROUP * NKQ + SEED)
            layer_norm(4)
            ffn(1, ROUND_FFN1, LN[4])


def _pack_attention(np, wq, wk, wv, wo):
    rounds = []
    for g in range(wq.shape[1] // UNIT):
        cut = slice(g * UNIT, (g + 1) * UNIT)
        k, q, v = (w[:, cut].reshape(DC, P, UNIT).transpose(1, 0, 2) for w in (wk, wq, wv))
        o = wo[cut].reshape(GROUP, P, D).transpose(1, 0, 2)
        kq = [np.concatenate([w[:, :, j * P:(j + 1) * P].reshape(P, DC * P) for w in (k, q)], axis=1)
              for j in range(GROUP)]
        out = [o[:, 2 * r:2 * r + 2].reshape(P, UNIT) for r in range(2)]
        rounds.append(np.concatenate([kq[0], v[:, 0], v[:, 1], kq[1], kq[2], out[0], kq[3], out[1]], axis=1))
    return rounds


def _pack_mlp(np, w1, w2):
    first = w1.reshape(DC, P, F // P, P).transpose(1, 2, 0, 3).reshape(P, -1)
    second = w2.reshape(F // P, P, D).transpose(1, 0, 2).reshape(P, -1)
    return [np.concatenate([first, second], axis=1)]


def _slots(np, w, axis, twice=False):
    shape = list(w.shape)
    shape[axis:axis + 1] = [H, HD0]
    padded = list(shape)
    padded[axis + 1] = SLOT
    out = np.zeros(padded, w.dtype)
    for k in range(2 if twice else 1):
        out[tuple([slice(None)] * (axis + 1) + [slice(k * HD0, (k + 1) * HD0)])] = w.reshape(shape)
    final = list(w.shape)
    final[axis] = H * SLOT
    return out.reshape(final)


def kernel(**inputs):
    import numpy as np
    import concourse.bacc as bacc
    from concourse.bass_utils import run_bass_kernel_spmd

    a = {k: np.asarray(v) for k, v in inputs.items()}
    l0 = {k[len("L0_xattn_"):]: v for k, v in a.items() if k.startswith("L0_xattn_")}
    l1 = {k[len("L1_xattn_"):]: v for k, v in a.items() if k.startswith("L1_xattn_")}

    rounds = _pack_attention(np, _slots(np, l0["q_w"], 1), _slots(np, l0["k_w"], 1),
                             _slots(np, l0["v_w"], 1, True), _slots(np, l0["cproj_w"], 0, True))
    rounds += _pack_mlp(np, l0["fc_w"], l0["proj_w"])
    for n in "12":
        rounds += _pack_attention(np, l1["wq" + n], l1["wk" + n], l1["wv" + n], l1["wo" + n])
    rounds += _pack_mlp(np, l1["w_fc1"], l1["w_fc2"])
    weights = np.stack(rounds)

    q0 = _slots(np, l0["q_b"], 0).reshape(NGROUP, GROUP, SLOT)
    q0[:, :, HD0] = math.sqrt(HD0)
    vectors = [q0, _slots(np, l0["k_b"], 0), _slots(np, l0["v_b"], 0), l0["ln1_w"], l0["ln1_b"],
               l0["ln2_w"], l0["ln2_b"], l1["ln1_scale"], l1["ln1_offset"], l1["ln2_scale"], l1["ln2_offset"],
               l1["ln_mlp_scale"], l1["ln_mlp_offset"], l0["fc_b"], l1["b_fc1"]]
    for n in "12":
        vectors += [l1["bq" + n], l1["bk" + n], l1["bias_k" + n], l1["bias_v" + n]]
    cols = np.concatenate([v.reshape(-1, P) for v in vectors]).T
    rows = np.stack([l0["cproj_b"], l0["proj_b"], l1["bo1"], l1["bo2"], l1["b_fc2"]])
    vrows = np.stack([v.reshape(-1) for n in "12" for v in (l1["bv" + n], l1["bias_v" + n])])

    arrays = {"x": a["x"].reshape(NTOK, D), "ctxt": a["ctx_2048"].reshape(NTOK, D).T,
              "mask": a["mask_BxS2_bf1"].reshape(1, NTOK).view(np.uint8), "ident": np.eye(P, dtype=np.float32),
              "weights": weights, "cols": cols, "rows": rows, "vrows": vrows}
    arrays = {"in_" + k: np.ascontiguousarray(v) for k, v in arrays.items()}
    nc = bacc.Bacc("TRN2", target_bir_lowering=False, num_devices=1)
    d = {k[3:]: nc.dram_tensor(k, v.shape, mybir.dt.from_np(v.dtype), kind="ExternalInput").ap()
         for k, v in arrays.items()}
    out = nc.dram_tensor("out", (NTOK, D), mybir.dt.float32, kind="ExternalOutput").ap()
    xattn_kernel(nc, d["x"].rearrange("(t p) d -> p t d", p=P), d["ctxt"].rearrange("(c p) t -> p c t", p=P),
                 d["mask"], d["ident"], d["weights"], d["cols"], d["rows"], d["vrows"],
                 out.rearrange("(t p) d -> p t d", p=P))
    r = run_bass_kernel_spmd(nc, [arrays], core_ids=[0])
    return r.results[0]["out"].reshape(B, S, D)
```

```python
import math
from contextlib import ExitStack

import concourse.bass as bass
from concourse import mybir

P = 128
B, S, D = 4, 256, 256
H = 16
HD0, HD1 = D // H, 128
F = 1024
NTOK = B * S
NT = NTOK // P
DC = D // P
HALF = NTOK // 2
QC = S // P
EPS = 1e-5
SLOT = 32
GROUP = 4
NGROUP = H // GROUP
KEYS1 = S + 1
KEYS1_EVEN = KEYS1 + 1
LIVE = 4
MASKED = -3.0e38

UNIT, UNITS = 512, 8
KQ_COL = [j * UNIT for j in range(GROUP)]
V_COL = GROUP * UNIT
O_COL = V_COL + 2 * UNIT
WCOLS = UNITS * UNIT
UNIT_COL = [KQ_COL[0], V_COL, V_COL + UNIT, KQ_COL[1], KQ_COL[2], O_COL, KQ_COL[3], O_COL + UNIT]
KQ_UNIT = [0, 3, 4, 6]
V_UNIT_LAST = 2
O_UNIT = [5, 7]
RING = 4
FFN1_COL = [UNIT_COL[f // 2] + f % 2 * (UNIT // 2) for f in range(F // P)]
FFN2_COL = [UNIT_COL[UNITS // 2 + f // 2] + f % 2 * (UNIT // 2) for f in range(F // P)]
ROUND_L0, ROUND_FFN0, ROUND_L1A, ROUND_L1B, ROUND_FFN1, ROUNDS = 0, 1, 2, 6, 10, 11

_COLS = {}
_n = 0
for _name, _w in [("q0", NGROUP), ("k0", NGROUP), ("v0", NGROUP), ("ln0a_w", DC), ("ln0a_b", DC),
                  ("ln0b_w", DC), ("ln0b_b", DC), ("ln1a_w", DC), ("ln1a_b", DC), ("ln1b_w", DC),
                  ("ln1b_b", DC), ("ln1c_w", DC), ("ln1c_b", DC), ("fc0", F // P), ("fc1", F // P),
                  ("q1a", H), ("k1a", H), ("bk1a", H), ("bv1a", H),
                  ("q1b", H), ("k1b", H), ("bk1b", H), ("bv1b", H)]:
    _COLS[_name] = (_n, _w)
    _n += _w
NCOLS = _n


def xattn_kernel(nc, x_d, ctxt_d, mask_d, ident_d, weights_d, cols_d, rows_d, vrows_d, out_d):
    f32, f32r, bf16, u8 = mybir.dt.float32, mybir.dt.float32r, mybir.dt.bfloat16, mybir.dt.uint8
    ALU, ACT, AX = mybir.AluOpType, mybir.ActivationFunctionType, mybir.AxisListType
    ds = bass.ds

    with ExitStack() as ctx:
        def sem(name):
            return ctx.enter_context(nc.semaphore(name))

        def pb(name, shape):
            return ctx.enter_context(nc.psum_tensor(name, shape, f32))

        def sb(name, shape, dt=f32):
            return ctx.enter_context(nc.sbuf_tensor(name, shape, dt))

        x_sb = sb("x_sb", [P, NT, D])
        ht_hi, ht_lo = sb("ht_hi", [P, DC, NTOK], f32r), sb("ht_lo", [P, DC, NTOK], f32r)
        ct_hi, ct_lo = sb("ct_hi", [P, DC, NTOK], f32r), sb("ct_lo", [P, DC, NTOK], f32r)
        w_hi, w_lo = sb("w_hi", [P, WCOLS], f32r), sb("w_lo", [P, WCOLS], f32r)
        w_raw = sb("w_raw", [P, RING, UNIT])
        cols = sb("cols", [P, NCOLS])
        rows = sb("rows", [P, 5, D])
        ident = sb("ident", [P, P])
        xn = sb("xn", [P, NT, D])
        tmp = sb("tmp", [P, 2, HALF])
        vrow = sb("vrow", [P, 2, H * HD1 // 2])
        probs = sb("probs", [P, LIVE, QC, KEYS1_EVEN])
        nmax, sums, rden = sb("nmax", [P, LIVE, QC]), sb("sums", [P, LIVE, QC]), sb("rden", [P, LIVE, QC])
        stats = sb("stats", [P, NT, 6])
        mv = sb("mv", [P, NT, 2])
        half_pow, rstd, vare = sb("half_pow", [P, NT]), sb("rstd", [P, NT]), sb("vare", [P, NT])

        base = nc.sbuf_base
        base = (base + 63) // 64 * 64
        KB = 1024

        def at(name, off, shape, dt=f32):
            return nc.alloc_sbuf_tensor_at(name, shape, dt, offset=base + off)

        kt_hi = at("kt_hi", 0, [P, 2, B, KEYS1_EVEN], f32r)
        kt_lo = at("kt_lo", 9 * KB, [P, 2, B, KEYS1_EVEN], f32r)
        v_hi, v_lo = at("v_hi", 18 * KB, [P, NT, UNIT], f32r), at("v_lo", 34 * KB, [P, NT, UNIT], f32r)
        qt_hi, qt_lo = at("qt_hi", 50 * KB, [P, 2, NTOK], f32r), at("qt_lo", 58 * KB, [P, 2, NTOK], f32r)
        cx_hi, cx_lo = at("cx_hi", 66 * KB, [P, 2, NTOK], f32r), at("cx_lo", 74 * KB, [P, 2, NTOK], f32r)
        pt_hi, pt_lo = at("pt_hi", 82 * KB, [P, 2, QC * S], f32r), at("pt_lo", 86 * KB, [P, 2, QC * S], f32r)
        v0_all = at("v0_all", 0, [P, NT, UNIT], f32r)
        v0_now = at("v0_now", 16 * KB, [P, NT, GROUP, P], f32r)
        q0_hi, q0_lo = at("q0_hi", 32 * KB, [P, NTOK], f32r), at("q0_lo", 36 * KB, [P, NTOK], f32r)
        k0_hi, k0_lo = at("k0_hi", 40 * KB, [P, NTOK], f32r), at("k0_lo", 44 * KB, [P, NTOK], f32r)
        c0_hi, c0_lo = at("c0_hi", 60 * KB, [P, NTOK], f32r), at("c0_lo", 64 * KB, [P, NTOK], f32r)
        kq_hi, kq_lo = at("kq_hi", 68 * KB, [P, UNIT], f32r), at("kq_lo", 70 * KB, [P, UNIT], f32r)
        p0_hi, p0_lo = at("p0_hi", 50 * KB, [P, 4, QC * S], f32r), at("p0_lo", 72 * KB, [P, 4, QC * S], f32r)
        vtmp = at("vtmp", 82 * KB, [P, H * HD1])
        mask_raw = at("mask_raw", 48 * KB, [1, NTOK], u8)
        mask_slot = at("mask_slot", 49 * KB, [1, P], bf16)
        mask_row = at("mask_row", 58 * KB, [1, NTOK], bf16)
        g_hi, g_lo = at("g_hi", 50 * KB, [P, F // P, HALF], f32r), at("g_lo", 66 * KB, [P, F // P, HALF], f32r)
        ct_raw = at("ct_raw", 50 * KB, [P, DC, NTOK])

        ps_proj = pb("ps_proj", [P, 2, 512])
        ps_score = pb("ps_score", [P, 2, QC, 512])
        ps_trans = pb("ps_trans", [P, 512])
        ps_ctx = pb("ps_ctx", [P, 512])

        def score_banks(n, width):
            if width == S:
                return ps_score[:, n % 2, 0, :].rearrange("p (c k) -> p c k", c=QC)
            return ps_score[:, n % 2, :, 0:width]

        def trans0(n):
            return ps_score[:, n % 2, 1, :]

        def ctx0(b):
            return (ps_ctx, ps_trans)[b % 2]

        def xn_piece(half, c):
            return xn[:, 4 * half + 2 * c:4 * half + 2 * c + 2, :].rearrange("p t d -> p (t d)")

        def ps_norm(c):
            return ps_score[:, 0, c, :]

        def col(name, k=0):
            n, w = _COLS[name]
            return cols[:, n + k:n + k + 1]

        def col_at(name, k):
            return cols[:, ds(k + _COLS[name][0], 1)]

        x_loaded, ct_loaded, cols_loaded = sem("x_loaded"), sem("ct_loaded"), sem("cols_loaded")
        rows_loaded, ident_loaded, mask_loaded = sem("rows_loaded"), sem("ident_loaded"), sem("mask_loaded")
        vrow_loaded, vrow_ready, out_stored = sem("vrow_loaded"), sem("vrow_ready"), sem("out_stored")
        raw_loaded = [sem(f"raw_loaded{r}") for r in range(RING)]
        w_hi_ready, w_lo_ready = sem("w_hi_ready"), sem("w_lo_ready")
        consts_ready, cols_scaled, mask_ready = sem("consts_ready"), sem("cols_scaled"), sem("mask_ready")
        waited, slots_cleared = sem("waited"), sem("slots_cleared")
        ct_hi_ready, ct_lo_ready = sem("ct_hi_ready"), sem("ct_lo_ready")

        class NormSems:
            def __init__(self, stage):
                def own(name):
                    return sem(f"ln{stage}_{name}")

                self.stats, self.pool, self.rstd = own("stats"), own("pool"), own("rstd")
                self.norm, self.turned, self.h32 = own("norm"), own("turned"), own("h32")
                self.hi, self.lo, self.biased = own("hi"), own("lo"), own("biased")

        class AttentionSems:
            def __init__(self, stage):
                def own(name):
                    return sem(f"att{stage}_{name}")

                self.proj, self.kq_hi, self.kq_lo = own("proj"), own("kq_hi"), own("kq_lo")
                self.v32, self.v_hi, self.v_lo = own("v32"), own("v_hi"), own("v_lo")
                self.v_lo_odd, self.v_now, self.w_now = own("v_lo_odd"), own("v_now"), own("w_now")
                self.learned, self.score, self.nmax = own("learned"), own("score"), own("nmax")
                self.exp, self.rden, self.prob = own("exp"), own("rden"), own("prob")
                self.turned, self.pt_hi, self.pt_lo = own("turned"), own("pt_hi"), own("pt_lo")
                self.pv, self.cx_hi, self.cx_lo = own("pv"), own("cx_hi"), own("cx_lo")
                self.acc = own("acc")

        class MlpSems:
            def __init__(self, stage):
                def own(name):
                    return sem(f"ffn{stage}_{name}")

                self.fc1, self.gelu, self.hi = own("fc1"), own("gelu"), own("hi")
                self.lo, self.fc2, self.acc = own("lo"), own("fc2"), own("acc")

        LN = {s: NormSems(s) for s in range(5)}
        ATT = {s: AttentionSems(s) for s in ("0", "1a", "1b")}
        SEED = LIVE
        FFN = {s: MlpSems(s) for s in (0, 1)}

        ITEMS, OUTS, NKQ, LEAD, LEAD0 = GROUP * B, 2 * B, 4 * GROUP, 3, 4
        KQ_TILES = [(w, j, h) for j in range(GROUP + 1)
                    for w, h in ((("k", 0), ("k", 1), ("q", 0), ("q", 1)) if j % GROUP == 0 else
                                 (("k", 0), ("q", 0), ("k", 1), ("q", 1)))]
        OUT_AT = {7: [0], 8: [1], 10: [2], 11: [3], 14: [4], 15: [5], 16: [6, 7]}
        KQ_AT = {n: 5 + n for n in range(ITEMS - GROUP - 1)}
        KQ_AT.update({ITEMS - GROUP + k: NKQ + k for k in range(LEAD)})
        KQ_DONE = {tile: k + 1 for k, tile in enumerate(KQ_TILES)}

        def plan(last):
            values = [("v", t, 0) for t in range(NT)]
            tiles = KQ_TILES[:LEAD] + values[:2] + KQ_TILES[LEAD:4] + values[2:] + KQ_TILES[4:5]
            ahead, by_item = range(LEAD, len(tiles)), {}
            for n in range(ITEMS + 1):
                more = [KQ_TILES[KQ_AT[n]]] if n in KQ_AT and not (last and n >= ITEMS - GROUP) else []
                more += [("o", o, 0) for o in OUT_AT.get(n, ())]
                by_item[n] = range(len(tiles), len(tiles) + len(more))
                tiles += more
            return tiles, ahead, by_item, {tile: k + 1 for k, tile in enumerate(tiles)}

        PLAN = {last: plan(last) for last in (False, True)}
        NTILE = len(PLAN[False][0]) - LEAD
        SPLIT_AT = {0: [1], 1: [2], 3: [3], 7: [4], 12: [5], 13: [6], 16: [7]}
        UNIT_READ = [("q", 0, 1), ("v", NT - 1, 0), ("v", NT - 1, 0), ("q", 1, 1), ("q", 2, 1), ("o", B - 1, 0),
                     ("q", 3, 1), ("o", OUTS - 1, 0)]

        KQ0_TILES = [(w, k, h) for k in range(2) for h in range(2) for w in "kq"]
        KQ0_AT = {6: 4, 8: 5}
        W0_AT = 2
        SPLIT0_AT = {1 + 3 * u: u for u in range(UNITS // 2)}
        SPLIT_MLP_AT = {0: UNITS // 2, 1: UNITS // 2 + 1, 3: UNITS // 2 + 2, 5: UNITS // 2 + 3}
        NORM0_AT = {2: 0, 3: 1}
        NORM_MLP_AT = {2: 0, 4: 1}

        def plan0(last):
            tiles, before, behind = KQ0_TILES[:LEAD0], {}, {}
            for n in range(ITEMS + 2):
                ahead = [KQ0_TILES[KQ0_AT[n]]] if n in KQ0_AT else []
                ahead += [KQ0_TILES[6]] if n == ITEMS else []
                after = [KQ0_TILES[7]] if n == ITEMS else []
                if last:
                    ahead, after = [], []
                if n > GROUP and n % GROUP == 1:
                    after += [("o", n // GROUP - 1, 0)]
                before[n] = range(len(tiles), len(tiles) + len(ahead))
                tiles = tiles + ahead
                behind[n] = range(len(tiles), len(tiles) + len(after))
                tiles = tiles + after
            return tiles, before, behind, {tile: k + 1 for k, tile in enumerate(tiles)}

        PLAN0 = {last: plan0(last) for last in (False, True)}
        NTILE0 = len(PLAN0[False][0]) - LEAD0

        def rounds(engine, g0, body):
            with engine.Fori(g0, g0 + NGROUP - 1) as g:
                body(g, g - g0, False)
            body(g0 + NGROUP - 1, NGROUP - 1, True)

        def alone(engine):
            engine.sem_inc(waited, 1)

        block = ctx.enter_context(nc.Block())

        @block.sync
        def _(sp):
            sp.dma_start(x_sb[:, :, :], x_d).then_inc(x_loaded, 16)
            sp.dma_start(ident[:, :], ident_d).then_inc(ident_loaded, 16)
            sp.dma_start(cols[:, :], cols_d).then_inc(cols_loaded, 16)
            sp.dma_start(mask_raw[:, :], mask_d).then_inc(mask_loaded, 16)
            sp.dma_start(ct_raw[:, :, :], ctxt_d).then_inc(ct_loaded, 16)

            for u in range(RING):
                sp.dma_start(w_raw[:, u, :], weights_d[0, :, u * UNIT:(u + 1) * UNIT]).then_inc(raw_loaded[u], 16)
            sp.dma_start(rows[:, :, :], rows_d.partition_broadcast(P)).then_inc(rows_loaded, 16)
            for A in ATT.values():
                for started in (A.proj, A.kq_hi, A.kq_lo, A.v32, A.v_hi, A.v_lo, A.v_lo_odd, A.v_now, A.w_now,
                                A.learned, A.score, A.nmax, A.exp, A.rden, A.prob, A.turned, A.pt_hi, A.pt_lo, A.pv,
                                A.cx_hi, A.cx_lo, A.acc):
                    sp.sem_inc(started, SEED)
            for u in range(RING, UNITS):
                sp.wait_ge(w_lo_ready, u - RING + 1)
                sp.dma_start(w_raw[:, u - RING, :],
                             weights_d[0, :, u * UNIT:(u + 1) * UNIT]).then_inc(raw_loaded[u - RING], 16)
            with sp.Fori(1, ROUNDS) as g:
                for u in range(UNITS):
                    sp.wait_ge(w_lo_ready, g * UNITS + (u - RING + 1))
                    sp.dma_start(w_raw[:, u % RING, :],
                                 weights_d[ds(g, 1), :, u * UNIT:(u + 1) * UNIT]
                                 .rearrange("a p c -> (a p) c")).then_inc(raw_loaded[u % RING], 16)
            for t in range(2):
                sp.wait_ge(FFN[1].acc, 2 * (t + 1))
                sp.dma_start(out_d[:, 4 * t:4 * t + 4, :], x_sb[:, 4 * t:4 * t + 4, :]).then_inc(out_stored, 16)
            sp.wait_ge(out_stored, 32)

        @block.gpsimd
        def _(pool):
            def split_lo(g, u):
                c = UNIT_COL[u]
                pool.wait_ge(w_hi_ready, g * UNITS + u + 1)
                nc.gpsimd.tensor_tensor(w_lo[:, c:c + UNIT], w_raw[:, u % RING, :],
                                        w_hi[:, c:c + UNIT].bitcast(f32), ALU.subtract).then_inc(w_lo_ready, 1)

            def deviations(s, half):
                L = LN[s]
                t0 = 4 * half
                pool.wait_ge(L.stats, 8 * (half + 1))
                nc.gpsimd.tensor_scalar(vare[:, t0:t0 + 4], mv[:, t0:t0 + 4, 1], EPS, 1.0,
                                        ALU.add, ALU.mult).then_inc(L.pool, 1)
                pool.wait_ge(L.pool, half + 1)
                nc.gpsimd.tensor_tensor(rstd[:, t0:t0 + 4], vare[:, t0:t0 + 4], half_pow[:, t0:t0 + 4],
                                        ALU.pow).then_inc(L.rstd, 1)

            def output_bias(s, tiles):
                L = LN[s]
                pool.wait_ge(rows_loaded, 16)
                for t in tiles:
                    pool.wait_ge(L.norm, t + 1)
                    nc.gpsimd.tensor_tensor(x_sb[:, t, :], x_sb[:, t, :], rows[:, s, :],
                                            ALU.add).then_inc(L.biased, 1)

            def normalise(A, n, first, width):
                pool.wait_ge(A.rden, first + n + 1 + SEED)
                alone(pool)
                for c in range(QC):
                    e = probs[:, n % LIVE, c, 0:width]
                    last = nc.gpsimd.tensor_scalar(e, e, rden[:, n % LIVE, c:c + 1], 1.0, ALU.mult, ALU.mult)
                last.then_inc(A.prob, 1)

            def value_row(s, k, learned):
                w = H * HD1 // 2
                pool.wait_ge(vrow_loaded, 32 * (s + 1))
                nc.gpsimd.tensor_tensor(vrow[:, k, :], vrow[:, k, :], learned[:, k * w:(k + 1) * w],
                                        ALU.subtract).then_inc(vrow_ready, 1)

            def attention1(A, name, g0, norm):
                def learned_key(it, j):
                    par = j % 2
                    bk = cols[:, ds(it * GROUP + (_COLS["bk" + name][0] + j), 1)].to_broadcast([P, B])
                    pool.wait_ge(A.score, it * ITEMS + max(0, 4 * (j - 1)) + SEED)
                    alone(pool)
                    nc.gpsimd.tensor_copy(kt_hi[:, par, :, S], bk).then_inc(A.learned, 1)
                    pool.wait_ge(A.learned, it * 2 * GROUP + 2 * j + 1 + SEED)
                    alone(pool)
                    nc.gpsimd.tensor_tensor(kt_lo[:, par, :, S], bk, kt_hi[:, par, :, S].bitcast(f32),
                                            ALU.subtract).then_inc(A.learned, 1)

                def v_lo_tile(it, t):
                    pool.wait_ge(A.v_hi, it * NT + t + 1 + SEED)
                    nc.gpsimd.tensor_tensor(v_lo[:, t, :], tmp[:, 0, :], v_hi[:, t, :].bitcast(f32),
                                            ALU.subtract).then_inc(A.v_lo, 1)

                def body(g, it, last):
                    for t in range(0, NT, 2):
                        if t == NT - 2:
                            normalise(A, 0, it * ITEMS, S)
                        v_lo_tile(it, t)
                    normalise(A, 1, it * ITEMS, S)
                    split_lo(g + 1, 0)
                    for n in range(ITEMS + (1 if last else 2)):
                        j, b = divmod(n, B)
                        if 0 < n < ITEMS - 1:
                            normalise(A, n + 1, it * ITEMS, S)
                        for u in SPLIT_AT.get(n - 1, ()):
                            split_lo(g + 1, u)
                        if b == 0 and j < (GROUP - 1 if last else GROUP):
                            learned_key(it, j + 1)
                        if last and name == "1a" and n in (5, 9):
                            value_row(1, (5, 9).index(n), xn[:, :, :].rearrange("p t d -> p (t d)"))
                        if last and n == ITEMS - 1:
                            deviations(norm, 0)

                learned_key(0, 0)
                rounds(pool, g0, body)

            nc.gpsimd.memset(half_pow[:, :], -0.5).then_inc(consts_ready, 1)
            nc.gpsimd.memset(v0_now[:, :, :, :].bitcast(f32), 0.0).then_inc(slots_cleared, 1)
            pool.wait_ge(consts_ready, 1)
            deviations(0, 0)
            deviations(0, 1)
            for u in range(UNITS):
                split_lo(ROUND_L0, u)
            output_bias(0, range(NT))
            for k in range(2):
                value_row(0, k, vtmp)

            def group(g, i, last):
                for n in range(ITEMS):
                    normalise(ATT["0"], n, i * ITEMS, S)
                    if last and n == 11:
                        deviations(1, 0)
                    if last and n - 3 in SPLIT0_AT:
                        split_lo(ROUND_FFN0, SPLIT0_AT[n - 3])

            rounds(pool, 0, group)
            output_bias(1, range(2))
            deviations(1, 1)
            output_bias(1, range(2, NT))
            for u in range(UNITS // 2, UNITS):
                split_lo(ROUND_FFN0, u)
            deviations(2, 0)
            output_bias(2, range(4))
            for u in range(UNITS // 2):
                split_lo(ROUND_L1A, u)
            deviations(2, 1)
            for u in range(UNITS // 2, UNITS):
                split_lo(ROUND_L1A, u)
            output_bias(2, range(4, NT))
            attention1(ATT["1a"], "1a", ROUND_L1A, 3)
            output_bias(3, range(2))
            deviations(3, 1)
            split_lo(ROUND_L1B, UNITS - 1)
            output_bias(3, range(2, NT))
            attention1(ATT["1b"], "1b", ROUND_L1B, 4)
            output_bias(4, range(2))
            deviations(4, 1)
            split_lo(ROUND_FFN1, UNITS - 1)
            output_bias(4, range(2, NT))


        @block.scalar
        def _(act):
            def split_hi(g, u):
                c = UNIT_COL[u]
                act.wait_ge(raw_loaded[u % RING], g * (16 * UNITS // RING) + 16 * (u // RING + 1))
                nc.scalar.activation(w_hi[:, c:c + UNIT], w_raw[:, u % RING, :], ACT.Copy).then_inc(w_hi_ready, 1)

            def layer_norm(s, half, pieces=range(DC)):
                L = LN[s]
                name = ("ln0a", "ln0b", "ln1a", "ln1b", "ln1c")[s]
                act.wait_ge(cols_scaled, 5)
                for c in pieces:
                    e = DC * half + c
                    act.wait_ge(L.turned, DC * (half + 1))
                    nc.scalar.activation(xn_piece(half, c), ps_norm(c), ACT.Identity,
                                         scale=col(name + "_w", c), bias=col(name + "_b", c)).then_inc(L.h32, 1)
                    act.wait_ge(L.h32, e + 1)
                    nc.scalar.activation(ht_hi[:, c, half * HALF:(half + 1) * HALF], xn_piece(half, c),
                                         ACT.Copy).then_inc(L.hi, 1)

            def exps(A, n, first, width):
                act.wait_ge(A.nmax, first + n + 1 + SEED)
                act.wait_ge(A.turned, first + (n - LIVE + 1) + SEED)
                for c in range(QC):
                    last = nc.scalar.activation(probs[:, n % LIVE, c, 0:width], score_banks(n, width)[:, c, :], ACT.Exp,
                                                bias=nmax[:, n % LIVE, c:c + 1],
                                                accum_out=sums[:, n % LIVE, c:c + 1])
                last.then_inc(A.exp, 1)

            def load_value_rows(s, learned):
                act.dma_start(vrow[:, :, :].rearrange("p k w -> p (k w)"),
                              vrows_d[2 * s, :].partition_broadcast(P)).then_inc(vrow_loaded, 16)
                act.dma_start(learned, vrows_d[2 * s + 1, :].partition_broadcast(P)).then_inc(vrow_loaded, 16)

            for u in range(V_UNIT_LAST + 1):
                split_hi(0, u)
            act.wait_ge(ct_loaded, 16)
            for c in range(DC):
                nc.scalar.activation(ct_hi[:, c, :], ct_raw[:, c, :], ACT.Copy).then_inc(ct_hi_ready, 1)
            load_value_rows(0, vtmp[:, :])
            layer_norm(0, 0)

            A = ATT["0"]
            for t in range(NT):
                act.wait_ge(A.proj, t + 1 + SEED)
                nc.scalar.activation(v0_all[:, t, :].rearrange("p (h e) -> p h e", h=H)[:, :, 0:HD0],
                                     ps_proj[:, t % 2, :].rearrange("p (h e) -> p h e", h=H)[:, :, 0:HD0],
                                     ACT.Copy).then_inc(A.v_hi, 1)
                if t + V_UNIT_LAST + 1 < UNITS:
                    split_hi(0, t + V_UNIT_LAST + 1)
                if t in NORM0_AT:
                    layer_norm(0, 1, [NORM0_AT[t]])
            act.wait_ge(cols_scaled, 5)
            act.wait_ge(w_hi_ready, UNITS)
            nc.scalar.activation(kq_hi[:, :], w_hi[:, 0:UNIT], ACT.Copy).then_inc(A.w_now, 1)

            def kq0_tile(i, t, tile):
                w, k, half = tile
                dst = k0_hi if w == "k" else q0_hi
                if k:
                    act.wait_ge(A.score, i * ITEMS + (half + 1) * ITEMS // 2 + SEED)
                act.wait_ge(A.proj, i * NTILE0 + (NT + t + 1) + SEED)
                alone(act)
                nc.scalar.activation(dst[:, half * HALF:(half + 1) * HALF], ps_proj[:, t % 2, :], ACT.Identity,
                                     bias=col_at(w + "0", i + k)).then_inc(A.kq_hi, 1)

            def group(g, i, last):
                first = i * ITEMS
                tiles, before, behind, _ = PLAN0[last]
                for n in range(ITEMS + 1):
                    b, j = divmod(n, GROUP)
                    if n < ITEMS and n + 2 < (ITEMS if last else 2 * ITEMS):
                        exps(A, n + 2, first, S)
                    if n < ITEMS:
                        act.wait_ge(A.pv, first + (n - 3) + SEED)
                        act.wait_ge(A.turned, first + n + 1 + SEED)
                        nc.scalar.activation(p0_hi[:, n % 4, :], trans0(n), ACT.Copy).then_inc(A.pt_hi, 1)
                    for t in before[n]:
                        kq0_tile(i, t, tiles[t])
                    if j == 0 and b > 0:
                        act.wait_ge(A.proj, i * NTILE0 + (NT + PLAN0[False][3][("o", b - 1, 0)] - NTILE0) + SEED)
                        act.wait_ge(A.pv, first + n + SEED)
                        alone(act)
                        nc.scalar.activation(c0_hi[:, (b - 1) * S:b * S], ctx0(b - 1)[:, 0:S], ACT.Identity,
                                             bias=col_at("v0", i)).then_inc(A.cx_hi, 1)
                    if last and n == ITEMS:
                        layer_norm(1, 0)
                    for t in behind[n]:
                        if tiles[t][0] != "o":
                            kq0_tile(i, t, tiles[t])
                    if n == W0_AT and not last:
                        act.wait_ge(A.proj, i * NTILE0 + (NT + LEAD0) + SEED)
                        alone(act)
                        nc.scalar.activation(kq_hi[:, :], w_hi[:, ds(i * UNIT + UNIT, UNIT)], ACT.Copy)\
                            .then_inc(A.w_now, 1)
                    if last and n in SPLIT0_AT:
                        act.wait_ge(A.w_now, 2 * NGROUP + SEED)
                        act.wait_ge(A.proj, NT + LEAD0 + (NGROUP - 1) * NTILE0 + SEED)
                        split_hi(ROUND_FFN0, SPLIT0_AT[n])

            kq0_tile(0, 0, KQ0_TILES[0])
            kq0_tile(0, 1, KQ0_TILES[1])
            kq0_tile(0, 2, KQ0_TILES[2])
            exps(A, 0, 0, S)
            kq0_tile(0, 3, KQ0_TILES[3])
            exps(A, 1, 0, S)
            rounds(act, 0, group)
            def ffn(s, func, name, next_round):
                N = FFN[s]
                norm = 1 if s == 0 else 4
                for half in range(2):
                    for f in range(F // P):
                        k = half * (F // P) + f
                        act.wait_ge(N.fc1, k + 1)
                        if k >= 2:
                            act.wait_ge(N.lo, k - 1)
                        nc.scalar.activation(tmp[:, k % 2, :], ps_proj[:, k % 2, :], func,
                                             bias=col(name, f)).then_inc(N.gelu, 1)
                        if k in NORM_MLP_AT:
                            layer_norm(norm, 1, [NORM_MLP_AT[k]])
                        if s == 0 and k in SPLIT_MLP_AT:
                            act.wait_ge(ATT["0"].proj, NT + NGROUP * NTILE0 + SEED)
                            split_hi(ROUND_FFN0, SPLIT_MLP_AT[k])
                if next_round is not None:
                    layer_norm(2, 0)
                    act.wait_ge(N.fc1, 2 * F // P)
                    for u in range(UNITS):
                        if u == UNITS // 2:
                            act.wait_ge(N.fc2, 4)
                        split_hi(next_round, u)

            ffn(0, ACT.Gelu_apprx_tanh, "fc0", ROUND_L1A)

            def attention1(A, name, g0, norm):
                def kq_tile(it, t, tile):
                    w, j, half = tile
                    act.wait_ge(A.score, it * ITEMS + max(0, 4 * (j - 1)) + SEED)
                    act.wait_ge(A.proj, it * NTILE + (t + 1) + SEED)
                    alone(act)
                    bias = cols[:, ds(it * GROUP + (_COLS[w + name][0] + j), 1)]
                    if w == "k":
                        out = kt_hi[:, j % 2, 2 * half:2 * half + 2, 0:S]
                        src = ps_proj[:, t % 2, :].rearrange("p (b k) -> p b k", b=2)
                    else:
                        out = qt_hi[:, j % 2, half * HALF:(half + 1) * HALF]
                        src = ps_proj[:, t % 2, :]
                    nc.scalar.activation(out, src, ACT.Identity, bias=bias).then_inc(A.kq_hi, 1)

                def body(g, it, last):
                    first = it * ITEMS
                    tiles, ahead, by_item, done = PLAN[last]

                    def context(m):
                        j, b = divmod(m, B)
                        if j < 2:
                            act.wait_ge(A.proj, it * NTILE + LEAD + SEED)
                        else:
                            act.wait_ge(A.proj, it * NTILE + done[("o", b, 0)] + SEED)
                        act.wait_ge(A.pv, first + m + 1 + SEED)
                        alone(act)
                        nc.scalar.activation(cx_hi[:, j % 2, b * S:(b + 1) * S], ps_ctx[:, 0:S], ACT.Identity,
                                             bias=cols[:, ds(it * GROUP + (_COLS["bv" + name][0] + j), 1)])\
                            .then_inc(A.cx_hi, 1)

                    for t in ahead:
                        w, k, _ = tiles[t]
                        if w == "v":
                            act.wait_ge(A.v32, it * NT + k + 1 + SEED)
                            nc.scalar.activation(v_hi[:, k, :], tmp[:, k % 2, :], ACT.Copy).then_inc(A.v_hi, 1)
                            if k in (2, 5):
                                exps(A, k // 4, first, KEYS1)
                            if k == 3:
                                act.wait_ge(A.proj, it * NTILE + done[UNIT_READ[0]] + SEED)
                                split_hi(g + 1, 0)
                        else:
                            kq_tile(it, t, tiles[t])
                    for n in range(ITEMS + 1):
                        if 0 < n < ITEMS - 1:
                            exps(A, n + 1, first, KEYS1)
                        if n < ITEMS:
                            act.wait_ge(A.pv, first + max(0, n - 1) + SEED)
                            act.wait_ge(A.turned, first + n + 1 + SEED)
                            nc.scalar.activation(pt_hi[:, n % 2, :], ps_trans[:, :], ACT.Copy).then_inc(A.pt_hi, 1)
                        for t in by_item[n]:
                            if tiles[t][0] != "o":
                                kq_tile(it, t, tiles[t])
                        if n > 0:
                            context(n - 1)
                        if last and n == ITEMS:
                            layer_norm(norm + 1, 0)
                        if last and name == "1a" and n == 0:
                            act.wait_ge(A.v32, NGROUP * NT + SEED)
                            load_value_rows(1, xn[:, :, :].rearrange("p t d -> p (t d)"))
                        for u in SPLIT_AT.get(n, ()):
                            act.wait_ge(A.proj, it * NTILE + done[UNIT_READ[u]] + SEED)
                            split_hi(g + 1, u)

                for half in range(2):
                    if half:
                        layer_norm(norm, 1)
                    for t in range(2 * half, min(LEAD, 2 * half + 2)):
                        kq_tile(0, t, KQ_TILES[t])
                rounds(act, g0, body)

            attention1(ATT["1a"], "1a", ROUND_L1A, 2)
            attention1(ATT["1b"], "1b", ROUND_L1B, 3)
            ffn(1, ACT.Gelu, "fc1", None)

        @block.vector
        def _(dve):
            def split_context():
                for c in range(DC):
                    dve.wait_ge(ct_hi_ready, c + 1)
                    nc.vector.tensor_tensor(ct_lo[:, c, :], ct_raw[:, c, :], ct_hi[:, c, :].bitcast(f32),
                                            ALU.subtract).then_inc(ct_lo_ready, 1)

            def statistics(s, pair):
                L = LN[s]
                for t in (2 * pair, 2 * pair + 1):
                    nc.vector.bn_stats(stats[:, t, :], x_sb[:, t, :]).then_inc(L.stats, 1)
                for t in (2 * pair, 2 * pair + 1):
                    dve.wait_ge(L.stats, 4 * pair + t % 2 + 1)
                    nc.vector.bn_aggr(mv[:, t, :], stats[:, t, :]).then_inc(L.stats, 1)

            def normalised(s, half):
                L = LN[s]
                if s > 0:
                    dve.wait_ge(LN[s - 1].lo, 4)
                if s == 3:
                    dve.wait_ge(vrow_ready, 4)
                dve.wait_ge(L.stats, 8 * (half + 1))
                dve.wait_ge(L.rstd, half + 1)
                for t in range(4 * half, 4 * half + 4):
                    nc.vector.tensor_scalar(xn[:, t, :], x_sb[:, t, :], mv[:, t, 0:1], rstd[:, t:t + 1],
                                            ALU.subtract, ALU.mult).then_inc(L.norm, 1)

            def norm_lo(s, half, pieces=range(DC)):
                L = LN[s]
                for c in pieces:
                    tok = slice(half * HALF, (half + 1) * HALF)
                    dve.wait_ge(L.hi, DC * half + c + 1)
                    nc.vector.tensor_tensor(ht_lo[:, c, tok], xn_piece(half, c), ht_hi[:, c, tok].bitcast(f32),
                                            ALU.subtract).then_inc(L.lo, 1)

            def negmax(A, n, first, width):
                dve.wait_ge(A.score, first + n + 1 + SEED)
                nc.vector.tensor_reduce(nmax[:, n % LIVE, :], score_banks(n, width), AX.X, ALU.max,
                                        negate=True)\
                    .then_inc(A.nmax, 1)

            def reciprocals(A, n, first):
                dve.wait_ge(A.exp, first + n + 1 + SEED)
                nc.vector.reciprocal(rden[:, n % LIVE, :], sums[:, n % LIVE, :]).then_inc(A.rden, 1)

            def accumulate(A, bank, t):
                nc.vector.tensor_tensor(x_sb[:, t:t + 2, :], x_sb[:, t:t + 2, :],
                                        ps_proj[:, bank, :].rearrange("p (t d) -> p t d", t=2), ALU.add)\
                    .then_inc(A.acc, 1)

            nc.vector.memset(mask_slot[:, :], 0.0).then_inc(consts_ready, 1)
            dve.wait_ge(consts_ready, 2)
            nc.vector.memset(mask_slot[:, :].rearrange("p (j w) -> p j w", w=SLOT)[:, :, HD0:HD0 + 1], 1.0)\
                .then_inc(consts_ready, 1)
            dve.wait_ge(mask_loaded, 16)
            nc.vector.tensor_scalar(mask_row[:, :], mask_raw[:, :], 1.0, -MASKED, ALU.subtract, ALU.mult)\
                .then_inc(mask_ready, 1)
            dve.wait_ge(cols_loaded, 16)
            s0, s1 = 1.0 / math.sqrt(HD0), 1.0 / math.sqrt(HD1)
            for names, f in ((("q0",), s0), (("ln0a_w", "ln0a_b"), s0),
                             (("ln1a_w", "ln1a_b", "ln1b_w", "ln1b_b"), s1), (("q1a",), s1), (("q1b",), s1)):
                lo = _COLS[names[0]][0]
                hi = sum(_COLS[names[-1]])
                last = nc.vector.tensor_scalar(cols[:, lo:hi], cols[:, lo:hi], f, None, ALU.mult)
                last.then_inc(cols_scaled, 1)
            dve.wait_ge(x_loaded, 16)
            for pair in range(4):
                statistics(0, pair)
            for half in range(2):
                normalised(0, half)
            split_context()
            norm_lo(0, 0)

            A = ATT["0"]
            for t in range(NT):
                dve.wait_ge(A.v_hi, t + 1 + SEED)
                slots = v0_all[:, t, :].rearrange("p (h e) -> p h e", h=H)
                nc.vector.tensor_tensor(slots[:, :, HD0:SLOT],
                                        ps_proj[:, t % 2, :].rearrange("p (h e) -> p h e", h=H)[:, :, HD0:SLOT],
                                        slots[:, :, 0:HD0].bitcast(f32), ALU.subtract).then_inc(A.v_lo, 1)
                if t in NORM0_AT:
                    norm_lo(0, 1, [NORM0_AT[t]])
            dve.wait_ge(A.v_lo, NT + SEED)
            dve.wait_ge(slots_cleared, 1)
            dve.wait_ge(w_lo_ready, UNITS)
            nc.vector.tensor_copy(kq_lo[:, :], w_lo[:, 0:UNIT].bitcast(f32)).then_inc(A.w_now, 1)
            def kq0_tile(i, t, tile):
                w, k, half = tile
                hi, lo = (k0_hi, k0_lo) if w == "k" else (q0_hi, q0_lo)
                dve.wait_ge(A.kq_hi, i * LEAD0 + (KQ0_TILES.index(tile) + 1) + SEED)
                tok = slice(half * HALF, (half + 1) * HALF)
                nc.vector.scalar_tensor_tensor(out=lo[:, tok], in0=ps_proj[:, t % 2, :],
                                               scalar=col_at(w + "0", i + k), in1=hi[:, tok].bitcast(f32),
                                               op0=ALU.add, op1=ALU.subtract).then_inc(A.kq_lo, 1)

            def values_now(i, j):
                nc.vector.tensor_copy(v0_now[:, :, j, j * SLOT:(j + 1) * SLOT],
                                      v0_all[:, :, ds(i * P + j * SLOT, SLOT)].bitcast(f32)).then_inc(A.v_now, 1)

            def group(g, i, last):
                first = i * ITEMS
                tiles, before, behind, _ = PLAN0[last]
                for n in range(ITEMS + 2):
                    b, j = divmod(n, GROUP)
                    if n < ITEMS and n + 2 < (ITEMS if last else 2 * ITEMS):
                        reciprocals(A, n + 2, first)
                    if n < ITEMS and n + 3 < (ITEMS if last else 2 * ITEMS):
                        negmax(A, n + 3, first, S)
                    if n < ITEMS:
                        dve.wait_ge(A.pt_hi, first + n + 1 + SEED)
                        nc.vector.tensor_tensor(p0_lo[:, n % 4, :], trans0(n), p0_hi[:, n % 4, :].bitcast(f32),
                                                ALU.subtract).then_inc(A.pt_lo, 1)
                    for t in before[n]:
                        kq0_tile(i, t, tiles[t])
                    if j == 0 and b > 0:
                        if last and n == ITEMS:
                            normalised(1, 0)
                        tok = slice((b - 1) * S, b * S)
                        dve.wait_ge(A.cx_hi, i * B + b + SEED)
                        nc.vector.scalar_tensor_tensor(out=c0_lo[:, tok], in0=ctx0(b - 1)[:, 0:S],
                                                       scalar=col_at("v0", i), in1=c0_hi[:, tok].bitcast(f32),
                                                       op0=ALU.add, op1=ALU.subtract).then_inc(A.cx_lo, 1)
                    if last and n == ITEMS:
                        statistics(1, B - 2)
                    if n == W0_AT and not last:
                        dve.wait_ge(A.proj, i * NTILE0 + (NT + LEAD0) + SEED)
                        nc.vector.tensor_copy(kq_lo[:, :], w_lo[:, ds(i * UNIT + UNIT, UNIT)].bitcast(f32))\
                            .then_inc(A.w_now, 1)
                    k = n - (ITEMS - GROUP + 2)
                    if k >= 0 and not last:
                        dve.wait_ge(A.pv, first + (ITEMS - GROUP + k + 1) + SEED)
                        values_now(i + 1, k)
                    for t in behind[n]:
                        if tiles[t][0] != "o":
                            kq0_tile(i, t, tiles[t])
                        else:
                            dve.wait_ge(LN[0].biased, NT)
                            dve.wait_ge(A.acc, i * B + SEED)
                            dve.wait_ge(A.proj, i * NTILE0 + (NT + t + 1) + SEED)
                            accumulate(A, t % 2, 2 * tiles[t][1])
                            if last:
                                dve.wait_ge(A.acc, (NGROUP - 1) * B + (tiles[t][1] + 1) + SEED)
                                if tiles[t][1] != B - 2:
                                    statistics(1, tiles[t][1])

            for j in range(GROUP):
                values_now(0, j)
            kq0_tile(0, 0, KQ0_TILES[0])
            kq0_tile(0, 1, KQ0_TILES[1])
            kq0_tile(0, 2, KQ0_TILES[2])
            negmax(A, 0, 0, S)
            negmax(A, 1, 0, S)
            kq0_tile(0, 3, KQ0_TILES[3])
            reciprocals(A, 0, 0)
            negmax(A, 2, 0, S)
            reciprocals(A, 1, 0)
            rounds(dve, 0, group)

            def ffn(s):
                N = FFN[s]
                nf = F // P
                norm = 1 if s == 0 else 4
                norm_lo(norm, 0)
                normalised(norm, 1)
                for half in range(2):
                    for f in range(nf):
                        k = half * nf + f
                        if k - 1 in NORM_MLP_AT:
                            norm_lo(norm, 1, [NORM_MLP_AT[k - 1]])
                        if s == 0 and half and f == 4:
                            normalised(2, 0)
                        if half:
                            dve.wait_ge(N.fc2, 2)
                        dve.wait_ge(N.gelu, k + 1)
                        nc.vector.tensor_copy(g_hi[:, f, :], tmp[:, k % 2, :]).then_inc(N.hi, 1)
                        dve.wait_ge(N.hi, k + 1)
                        nc.vector.tensor_tensor(g_lo[:, f, :], tmp[:, k % 2, :], g_hi[:, f, :].bitcast(f32),
                                                ALU.subtract).then_inc(N.lo, 1)
                    for r in range(2):
                        k, t = 2 * half + r, 4 * half + 2 * r
                        dve.wait_ge(LN[norm].biased, t + 2)
                        dve.wait_ge(N.fc2, k + 1)
                        nc.vector.tensor_tensor(x_sb[:, t:t + 2, :], x_sb[:, t:t + 2, :],
                                                ps_score[:, half, r, :].rearrange("p (t d) -> p t d", t=2), ALU.add)\
                            .then_inc(N.acc, 1)
                        if s == 0:
                            dve.wait_ge(N.acc, k + 1)
                            statistics(2, k)

            for part in (kt_hi, kt_lo):
                nc.vector.memset(part[:, :, :, KEYS1:KEYS1_EVEN].bitcast(f32), 0.0).then_inc(consts_ready, 1)
            ffn(0)

            def attention1(A, name, g0, s):
                norm = 2 + s
                vr = vrow[:, :, :].rearrange("p k w -> p (k w)")

                def kq_tile(it, t, tile):
                    w, j, half = tile
                    dve.wait_ge(A.kq_hi, it * NKQ + KQ_DONE[tile] + SEED)
                    bias = cols[:, ds(it * GROUP + (_COLS[w + name][0] + j), 1)]
                    if w == "k":
                        out = kt_lo[:, j % 2, 2 * half:2 * half + 2, 0:S]
                        hi = kt_hi[:, j % 2, 2 * half:2 * half + 2, 0:S]
                        src = ps_proj[:, t % 2, :].rearrange("p (b k) -> p b k", b=2)
                    else:
                        out = qt_lo[:, j % 2, half * HALF:(half + 1) * HALF]
                        hi = qt_hi[:, j % 2, half * HALF:(half + 1) * HALF]
                        src = ps_proj[:, t % 2, :]
                    nc.vector.scalar_tensor_tensor(out=out, in0=src, scalar=bias, in1=hi.bitcast(f32),
                                                   op0=ALU.add, op1=ALU.subtract).then_inc(A.kq_lo, 1)

                def body(g, it, last):
                    first = it * ITEMS
                    tiles, ahead, by_item, _ = PLAN[last]

                    def context(m):
                        j, b = divmod(m, B)
                        dve.wait_ge(A.cx_hi, first + m + 1 + SEED)
                        nc.vector.scalar_tensor_tensor(out=cx_lo[:, j % 2, b * S:(b + 1) * S], in0=ps_ctx[:, 0:S],
                                                       scalar=cols[:, ds(it * GROUP + (_COLS["bv" + name][0] + j), 1)],
                                                       in1=cx_hi[:, j % 2, b * S:(b + 1) * S].bitcast(f32),
                                                       op0=ALU.add, op1=ALU.subtract).then_inc(A.cx_lo, 1)

                    def odd_values_lo(k):
                        dve.wait_ge(A.v_hi, it * NT + k + 1 + SEED)
                        nc.vector.tensor_tensor(v_lo[:, k, :], tmp[:, 1, :], v_hi[:, k, :].bitcast(f32),
                                                ALU.subtract).then_inc(A.v_lo_odd, 1)

                    for t in ahead:
                        w, k, _ = tiles[t]
                        if w == "v":
                            if k % 2 == 0:
                                dve.wait_ge(A.v_lo, it * (NT // 2) + k // 2 + SEED)
                            else:
                                dve.wait_ge(A.v_lo_odd, it * (NT // 2) + k // 2 + SEED)
                            dve.wait_ge(A.proj, it * NTILE + (t + 1) + SEED)
                            nc.vector.tensor_tensor(tmp[:, k % 2, :], ps_proj[:, t % 2, :],
                                                    vr[:, ds(it * UNIT, UNIT)], ALU.add).then_inc(A.v32, 1)
                            if k == 1:
                                negmax(A, 0, first, KEYS1)
                            if k == 3:
                                reciprocals(A, 0, first)
                                negmax(A, 1, first, KEYS1)
                            if k == 6:
                                reciprocals(A, 1, first)
                        else:
                            kq_tile(it, t, tiles[t])
                        if w == "v" and k % 2 == 0 and k > 0:
                            odd_values_lo(k - 1)
                    for n in range(ITEMS + 1):
                        if 0 < n < ITEMS - 1:
                            reciprocals(A, n + 1, first)
                        if 0 < n < ITEMS - 2:
                            negmax(A, n + 2, first, KEYS1)
                        if n < ITEMS:
                            dve.wait_ge(A.pt_hi, first + n + 1 + SEED)
                            nc.vector.tensor_tensor(pt_lo[:, n % 2, :], ps_trans[:, :],
                                                    pt_hi[:, n % 2, :].bitcast(f32), ALU.subtract).then_inc(A.pt_lo, 1)
                        if n == 0:
                            negmax(A, 2, first, KEYS1)
                            odd_values_lo(NT - 1)
                        for t in by_item[n]:
                            if tiles[t][0] != "o":
                                kq_tile(it, t, tiles[t])
                        if n > 0:
                            context(n - 1)
                        for t in by_item[n]:
                            if tiles[t][0] == "o":
                                o = tiles[t][1]
                                dve.wait_ge(A.acc, it * OUTS + o // B * B + SEED)
                                dve.wait_ge(A.proj, it * NTILE + (t + 1) + SEED)
                                accumulate(A, t % 2, 2 * (o % B))
                                if last and o >= B:
                                    dve.wait_ge(A.acc, (NGROUP - 1) * OUTS + (o + 1) + SEED)
                                    statistics(norm + 1, o - B)
                                if last and o == OUTS - 2:
                                    normalised(norm + 1, 0)

                norm_lo(norm, 0)
                normalised(norm, 1)
                for half in range(2):
                    if half:
                        norm_lo(norm, 1)
                    for t in range(2 * half, min(LEAD, 2 * half + 2)):
                        kq_tile(0, t, KQ_TILES[t])
                dve.wait_ge(vrow_ready, 2 * (s + 1))
                dve.wait_ge(LN[norm].biased, NT)
                rounds(dve, g0, body)

            attention1(ATT["1a"], "1a", ROUND_L1A, 0)
            attention1(ATT["1b"], "1b", ROUND_L1B, 1)
            ffn(1)

        @block.tensor
        def _(pe):
            def mm3(out, w, x, start, stop):
                (wh, wl), (xh, xl) = w, x
                pe.matmul(out, wl, xh, start=start, stop=False)
                pe.matmul(out, wh, xl, start=False, stop=False)
                return pe.matmul(out, wh, xh, start=False, stop=stop)

            def both(pair, *index):
                return pair[0][index], pair[1][index]

            W, HT, CT = (w_hi, w_lo), (ht_hi, ht_lo), (ct_hi, ct_lo)
            ALLP = slice(None)

            def layer_norm(s, half):
                L = LN[s]
                pe.wait_ge(L.norm, 4 * (half + 1))
                for c in range(DC):
                    if half:
                        pe.wait_ge(L.h32, c + 1)
                    for k in range(4):
                        last = pe.transpose(ps_norm(c)[:, k * P:(k + 1) * P],
                                            xn[:, 4 * half + k, c * P:(c + 1) * P], ident[:, :])
                    last.then_inc(L.turned, 1)

            def transposes(A, n, first, bank, read):
                pe.wait_ge(A.prob, first + n + 1 + SEED)
                pe.wait_ge(A.pt_lo, first + read + SEED)
                for kc in range(QC):
                    for c in range(QC):
                        last = pe.transpose(bank[:, kc * S + c * P:kc * S + (c + 1) * P],
                                            probs[:, n % LIVE, c, kc * P:(kc + 1) * P], ident[:, :])
                last.then_inc(A.turned, 1)

            pe.wait_ge(ident_loaded, 16)
            layer_norm(0, 0)

            A = ATT["0"]
            pe.wait_ge(ct_lo_ready, DC)
            pe.wait_ge(w_lo_ready, V_UNIT_LAST + 1)
            for t in range(NT):
                if t >= 2:
                    pe.wait_ge(A.v_lo, t - 1 + SEED)
                if t == 2:
                    layer_norm(0, 1)
                for c in range(DC):
                    last = mm3(ps_proj[:, t % 2, :], both(CT, ALLP, c, slice(t * P, (t + 1) * P)),
                               both(W, ALLP, slice(V_COL + c * UNIT, V_COL + (c + 1) * UNIT)),
                               c == 0, c == DC - 1)
                last.then_inc(A.proj, 1)
            pe.wait_ge(LN[0].lo, 4)
            pe.wait_ge(A.v_lo, NT + SEED)
            pe.wait_ge(w_lo_ready, UNITS)
            pe.wait_ge(mask_ready, 1)
            pe.wait_ge(consts_ready, 3)

            def kq0_tile(i, t, tile):
                w, k, half = tile
                pe.wait_ge(A.w_now, (i + k) * 2 + 2 + SEED)
                tok = slice(half * HALF, (half + 1) * HALF)
                for c in range(DC):
                    o = (0 if w == "k" else D) + c * P
                    last = mm3(ps_proj[:, t % 2, :], (kq_hi[:, o:o + P], kq_lo[:, o:o + P]),
                               both(CT if w == "k" else HT, ALLP, c, tok), c == 0, w == "q" and c == DC - 1)
                if w == "k":
                    last = pe.matmul(ps_proj[:, t % 2, :], mask_slot[:, :], mask_row[:, tok],
                                     start=False, stop=True)
                last.then_inc(A.proj, 1)

            def scores0(i, m):
                b, j = divmod(m % ITEMS, GROUP)
                rows_j = slice(j * SLOT, (j + 1) * SLOT)
                need = m // ITEMS * 4 + (2 if b < 2 else 4)
                pe.wait_ge(A.kq_lo, i * 4 + need + SEED)
                pe.wait_ge(A.exp, i * ITEMS + (m - 1) + SEED)
                for c in range(QC):
                    q = b * S + c * P
                    last = mm3(score_banks(m, S)[:, c, :], both((q0_hi, q0_lo), rows_j, slice(q, q + P)),
                               both((k0_hi, k0_lo), rows_j, slice(b * S, (b + 1) * S)), True, True)
                last.then_inc(A.score, 1)

            def group(g, i, last_group):
                first = i * ITEMS
                tiles, before, behind, _ = PLAN0[last_group]

                def tile(t):
                    w, k, half = tiles[t]
                    prev = tiles[t - 2]
                    if t < LEAD0 + 2:
                        pe.wait_ge(A.kq_lo, i * LEAD0 + LEAD0 + SEED)
                        pe.wait_ge(A.acc, i * B + SEED)
                    elif prev[0] == "o":
                        pe.wait_ge(A.acc, i * B + (prev[1] + 1) + SEED)
                    else:
                        pe.wait_ge(A.kq_lo, i * LEAD0 + (KQ0_TILES.index(prev) + 1) + SEED)
                    if w != "o":
                        kq0_tile(i, t, tiles[t])
                        return
                    pe.wait_ge(A.cx_lo, i * B + (k + 1) + SEED)
                    for q in range(QC):
                        r = QC * k + q
                        last = mm3(ps_proj[:, t % 2, q * D:(q + 1) * D],
                                   (c0_hi[:, r * P:(r + 1) * P], c0_lo[:, r * P:(r + 1) * P]),
                                   both(W, ALLP, ds(i * D + O_COL, D)), True, True)
                    last.then_inc(A.proj, 1)

                def context(m):
                    b, j = divmod(m, GROUP)
                    pe.wait_ge(A.pt_lo, first + m + 1 + SEED)
                    if b == 0:
                        pe.wait_ge(A.v_now, i * GROUP + (j + 1) + SEED)
                    if j == 0:
                        pe.wait_ge(A.cx_lo, i * B + (b - 1) + SEED)
                    for kc in range(QC):
                        for part in (p0_lo, p0_hi):
                            last = pe.matmul(ctx0(b)[:, 0:S], v0_now[:, QC * b + kc, j, :],
                                             part[:, m % 4, kc * S:(kc + 1) * S],
                                             start=(j, kc) == (0, 0) and part is p0_lo,
                                             stop=(j, kc) == (GROUP - 1, QC - 1) and part is p0_hi)
                    last.then_inc(A.pv, 1)

                for n in range(ITEMS + 2):
                    if n < ITEMS:
                        transposes(A, n, first, trans0(n), n - 1)
                    if n < ITEMS and n + 3 < (ITEMS if last_group else 2 * ITEMS):
                        scores0(i, n + 3)
                    for t in before[n]:
                        tile(t)
                    if 0 < n <= ITEMS:
                        context(n - 1)
                    if last_group and n == ITEMS:
                        layer_norm(1, 0)
                    for t in behind[n]:
                        tile(t)

            kq0_tile(0, 0, KQ0_TILES[0])
            kq0_tile(0, 1, KQ0_TILES[1])
            pe.wait_ge(A.kq_lo, 1 + SEED)
            kq0_tile(0, 2, KQ0_TILES[2])
            scores0(0, 0)
            scores0(0, 1)
            kq0_tile(0, 3, KQ0_TILES[3])
            scores0(0, 2)
            rounds(pe, 0, group)
            pe.wait_ge(A.kq_lo, NGROUP * 4 + SEED)


            def ffn(s, g, norm):
                N = FFN[s]
                nf = F // P
                for half in range(2):
                    tok = slice(half * HALF, (half + 1) * HALF)
                    for f in range(nf):
                        k = half * nf + f
                        if f == 0:
                            pe.wait_ge(LN[norm].lo, 2 * (half + 1))
                        if k >= 2:
                            pe.wait_ge(N.gelu, k - 1)
                        pe.wait_ge(w_lo_ready, g * UNITS + f // 2 + 1)
                        for c in range(DC):
                            o = FFN1_COL[f] + c * P
                            last = mm3(ps_proj[:, k % 2, :], both(W, ALLP, slice(o, o + P)),
                                       both(HT, ALLP, c, tok), c == 0, c == DC - 1)
                        last.then_inc(N.fc1, 1)
                        if k == 2:
                            layer_norm(norm, 1)
                    if s == 0 and half:
                        layer_norm(2, 0)
                    for r in range(2):
                        for q in range(2):
                            t = 2 * r + q
                            for f in range(nf):
                                if t == 0:
                                    pe.wait_ge(w_lo_ready, g * UNITS + (UNITS // 2 + f // 2 + 1))
                                    pe.wait_ge(N.lo, half * nf + f + 1)
                                o = FFN2_COL[f]
                                last = mm3(ps_score[:, half, r, q * D:(q + 1) * D],
                                           both((g_hi, g_lo), ALLP, f, slice(t * P, (t + 1) * P)),
                                           both(W, ALLP, slice(o, o + D)), f == 0, f == nf - 1)
                        last.then_inc(N.fc2, 1)

            ffn(0, ROUND_FFN0, 1)
            pe.wait_ge(FFN[0].gelu, 2 * F // P)

            def attention1(A, g0, norm):
                pe.wait_ge(consts_ready, 5)
                def kq_tile(g, it, t, tile):
                    w, j, half = tile
                    if w == "k" and half == 0:
                        pe.wait_ge(w_lo_ready, g * UNITS + (j // GROUP * UNITS + KQ_UNIT[j % GROUP] + 1))
                    if w == "q" and j == 0:
                        pe.wait_ge(LN[norm].lo, 2 * (half + 1))
                    tok = slice(half * HALF, (half + 1) * HALF)
                    for c in range(DC):
                        o = KQ_COL[j % GROUP] + (0 if w == "k" else D) + c * P
                        last = mm3(ps_proj[:, t % 2, :], both(W, ALLP, slice(o, o + P)),
                                   both(CT if w == "k" else HT, ALLP, c, tok), c == 0, c == DC - 1)
                    last.then_inc(A.proj, 1)

                def body(g, it, last_round):
                    first = it * ITEMS
                    tiles, ahead, by_item, _ = PLAN[last_round]

                    def tile(t):
                        w, j, half = tiles[t]
                        bank = ps_proj[:, t % 2, :]
                        before = tiles[t - 2]
                        if t < LEAD + 2:
                            pe.wait_ge(A.kq_lo, it * NKQ + (t - 1) + SEED)
                            pe.wait_ge(A.acc, it * OUTS + (t - LEAD - 1) + SEED)
                        elif before[0] == "v":
                            pe.wait_ge(A.v32, it * NT + (before[1] + 1) + SEED)
                        elif before[0] == "o":
                            pe.wait_ge(A.acc, it * OUTS + (before[1] + 1) + SEED)
                        else:
                            pe.wait_ge(A.kq_lo, it * NKQ + KQ_DONE[before] + SEED)
                        if w == "o":
                            pair, b = divmod(j, B)
                            pe.wait_ge(A.cx_lo, first + (2 * pair + 1) * B + b + 1 + SEED)
                            if b == 0:
                                pe.wait_ge(w_lo_ready, g * UNITS + (O_UNIT[pair] + 1))
                            for q in range(QC):
                                t0 = QC * b + q
                                for k in range(2):
                                    o_col = O_COL + (2 * pair + k) * D
                                    last = mm3(bank[:, q * D:(q + 1) * D],
                                               both((cx_hi, cx_lo), ALLP, k, slice(t0 * P, (t0 + 1) * P)),
                                               both(W, ALLP, slice(o_col, o_col + D)), k == 0, k == 1)
                            last.then_inc(A.proj, 1)
                        elif w == "v":
                            if j == 0:
                                pe.wait_ge(w_lo_ready, g * UNITS + (V_UNIT_LAST + 1))
                            for c in range(DC):
                                last = mm3(bank, both(CT, ALLP, c, slice(j * P, (j + 1) * P)),
                                           both(W, ALLP, slice(V_COL + c * UNIT, V_COL + (c + 1) * UNIT)),
                                           c == 0, c == DC - 1)
                            last.then_inc(A.proj, 1)
                        else:
                            kq_tile(g, it, t, tiles[t])

                    def scores(n):
                        j, b = divmod(n, B)
                        if n == 0:
                            pe.wait_ge(LN[norm].h32, 2 * DC)
                        pe.wait_ge(A.kq_lo, it * NKQ + KQ_DONE[("q", j, b // 2)] + SEED)
                        if b == 0:
                            pe.wait_ge(A.learned, it * 2 * GROUP + 2 * j + 2 + SEED)
                        pe.wait_ge(A.exp, first + (n - 1) + SEED)
                        for c in range(QC):
                            q = b * S + c * P
                            last = mm3(ps_score[:, n % 2, c, 0:KEYS1_EVEN],
                                       both((qt_hi, qt_lo), ALLP, j % 2, slice(q, q + P)),
                                       both((kt_hi, kt_lo), ALLP, j % 2, b, ALLP), True, True)
                        last.then_inc(A.score, 1)

                    def context(m):
                        j, b = divmod(m, B)
                        if j == 0:
                            pe.wait_ge(A.v_lo, it * (NT // 2) + b + 1 + SEED)
                            pe.wait_ge(A.v_lo_odd, it * (NT // 2) + b + 1 + SEED)
                        pe.wait_ge(A.pt_lo, first + m + 1 + SEED)
                        pe.wait_ge(A.cx_lo, first + m + SEED)
                        for kc in range(QC):
                            last = mm3(ps_ctx[:, 0:S],
                                       both((v_hi, v_lo), ALLP, QC * b + kc, slice(j * HD1, (j + 1) * HD1)),
                                       both((pt_hi, pt_lo), ALLP, m % 2, slice(kc * S, (kc + 1) * S)),
                                       kc == 0, kc == QC - 1)
                        last.then_inc(A.pv, 1)

                    for t in ahead:
                        if tiles[t] == ("q", 0, 1):
                            scores(0)
                        if tiles[t] == ("v", 3, 0):
                            scores(1)
                        tile(t)
                    for n in range(ITEMS + 1):
                        if n < ITEMS:
                            transposes(A, n, first, ps_trans, n)
                        if n + 2 < ITEMS:
                            scores(n + 2)
                        for t in by_item[n]:
                            if tiles[t][0] != "o":
                                tile(t)
                        if n > 0:
                            context(n - 1)
                        for t in by_item[n]:
                            if tiles[t][0] == "o":
                                tile(t)
                    if last_round:
                        layer_norm(norm + 1, 0)

                if norm > 2:
                    pe.wait_ge(ATT["1a"].acc, NGROUP * OUTS + SEED)
                for t in range(LEAD):
                    if t == 2:
                        layer_norm(norm, 1)
                    if t >= 2:
                        pe.wait_ge(A.kq_lo, (t - 1) + SEED)
                    kq_tile(g0, 0, t, KQ_TILES[t])
                rounds(pe, g0, body)

            attention1(ATT["1a"], ROUND_L1A, 2)
            attention1(ATT["1b"], ROUND_L1B, 3)
            pe.wait_ge(ATT["1b"].acc, NGROUP * OUTS + SEED)
            ffn(1, ROUND_FFN1, 4)


def _pack_attention(np, wq, wk, wv, wo):
    rounds = []
    for g in range(wq.shape[1] // UNIT):
        cut = slice(g * UNIT, (g + 1) * UNIT)
        k, q, v = (w[:, cut].reshape(DC, P, UNIT).transpose(1, 0, 2) for w in (wk, wq, wv))
        o = wo[cut].reshape(GROUP, P, D).transpose(1, 0, 2)
        kq = [np.concatenate([w[:, :, j * P:(j + 1) * P].reshape(P, DC * P) for w in (k, q)], axis=1)
              for j in range(GROUP)]
        out = [o[:, 2 * r:2 * r + 2].reshape(P, UNIT) for r in range(2)]
        rounds.append(np.concatenate([kq[0], v[:, 0], v[:, 1], kq[1], kq[2], out[0], kq[3], out[1]], axis=1))
    return rounds


def _pack_mlp(np, w1, w2):
    first = w1.reshape(DC, P, F // P, P).transpose(1, 2, 0, 3).reshape(P, -1)
    second = w2.reshape(F // P, P, D).transpose(1, 0, 2).reshape(P, -1)
    return [np.concatenate([first, second], axis=1)]


def _slots(np, w, axis, twice=False):
    shape = list(w.shape)
    shape[axis:axis + 1] = [H, HD0]
    padded = list(shape)
    padded[axis + 1] = SLOT
    out = np.zeros(padded, w.dtype)
    for k in range(2 if twice else 1):
        out[tuple([slice(None)] * (axis + 1) + [slice(k * HD0, (k + 1) * HD0)])] = w.reshape(shape)
    final = list(w.shape)
    final[axis] = H * SLOT
    return out.reshape(final)


def kernel(**inputs):
    import numpy as np
    import concourse.bacc as bacc
    from concourse.bass_utils import run_bass_kernel_spmd

    a = {k: np.asarray(v) for k, v in inputs.items()}
    l0 = {k[len("L0_xattn_"):]: v for k, v in a.items() if k.startswith("L0_xattn_")}
    l1 = {k[len("L1_xattn_"):]: v for k, v in a.items() if k.startswith("L1_xattn_")}

    rounds = _pack_attention(np, _slots(np, l0["q_w"], 1), _slots(np, l0["k_w"], 1),
                             _slots(np, l0["v_w"], 1, True), _slots(np, l0["cproj_w"], 0, True))
    rounds += _pack_mlp(np, l0["fc_w"], l0["proj_w"])
    for n in "12":
        rounds += _pack_attention(np, l1["wq" + n], l1["wk" + n], l1["wv" + n], l1["wo" + n])
    rounds += _pack_mlp(np, l1["w_fc1"], l1["w_fc2"])
    weights = np.stack(rounds)

    q0 = _slots(np, l0["q_b"], 0).reshape(NGROUP, GROUP, SLOT)
    q0[:, :, HD0] = math.sqrt(HD0)
    vectors = [q0, _slots(np, l0["k_b"], 0), _slots(np, l0["v_b"], 0), l0["ln1_w"], l0["ln1_b"],
               l0["ln2_w"], l0["ln2_b"], l1["ln1_scale"], l1["ln1_offset"], l1["ln2_scale"], l1["ln2_offset"],
               l1["ln_mlp_scale"], l1["ln_mlp_offset"], l0["fc_b"], l1["b_fc1"]]
    for n in "12":
        vectors += [l1["bq" + n], l1["bk" + n], l1["bias_k" + n], l1["bias_v" + n]]
    cols = np.concatenate([v.reshape(-1, P) for v in vectors]).T
    rows = np.stack([l0["cproj_b"], l0["proj_b"], l1["bo1"], l1["bo2"], l1["b_fc2"]])
    vrows = np.stack([v.reshape(-1) for n in "12" for v in (l1["bv" + n], l1["bias_v" + n])])

    arrays = {"x": a["x"].reshape(NTOK, D), "ctxt": a["ctx_2048"].reshape(NTOK, D).T,
              "mask": a["mask_BxS2_bf1"].reshape(1, NTOK).view(np.uint8), "ident": np.eye(P, dtype=np.float32),
              "weights": weights, "cols": cols, "rows": rows, "vrows": vrows}
    arrays = {"in_" + k: np.ascontiguousarray(v) for k, v in arrays.items()}
    nc = bacc.Bacc("TRN2", target_bir_lowering=False, num_devices=1)
    d = {k[3:]: nc.dram_tensor(k, v.shape, mybir.dt.from_np(v.dtype), kind="ExternalInput").ap()
         for k, v in arrays.items()}
    out = nc.dram_tensor("out", (NTOK, D), mybir.dt.float32, kind="ExternalOutput").ap()
    xattn_kernel(nc, d["x"].rearrange("(t p) d -> p t d", p=P), d["ctxt"].rearrange("(c p) t -> p c t", p=P),
                 d["mask"], d["ident"], d["weights"], d["cols"], d["rows"], d["vrows"],
                 out.rearrange("(t p) d -> p t d", p=P))
    r = run_bass_kernel_spmd(nc, [arrays], core_ids=[0])
    return r.results[0]["out"].reshape(B, S, D)
```
